# Optimizing a Trainium2 kernel written in Bass

```python
import numpy as np
import jax
import jax.numpy as jnp

def _softmax(x, axis=-1):
    return jax.nn.softmax(x, axis=axis)

def _gelu(x):
    return jax.nn.gelu(x, approximate=True)

def _silu(x):
    return jax.nn.silu(x)

def _sigmoid(x):
    return jax.nn.sigmoid(x)

def _layernorm(x, axis=-1, eps=1e-05):
    m = jnp.mean(x, axis=axis, keepdims=True)
    v = jnp.var(x, axis=axis, keepdims=True)
    return (x - m) / jnp.sqrt(v + eps)

def _scatter_add(tgt, idx, src, axis=0):
    return tgt.at[idx].add(src)

def _segment_sum(src, seg, n):
    return jax.ops.segment_sum(src, seg, n)
kernel_name = 'mk_flamingo_gated_d2_seqx_r4_0f6c3f'

def setup_inputs(seed: int=0):
    np.random.seed(seed)
    _w = jnp.asarray

    def _rec_inputs():
        import jax
        import jax.numpy as jnp
        _rk = jax.random.key(seed)
        x = 7.22e-05 + 1 * jax.random.normal(jax.random.fold_in(_rk, 1), (4, 1024, 256), jnp.float32)
        _lenS = 1024 - jax.random.randint(jax.random.fold_in(_rk, 7), (4,), 0, max(1, 1024 // 4) + 1, jnp.int32)
        _lenS2 = 77 - jax.random.randint(jax.random.fold_in(_rk, 8), (4,), 0, max(1, 77 // 4) + 1, jnp.int32)
        _ctx_1024P = jax.random.normal(jax.random.fold_in(_rk, 11), (4, 16, 256), jnp.float32)
        _ctx_1024c = jax.random.dirichlet(jax.random.fold_in(_rk, 511), 0.3 * jnp.ones((16,), jnp.float32), (4, 77))
        _ctx_1024t = jnp.einsum('bsk,bkd->bsd', _ctx_1024c, _ctx_1024P)
        _ctx_1024t = _ctx_1024t * jax.lax.rsqrt(jnp.mean(jnp.square(_ctx_1024t)) + 1e-12) * 0.953939
        ctx_1024 = 4.13588e-05 + 0.999923 * (_ctx_1024t + 0.3 * jax.random.normal(jax.random.fold_in(_rk, 611), (4, 77, 256), jnp.float32))
        _g = jax.random.normal(jax.random.fold_in(_rk, 9001), (2, 2), jnp.float32)
        _g = jnp.sign(_g) * jnp.maximum(jnp.abs(_g), 1.0) + (_g == 0) * 1.0
        g_xattn = _g[0]
        g_ffn = _g[1]
        return (x, ctx_1024, g_xattn, g_ffn)
    x, ctx_1024, g_xattn, g_ffn = _rec_inputs()

    def _L0_xattn_setup():
        import jax, jax.numpy as jnp
        import numpy as np
        DIM = 256
        NUM_HEADS = 16
        HEAD_DIM = DIM // NUM_HEADS
        SCALE = HEAD_DIM ** (-0.5)
        key = jax.random.key(seed)
        ks = jax.random.split(key, 11)
        B, N = (4, 512)
        init = 1.0 / np.sqrt(DIM)
        return {'q': jax.random.normal(ks[0], (B, N, DIM), jnp.float32), 'k': jax.random.normal(ks[1], (B, N, DIM), jnp.float32), 'v': jax.random.normal(ks[2], (B, N, DIM), jnp.float32), 'wq': jax.random.normal(ks[3], (DIM, DIM), jnp.float32) * init, 'bq': jax.random.normal(ks[4], (DIM,), jnp.float32) * init, 'wk': jax.random.normal(ks[5], (DIM, DIM), jnp.float32) * init, 'bk': jax.random.normal(ks[6], (DIM,), jnp.float32) * init, 'wv': jax.random.normal(ks[7], (DIM, DIM), jnp.float32) * init, 'bv': jax.random.normal(ks[8], (DIM,), jnp.float32) * init, 'wo': jax.random.normal(ks[9], (DIM, DIM), jnp.float32) * init, 'bo': jax.random.normal(ks[10], (DIM,), jnp.float32) * init}
    _L0_xattn_all = _L0_xattn_setup()
    _L0_xattn_in = {k: v for k, v in _L0_xattn_all.items() if k in ('wq', 'bq', 'wk', 'bk', 'wv', 'bv', 'wo', 'bo')}
    del _L0_xattn_all

    def _L0_ffn_setup():
        import jax, jax.numpy as jnp
        import numpy as np
        D_IN, D_HID = (256, 1024)

        def _ternary(key, shape):
            return jax.random.randint(key, shape, -1, 2).astype(jnp.float32)

        def _tlin(x, w, s):
            return jnp.einsum('bsi,oi->bso', x, w) * s
        key = jax.random.key(seed)
        ks = jax.random.split(key, 12)
        inv = lambda fan: 1.0 / np.sqrt(fan).astype(np.float32)
        return {'x': jax.random.normal(ks[0], (4, 512, D_IN), dtype=jnp.float32), 'w1_w': _ternary(ks[1], (D_HID, D_IN)), 'w1_s': jax.random.uniform(ks[2], (D_HID,), dtype=jnp.float32) * inv(D_IN), 'w2_w': _ternary(ks[3], (D_HID, D_IN)), 'w2_s': jax.random.uniform(ks[4], (D_HID,), dtype=jnp.float32) * inv(D_IN), 'h1_w': _ternary(ks[5], (D_HID, D_HID)), 'h1_s': jax.random.uniform(ks[6], (D_HID,), dtype=jnp.float32) * inv(D_HID), 'h2_w': _ternary(ks[7], (D_HID, D_HID)), 'h2_s': jax.random.uniform(ks[8], (D_HID,), dtype=jnp.float32) * inv(D_HID), 'w3_w': _ternary(ks[9], (D_IN, D_HID)), 'w3_s': jax.random.uniform(ks[10], (D_IN,), dtype=jnp.float32) * inv(D_HID)}
    _L0_ffn_all = _L0_ffn_setup()
    _L0_ffn_in = {k: v for k, v in _L0_ffn_all.items() if k in ('w1_w', 'w1_s', 'w2_w', 'w2_s', 'h1_w', 'h1_s', 'h2_w', 'h2_s', 'w3_w', 'w3_s')}
    del _L0_ffn_all

    def _L1_xattn_setup():
        import jax, jax.numpy as jnp
        import numpy as np
        DIM = 256
        DIM_VISUAL = 256
        DIM_HEAD = 64
        HEADS = 8
        INNER = DIM_HEAD * HEADS

        def _layer_norm(x, scale, bias, eps=1e-05):
            mu = jnp.mean(x, axis=-1, keepdims=True)
            var = jnp.mean(jnp.square(x - mu), axis=-1, keepdims=True)
            return (x - mu) * jax.lax.rsqrt(var + eps) * scale + bias
        key = jax.random.key(seed)
        ks = jax.random.split(key, 7)
        B, Ttxt, Timg = (4, 512, 512)
        x = jax.random.normal(ks[0], (B, Ttxt, DIM), dtype=jnp.float32)
        y = jax.random.normal(ks[1], (B, Timg, DIM_VISUAL), dtype=jnp.float32)
        ln_scale = jnp.ones((DIM,), dtype=jnp.float32)
        ln_bias = jnp.zeros((DIM,), dtype=jnp.float32)
        Wq = jax.random.normal(ks[2], (DIM, INNER), dtype=jnp.float32) / np.sqrt(DIM)
        Wkv = jax.random.normal(ks[3], (DIM_VISUAL, 2 * INNER), dtype=jnp.float32) / np.sqrt(DIM_VISUAL)
        Wo = jax.random.normal(ks[4], (INNER, DIM), dtype=jnp.float32) / np.sqrt(INNER)
        return {'x': x, 'y': y, 'ln_scale': ln_scale, 'ln_bias': ln_bias, 'Wq': Wq, 'Wkv': Wkv, 'Wo': Wo}
    _L1_xattn_all = _L1_xattn_setup()
    _L1_xattn_in = {k: v for k, v in _L1_xattn_all.items() if k in ('ln_scale', 'ln_bias', 'Wq', 'Wkv', 'Wo')}
    del _L1_xattn_all

    def _L1_ffn_setup():
        import jax, jax.numpy as jnp
        import numpy as np
        B, T, DIM, H, DH, TOPK = (4, 512, 256, 8, 64, 3)
        key = jax.random.key(seed)
        ks = jax.random.split(key, 6)
        x = jax.random.normal(ks[0], (B, T, DIM), dtype=jnp.float32)
        sc = 1.0 / np.sqrt(DIM)
        Wq = jax.random.normal(ks[1], (DIM, H * DH), dtype=jnp.float32) * sc
        Wkv = jax.random.normal(ks[2], (DIM, 2 * H * DH), dtype=jnp.float32) * sc
        Ws = jax.random.normal(ks[3], (DIM, H), dtype=jnp.float32) * sc
        Wo = jax.random.normal(ks[4], (H, DH, DIM), dtype=jnp.float32) * (1.0 / np.sqrt(DH))
        bo = jax.random.normal(ks[5], (H, DIM), dtype=jnp.float32) * 0.01
        return {'x': x, 'Wq': Wq, 'Wkv': Wkv, 'Ws': Ws, 'Wo': Wo, 'bo': bo}
    _L1_ffn_all = _L1_ffn_setup()
    _L1_ffn_in = {k: v for k, v in _L1_ffn_all.items() if k in ('Wq', 'Wkv', 'Ws', 'Wo', 'bo')}
    del _L1_ffn_all
    return {'x': x, 'ctx_1024': ctx_1024, 'g_xattn': g_xattn, 'g_ffn': g_ffn, 'L0_xattn_wq': _L0_xattn_in['wq'], 'L0_xattn_bq': _L0_xattn_in['bq'], 'L0_xattn_wk': _L0_xattn_in['wk'], 'L0_xattn_bk': _L0_xattn_in['bk'], 'L0_xattn_wv': _L0_xattn_in['wv'], 'L0_xattn_bv': _L0_xattn_in['bv'], 'L0_xattn_wo': _L0_xattn_in['wo'], 'L0_xattn_bo': _L0_xattn_in['bo'], 'L0_ffn_w1_w': _L0_ffn_in['w1_w'], 'L0_ffn_w1_s': _L0_ffn_in['w1_s'], 'L0_ffn_w2_w': _L0_ffn_in['w2_w'], 'L0_ffn_w2_s': _L0_ffn_in['w2_s'], 'L0_ffn_h1_w': _L0_ffn_in['h1_w'], 'L0_ffn_h1_s': _L0_ffn_in['h1_s'], 'L0_ffn_h2_w': _L0_ffn_in['h2_w'], 'L0_ffn_h2_s': _L0_ffn_in['h2_s'], 'L0_ffn_w3_w': _L0_ffn_in['w3_w'], 'L0_ffn_w3_s': _L0_ffn_in['w3_s'], 'L1_xattn_ln_scale': _L1_xattn_in['ln_scale'], 'L1_xattn_ln_bias': _L1_xattn_in['ln_bias'], 'L1_xattn_Wq': _L1_xattn_in['Wq'], 'L1_xattn_Wkv': _L1_xattn_in['Wkv'], 'L1_xattn_Wo': _L1_xattn_in['Wo'], 'L1_ffn_Wq': _L1_ffn_in['Wq'], 'L1_ffn_Wkv': _L1_ffn_in['Wkv'], 'L1_ffn_Ws': _L1_ffn_in['Ws'], 'L1_ffn_Wo': _L1_ffn_in['Wo'], 'L1_ffn_bo': _L1_ffn_in['bo']}

def reference(x, ctx_1024, g_xattn, g_ffn, L0_xattn_wq, L0_xattn_bq, L0_xattn_wk, L0_xattn_bk, L0_xattn_wv, L0_xattn_bv, L0_xattn_wo, L0_xattn_bo, L0_ffn_w1_w, L0_ffn_w1_s, L0_ffn_w2_w, L0_ffn_w2_s, L0_ffn_h1_w, L0_ffn_h1_s, L0_ffn_h2_w, L0_ffn_h2_s, L0_ffn_w3_w, L0_ffn_w3_s, L1_xattn_ln_scale, L1_xattn_ln_bias, L1_xattn_Wq, L1_xattn_Wkv, L1_xattn_Wo, L1_ffn_Wq, L1_ffn_Wkv, L1_ffn_Ws, L1_ffn_Wo, L1_ffn_bo):
    import jax
    import jax.numpy as jnp

    def _L0_xattn_ref(q, k, v, wq, bq, wk, bk, wv, bv, wo, bo):
        import jax, jax.numpy as jnp
        import numpy as np
        DIM = 256
        NUM_HEADS = 16
        HEAD_DIM = DIM // NUM_HEADS
        SCALE = HEAD_DIM ** (-0.5)
        B, Nq, C = q.shape
        Nk = k.shape[1]
        qh = (q @ wq.T + bq).reshape(B, Nq, NUM_HEADS, HEAD_DIM).transpose(0, 2, 1, 3)
        kh = (k @ wk.T + bk).reshape(B, Nk, NUM_HEADS, HEAD_DIM).transpose(0, 2, 1, 3)
        vh = (v @ wv.T + bv).reshape(B, Nk, NUM_HEADS, HEAD_DIM).transpose(0, 2, 1, 3)
        attn = jnp.einsum('bhqd,bhkd->bhqk', qh * SCALE, kh)
        attn = jax.nn.softmax(attn, axis=-1)
        out = jnp.einsum('bhqk,bhkd->bhqd', attn, vh)
        out = out.transpose(0, 2, 1, 3).reshape(B, Nq, C)
        return out @ wo.T + bo

    def _L0_ffn_ref(x, w1_w, w1_s, w2_w, w2_s, h1_w, h1_s, h2_w, h2_s, w3_w, w3_s):
        import jax, jax.numpy as jnp
        import numpy as np
        D_IN, D_HID = (256, 1024)

        def _ternary(key, shape):
            return jax.random.randint(key, shape, -1, 2).astype(jnp.float32)

        def _tlin(x, w, s):
            return jnp.einsum('bsi,oi->bso', x, w) * s
        h = jax.nn.silu(_tlin(x, w1_w, w1_s)) * _tlin(x, w2_w, w2_s)
        h = jax.nn.gelu(_tlin(h, h1_w, h1_s), approximate=False)
        h = jax.nn.gelu(_tlin(h, h2_w, h2_s), approximate=False)
        return _tlin(h, w3_w, w3_s)

    def _L1_xattn_ref(x, y, ln_scale, ln_bias, Wq, Wkv, Wo):
        import jax, jax.numpy as jnp
        import numpy as np
        DIM = 256
        DIM_VISUAL = 256
        DIM_HEAD = 64
        HEADS = 8
        INNER = DIM_HEAD * HEADS

        def _layer_norm(x, scale, bias, eps=1e-05):
            mu = jnp.mean(x, axis=-1, keepdims=True)
            var = jnp.mean(jnp.square(x - mu), axis=-1, keepdims=True)
            return (x - mu) * jax.lax.rsqrt(var + eps) * scale + bias
        B, Ttxt, _ = x.shape
        _, Timg, _ = y.shape
        h, d = (HEADS, DIM_HEAD)
        scale = d ** (-0.5)
        xn = _layer_norm(x, ln_scale, ln_bias)
        q = xn @ Wq
        kv = y @ Wkv
        k, v = jnp.split(kv, 2, axis=-1)
        q = q.reshape(B, Ttxt, h, d).transpose(0, 2, 1, 3) * scale
        k = k.reshape(B, Timg, h, d).transpose(0, 2, 1, 3)
        v = v.reshape(B, Timg, h, d).transpose(0, 2, 1, 3)
        sim = jnp.einsum('bhid,bhjd->bhij', q, k)
        sim = sim - jax.lax.stop_gradient(jnp.max(sim, axis=-1, keepdims=True))
        attn = jax.nn.softmax(sim, axis=-1)
        out = jnp.einsum('bhij,bhjd->bhid', attn, v)
        out = out.transpose(0, 2, 1, 3).reshape(B, Ttxt, h * d)
        return out @ Wo

    def _L1_ffn_ref(x, Wq, Wkv, Ws, Wo, bo):
        import jax, jax.numpy as jnp
        import numpy as np
        B, T, DIM, H, DH, TOPK = (4, 512, 256, 8, 64, 3)
        b, t, _ = x.shape
        s = jax.nn.sigmoid(x @ Ws)
        vals, idx = jax.lax.top_k(s, TOPK)
        bi = jnp.arange(b)[:, None, None]
        ti = jnp.arange(t)[None, :, None]
        scores = jnp.zeros_like(s).at[bi, ti, idx].set(vals)
        q = (x @ Wq).reshape(b, t, H, DH).transpose(0, 2, 1, 3)
        kv = (x @ Wkv).reshape(b, t, 2, H, DH).transpose(2, 0, 3, 1, 4)
        k, v = (kv[0], kv[1])
        scale = DH ** (-0.5)
        attn = jax.nn.softmax(jnp.einsum('bhid,bhjd->bhij', q * scale, k), axis=-1)
        out = jnp.einsum('bhij,bhjd->bhid', attn, v)
        proj = jnp.einsum('bhtd,hde->bhte', out, Wo) + bo[None, :, None, :]
        return jnp.einsum('bhte,bth->bte', proj, scores)
    x = x + jnp.tanh(g_xattn[0]) * _L0_xattn_ref(_layernorm(x, axis=-1), ctx_1024, ctx_1024, L0_xattn_wq, L0_xattn_bq, L0_xattn_wk, L0_xattn_bk, L0_xattn_wv, L0_xattn_bv, L0_xattn_wo, L0_xattn_bo)
    x = x + jnp.tanh(g_ffn[0]) * _L0_ffn_ref(_layernorm(x, axis=-1), L0_ffn_w1_w, L0_ffn_w1_s, L0_ffn_w2_w, L0_ffn_w2_s, L0_ffn_h1_w, L0_ffn_h1_s, L0_ffn_h2_w, L0_ffn_h2_s, L0_ffn_w3_w, L0_ffn_w3_s)
    x = x + jnp.tanh(g_xattn[1]) * _L1_xattn_ref(_layernorm(x, axis=-1), ctx_1024, L1_xattn_ln_scale, L1_xattn_ln_bias, L1_xattn_Wq, L1_xattn_Wkv, L1_xattn_Wo)
    x = x + jnp.tanh(g_ffn[1]) * _L1_ffn_ref(_layernorm(x, axis=-1), L1_ffn_Wq, L1_ffn_Wkv, L1_ffn_Ws, L1_ffn_Wo, L1_ffn_bo)
    return x

_drawn_inputs = setup_inputs


def setup_inputs(seed=0):
    import zlib

    import numpy as np

    out = dict(_drawn_inputs(seed))
    spreads = {'g_ffn': (-1.0, 0.2), 'L1_xattn_ln_scale': (1.0, 0.2), 'L1_xattn_ln_bias': (0.0, 0.1)}
    factors = {}
    for name, (base, spread) in spreads.items():
        noise = np.random.default_rng([zlib.crc32(name.encode()), seed]).standard_normal(out[name].shape)
        drawn = base * np.exp(spread * noise) if base else spread * noise
        out[name] = jnp.asarray(drawn.astype(out[name].dtype))
    for name, factor in factors.items():
        out[name] = (out[name] * factor).astype(out[name].dtype)
    return out
```

```python
from contextlib import ExitStack, contextmanager

import concourse.bass as bass
from concourse import mybir

F32 = mybir.dt.float32
F32R = mybir.dt.float32r
I32 = mybir.dt.int32
ALU = mybir.AluOpType
ACT = mybir.ActivationFunctionType
AX = mybir.AxisListType

P = 128
D = 256
DC = D // P
TOK = 128
PAIR = 2 * TOK
EPS = 1e-5
RSQRT_MAGIC = 0x5F3759DF


@contextmanager
def semaphores(nc, tag):
    made = []

    def sem(name):
        made.append(nc.alloc_semaphore(name=f"{tag}_{name}"))
        return made[-1]

    yield sem
    nc.clear_and_free_semaphores(made)
    nc.all_engine_barrier()


class Own:

    def __init__(self, eng, sem):
        self.eng, self.sem, self.n = eng, sem, 0

    def link(self, ins):
        ins.then_inc(self.sem, 1)
        self.n += 1

    def wait(self):
        self.eng.wait_ge(self.sem, self.n)

    def step(self, ins):
        self.link(ins)
        self.wait()

    def clear(self):
        if self.n:
            self.wait()
            self.eng.sem_clear(self.sem)
            self.n = 0


def spread(ap, dim, n):
    shape = list(ap.shape)
    shape[dim] = n
    return ap.broadcast_to(shape)


def split_passes(hi_lo_a, hi_lo_b):
    (ah, al), (bh, bl) = hi_lo_a, hi_lo_b
    return ((ah, bh), (ah, bl), (al, bh))


def rsqrt_guess(own, eng, var, v_eps, half, y):
    own.step(eng.tensor_scalar(v_eps, var, EPS, None, ALU.add))
    own.link(eng.tensor_scalar(half, v_eps, -0.5, None, ALU.mult))
    own.step(eng.tensor_scalar(y.bitcast(I32), v_eps.bitcast(I32), 1, None, ALU.logical_shift_right))


def newton(own, eng, half, y, t):
    for _ in range(3):
        own.step(eng.tensor_tensor(t, y, y, ALU.mult))
        own.step(eng.tensor_tensor(t, t, half, ALU.mult))
        own.step(eng.tensor_scalar(t, t, 1.5, None, ALU.add))
        own.step(eng.tensor_tensor(y, y, t, ALU.mult))


def cross_attention(nc, ident, gate, x_src, x_dst, ctxT, wqT, wkT, wvT, woT, bias, ln2, H, tag):
    B, _, S = ctxT.shape
    HD = wqT.shape[1]
    dh = HD // H
    C = HD // P
    HC = H // C
    G = H // 4
    SCALE = float(dh) ** -0.5
    NP = x_src.shape[0] // PAIR
    PB = NP // B
    TB = 2 * PB
    RING = 4
    QW = C * PAIR
    xs = x_src.rearrange("(n t p) d -> n p t d", t=2, p=P)
    xd = x_dst.rearrange("(n t p) d -> n p t d", t=2, p=P)
    assert PB == RING and 4 * S <= 512

    with semaphores(nc, tag) as sem, ExitStack() as ctx:
        def sb(name, shape, dt=F32):
            return ctx.enter_context(nc.sbuf_tensor(f"{tag}_{name}", shape, dt))

        wq_raw = sb("wq_raw", [P, DC, HD])
        wq = [sb("wq_hi", [P, DC, HD], F32R), sb("wq_lo", [P, DC, HD], F32R)]
        wo_raw = sb("wo_raw", [P, C, D])
        wo = [sb("wo_hi", [P, C, D], F32R), sb("wo_lo", [P, C, D], F32R)]
        wk = sb("wk", [P, DC, HD])
        wv = sb("wv", [P, DC, HD])
        cx = sb("cx", [P, DC, S])
        one = sb("one", [P, 1])
        head_mask = sb("head_mask", [P, HC])
        qbias = sb("qbias", [P, C])
        kbias = sb("kbias", [P, C])
        vbias = sb("vbias", [S, HD])
        obias = sb("obias", [P, D])
        ln_sb = sb("ln_sb", [P, 2, DC])
        kt = sb("kt", [P, C, S])
        kt_part = [sb("kt_hi", [P, C, S], F32R), sb("kt_lo", [P, C, S], F32R)]
        kblk = [sb("kblk_hi", [P, C, HC, S], F32R), sb("kblk_lo", [P, C, HC, S], F32R)]
        vt = sb("vt", [S, HD])
        vpad = [sb("vpad_hi", [S, H * P + P], F32R), sb("vpad_lo", [S, H * P + P], F32R)]
        x = sb("x", [P, RING, 2, D])
        stats = sb("stats", [P, 2, 6])
        mv = sb("mv", [P, 2, 2, 2])
        rs = sb("rs", [P, 2, 4, 2])
        xn = sb("xn", [P, 2, 2, D])
        xt = sb("xt", [P, DC, PAIR])
        xt_part = [sb("xt_hi", [P, DC, PAIR], F32R), sb("xt_lo", [P, DC, PAIR], F32R)]
        qt = sb("qt", [P, C, PAIR])
        q_part = [sb("q_hi", [P, 2, C, PAIR], F32R), sb("q_lo", [P, 2, C, PAIR], F32R)]
        prob = sb("prob", [P, 2, H, S])
        negmax = sb("negmax", [P, H])
        rsum = sb("rsum", [P, 2, 2, H])
        rwide = sb("rwide", [P, 2, HD])
        pt = [sb("pt_hi", [S, 2, H, PAIR], F32R), sb("pt_lo", [S, 2, H, PAIR], F32R)]
        ot = sb("ot", [P, C, PAIR])
        rt = sb("rt", [P, C, PAIR])
        o_part = [sb("o_hi", [P, C, PAIR], F32R), sb("o_lo", [P, C, PAIR], F32R)]
        y = sb("y", [P, 2, D])

        ps_s = ctx.enter_context(nc.psum_tensor(f"{tag}_ps_s", [P, G, 512], F32))
        ps_t = ctx.enter_context(nc.psum_tensor(f"{tag}_ps_t", [P, 2, 512], F32))
        ps_o = ctx.enter_context(nc.psum_tensor(f"{tag}_ps_o", [P, C, PAIR], F32))
        ps_m = ctx.enter_context(nc.psum_tensor(f"{tag}_ps_m", [P, 512 * max(1, C // 2)], F32))

        def diag(v):
            step = P + dh
            return [v[:, c * HC * P:c * HC * P + HC * step].rearrange("s (j w) -> s j w", w=step)[:, :, 0:dh]
                    for c in range(C)]

        s_w = [sem(f"w{i}") for i in range(6)]
        s_small = sem("small")
        s_ctx = sem("ctx")
        x_in = [sem(f"x_in{i}") for i in range(RING)]
        x_out = [sem(f"x_out{i}") for i in range(RING)]
        s_const, s_zeros = sem("head_mask_made"), sem("vpad_zeroed")
        w_hi, w_lo, s_qb = sem("w_hi"), sem("w_lo"), sem("qb")
        stat1, stat2, ln1, ln_done = sem("stat1"), sem("stat2"), sem("ln1"), sem("ln_done")
        e_xt, e_q, e_s, e_t, e_pv, e_rt, e_o, e_k, e_v = (sem(n) for n in (
            "pe_xt", "pe_q", "pe_s", "pe_t", "pe_pv", "pe_rt", "pe_o", "pe_k", "pe_v"))
        xt_raw, xt_hi, xt_lo = sem("xt_raw"), sem("s_xt_hi"), sem("s_xt_lo")
        qt_raw, q_hi, q_lo = sem("qt_raw"), sem("s_q_hi"), sem("s_q_lo")
        kt_raw, kt_hi, kt_lo, kb_hi, kb_lo = (sem(n) for n in ("s_kt", "s_kt_hi", "s_kt_lo", "s_kb_hi", "s_kb_lo"))
        vt_raw, v_hi, v_lo = sem("s_vt"), sem("s_v_hi"), sem("s_v_lo")
        d_sub, a_exp, d_r = sem("sub"), sem("exp"), sem("r")
        t_hi, t_lo = sem("t_hi"), sem("t_lo")
        r_wide, rt_copied = sem("r_wide"), sem("rt_copied")
        o_raw, o_hi, o_lo, d_fin = sem("o_raw"), sem("s_o_hi"), sem("s_o_lo"), sem("fin")
        own_v, own_a, own_p = sem("own_v"), sem("own_a"), sem("own_p")

        def batches(eng, body, own=None):
            body(0, True)
            if own:
                own.clear()
            with eng.Fori(1, B) as b:
                body(b, False)
                if own:
                    own.clear()

        block = ctx.enter_context(nc.Block())

        @block.sync
        def _(sp):
            def load_x(n, at):
                sp.dma_start(x[:, at % RING, :, :], xs[n]).then_inc(x_in[at % RING], 16)

            def load_ctx(b):
                sp.dma_start(cx[:, :, :], ctxT[b].rearrange("(c p) s -> p c s", p=P)).then_inc(s_ctx, 16)

            load_x(0, 0)
            load_ctx(0)
            for i, (dst, src) in enumerate(((wk, wkT), (wv, wvT), (wq_raw, wqT), (wo_raw, woT))):
                sp.dma_start(dst[:, :, :], src.rearrange("(c p) n -> p c n", p=P)).then_inc(s_w[i], 16)
            small = []
            if bias:
                bq, bk, bv, bo = bias
                small += [(qbias[:, :], bq),
                          (kbias[:, :], bk),
                          (vbias[:, :], spread(bv.rearrange("(a n) -> a n", a=1), 0, S)),
                          (obias[:, :], spread(bo.rearrange("(a n) -> a n", a=1), 0, P))]
            if ln2:
                small += [(ln_sb[:, i, :], v) for i, v in enumerate(ln2)]
            for dst, src in small:
                sp.dma_start(dst, src).then_inc(s_small, 16)
            for n in range(1, RING - 1):
                load_x(n, n)

            def body(b, first):
                for p in range(PB):
                    n = PB * b + p
                    if p == 0:
                        sp.wait_ge(e_v, b + 1)
                        if first or B > 1:
                            load_ctx_next(b, first)
                    if not (first and p == 0):
                        sp.wait_ge(d_fin, n)
                        sp.dma_start(xd[n - 1], x[:, (p - 1) % RING, :, :]).then_inc(x_out[(p - 1) % RING], 16)
                        sp.wait_ge(x_out[(p - 1) % RING], 16 * (b + (1 if p else 0)))
                    load_next(n, p)

            def load_ctx_next(b, first):
                sp.dma_start(cx[:, :, :], ctxT[b + 1].rearrange("(c p) s -> p c s", p=P)).then_inc(s_ctx, 16)

            def load_next(n, p):
                load_x(n + RING - 1, p - 1)

            body(0, True)
            with sp.Fori(1, B - 1) as b:
                body(b, False)

            def load_ctx_next(b, first):
                load_ctx(0)

            def load_next(n, p):
                load_x(n + RING - 1 if p == 0 else p - 1, p - 1)

            body(B - 1, False)
            sp.wait_ge(d_fin, NP)
            sp.dma_start(xd[NP - 1], x[:, RING - 1, :, :]).then_inc(x_out[RING - 1], 16)
            for i in range(RING):
                sp.wait_ge(x_out[i], 16 * B)

        @block.tensor
        def _(pe):
            def k_proj(b, t):
                pe.wait_ge(s_ctx, 16 * b + 16)
                for c in range(C):
                    for k in range(DC):
                        mm = pe.matmul(ps_m[:, c * S:(c + 1) * S], wk[:, k, c * P:(c + 1) * P], cx[:, k, :],
                                       start=k == 0, stop=k == DC - 1)
                mm.then_inc(e_k, 1)

            def v_proj():
                for k in range(DC):
                    mm = pe.matmul(ps_m[0:S, 0:HD], cx[:, k, :], wv[:, k, :], start=k == 0, stop=k == DC - 1)
                mm.then_inc(e_v, 1)

            def x_transpose(n, par):
                pe.wait_ge(ln_done, n + 1)
                for c in range(DC):
                    for t in range(2):
                        at = c * PAIR + t * TOK
                        mm = pe.transpose(ps_m[:, at:at + TOK], xn[:, par, t, c * P:(c + 1) * P], ident[:, :])
                mm.then_inc(e_xt, 1)

            def q_proj(n):
                pe.wait_ge(xt_hi, n + 1)
                pe.wait_ge(xt_lo, n + 1)
                for c in range(C):
                    i = 0
                    for k in range(DC):
                        for w, a in split_passes(wq, xt_part):
                            mm = pe.matmul(ps_m[:, c * PAIR:(c + 1) * PAIR], w[:, k, c * P:(c + 1) * P],
                                           a[:, k, :], start=i == 0, stop=i == 3 * DC - 1)
                            i += 1
                mm.then_inc(e_q, 1)

            def scores(n, t, T):
                par = (t // 2) % 2
                cols = slice((t % 2) * TOK, (t % 2) * TOK + TOK)
                for g in range(G):
                    per = min(HC, 4)
                    for j in range(4 // per):
                        h = 4 * g + j * per
                        c = h // HC
                        for i, (a, kk) in enumerate(split_passes(q_part, kblk)):
                            mm = pe.matmul(ps_s[:, g, j * per * S:(j + 1) * per * S], a[:, par, c, cols],
                                           kk[:, c, h % HC:h % HC + per, :],
                                           start=i == 0, stop=i == 2)
                mm.then_inc(e_s, 1)

            def p_transpose(T, t):
                pe.wait_ge(a_exp, T + 1)
                for g in range(G):
                    u = G * T + g
                    if not (isinstance(u, int) and u < 2):
                        pe.wait_ge(t_lo, u - 1)
                    for j in range(4):
                        mm = pe.transpose(ps_t[0:S, g % 2, j * TOK:(j + 1) * TOK],
                                          prob[:, t % 2, 4 * g + j, :], ident[:, :])
                    mm.then_inc(e_t, 1)

            def pv(n, par):
                pe.wait_ge(t_lo, G * (2 * n + 2))
                for c in range(C):
                    i = 0
                    for j in range(HC):
                        h = c * HC + j
                        for v, a in split_passes(vpad, pt):
                            mm = pe.matmul(ps_o[:, c, :], v[:, h * P:(h + 1) * P], a[:, par, h, :],
                                           start=i == 0, stop=i == 3 * HC - 1)
                            i += 1
                mm.then_inc(e_pv, 1)

            def r_transpose(n):
                pe.wait_ge(r_wide, 2 * n + 2)
                for c in range(C):
                    for t in range(2):
                        at = c * PAIR + t * TOK
                        mm = pe.transpose(ps_m[:, at:at + TOK], rwide[:, t, c * P:(c + 1) * P], ident[:, :])
                mm.then_inc(e_rt, 1)

            def out_proj(n):
                pe.wait_ge(o_hi, n + 1)
                pe.wait_ge(o_lo, n + 1)
                for t in range(2):
                    i = 0
                    for c in range(C):
                        for a, w in split_passes(o_part, wo):
                            mm = pe.matmul(ps_m[:, t * D:(t + 1) * D], a[:, c, t * TOK:(t + 1) * TOK],
                                           w[:, c, :], start=i == 0, stop=i == 3 * C - 1)
                            i += 1
                mm.then_inc(e_o, 1)

            pe.wait_ge(s_w[0], 16)
            k_proj(0, 0)
            pe.wait_ge(kt_raw, 1)
            pe.wait_ge(s_w[1], 16)
            v_proj()
            pe.wait_ge(vt_raw, 1)
            x_transpose(0, 0)
            pe.wait_ge(xt_raw, 1)
            pe.wait_ge(w_hi, 2)
            pe.wait_ge(w_lo, 2)
            q_proj(0)

            def body(b, first):
                for p in range(PB):
                    n = PB * b + p
                    lag = not (first and p == 0)
                    T = 2 * n
                    if p == 0:
                        pe.wait_ge(kb_hi, b + 1)
                        pe.wait_ge(kb_lo, b + 1)
                    pe.wait_ge(q_hi, n + 1)
                    pe.wait_ge(q_lo, n + 1)
                    if lag:
                        pe.wait_ge(d_sub, T)
                    scores(n, 2 * p, T)
                    if not lag:
                        pe.wait_ge(qt_raw, 1)
                    elif not (first and p == 1):
                        pe.wait_ge(d_fin, n - 1)
                    x_transpose(n + 1, (p + 1) % 2)
                    if lag:
                        p_transpose(T - 1, 1)
                        if not (first and p == 1):
                            pe.wait_ge(o_raw, n - 1)
                        if p == 1:
                            pe.wait_ge(v_hi, b + 1)
                            pe.wait_ge(v_lo, b + 1)
                        pv(n - 1, (p - 1) % 2)
                        pe.wait_ge(xt_raw, n + 2)
                        r_transpose(n - 1)
                        if p == 0:
                            pe.wait_ge(rt_copied, n)
                            v_proj()
                    pe.wait_ge(d_sub, T + 1)
                    scores(n, 2 * p + 1, T + 1)
                    if not lag:
                        pe.wait_ge(xt_raw, n + 2)
                    elif p == 0:
                        pe.wait_ge(vt_raw, b + 1)
                    else:
                        pe.wait_ge(rt_copied, n)
                    if p == PB - 1:
                        k_proj(b + 1, n)
                        pe.wait_ge(kt_raw, b + 2)
                    q_proj(n + 1)
                    p_transpose(T, 0)
                    if lag:
                        pe.wait_ge(qt_raw, n + 2)
                        out_proj(n - 1)

            batches(pe, body)
            n = NP
            pe.wait_ge(qt_raw, n + 1)
            p_transpose(2 * n - 1, 1)
            pe.wait_ge(o_raw, n - 1)
            pv(n - 1, (n - 1) % 2)
            pe.wait_ge(d_fin, n - 1)
            r_transpose(n - 1)
            pe.wait_ge(rt_copied, n)
            out_proj(n - 1)

        @block.scalar
        def _(act):
            own = Own(act, own_a)

            def x_parts(n):
                act.wait_ge(e_xt, n + 1)
                if not (isinstance(n, int) and n == 0):
                    act.wait_ge(xt_lo, n)
                for c in range(DC):
                    src = ps_m[:, c * PAIR:(c + 1) * PAIR]
                    if ln2:
                        ins = act.activation(xt[:, c, :], src, ACT.Identity, bias=ln_sb[:, 1, c:c + 1],
                                             scale=ln_sb[:, 0, c:c + 1])
                    else:
                        ins = act.activation(xt[:, c, :], src, ACT.Copy)
                ins.then_inc(xt_raw, 1)
                act.wait_ge(xt_raw, n + 1)
                if not (isinstance(n, int) and n == 0):
                    act.wait_ge(e_q, n)
                act.activation(xt_part[0][:, :, :], xt[:, :, :], ACT.Copy).then_inc(xt_hi, 1)

            def q_parts(n, par):
                act.wait_ge(e_q, n + 1)
                if not (isinstance(n, int) and n == 0):
                    act.wait_ge(q_lo, n)
                for c in range(C):
                    src = ps_m[:, c * PAIR:(c + 1) * PAIR]
                    if bias:
                        ins = act.activation(qt[:, c, :], src, ACT.Identity, bias=qbias[:, c:c + 1], scale=SCALE)
                    else:
                        ins = act.activation(qt[:, c, :], src, ACT.Copy, scale=SCALE)
                ins.then_inc(qt_raw, 1)
                act.wait_ge(qt_raw, n + 1)
                act.activation(q_part[0][:, par, :, :], qt[:, :, :], ACT.Copy).then_inc(q_hi, 1)

            def k_parts(b):
                act.wait_ge(e_k, b + 1)
                if not (isinstance(b, int) and b == 0):
                    act.wait_ge(kt_lo, b)
                    act.wait_ge(kb_hi, b)
                for c in range(C):
                    src = ps_m[:, c * S:(c + 1) * S]
                    if bias:
                        ins = act.activation(kt[:, c, :], src, ACT.Identity, bias=kbias[:, c:c + 1], scale=1.0)
                    else:
                        ins = act.activation(kt[:, c, :], src, ACT.Copy)
                ins.then_inc(kt_raw, 1)
                act.wait_ge(kt_raw, b + 1)
                act.activation(kt_part[0][:, :, :], kt[:, :, :], ACT.Copy).then_inc(kt_hi, 1)

            def v_parts(b, n):
                act.wait_ge(vt_raw, b + 1)
                if n is not None:
                    act.wait_ge(e_pv, n)
                for c, dst in enumerate(diag(vpad[0])):
                    ins = act.activation(dst, vt[:, c * P:(c + 1) * P].rearrange("s (j w) -> s j w", w=dh), ACT.Copy)
                ins.then_inc(v_hi, 1)

            def prob_hi(T, par, t):
                for g in range(G):
                    act.wait_ge(e_t, G * T + g + 1)
                    dst = pt[0][:, par, 4 * g:4 * g + 4, t * TOK:(t + 1) * TOK]
                    act.activation(dst, ps_t[0:S, g % 2, :].rearrange("s (h q) -> s h q", h=4),
                                   ACT.Copy).then_inc(t_hi, 1)

            def exp(T, t):
                act.wait_ge(d_sub, T + 1)
                act.activation(prob[:, t, :, :], prob[:, t, :, :], ACT.Exp).then_inc(a_exp, 1)

            def rt_copy(n):
                act.wait_ge(e_rt, n + 1)
                act.activation(rt[:, :, :], ps_m[:, 0:QW].rearrange("p (c q) -> p c q", c=C),
                               ACT.Copy).then_inc(rt_copied, 1)

            def out_hi(n):
                act.wait_ge(o_raw, n + 1)
                act.activation(o_part[0][:, :, :], ot[:, :, :], ACT.Copy).then_inc(o_hi, 1)

            if small_n := 16 * ((4 if bias else 0) + (2 if ln2 else 0)):
                act.wait_ge(s_small, small_n)
            if bias:
                own.step(act.activation(qbias[:, :], qbias[:, :], ACT.Copy, scale=SCALE))
            k_parts(0)
            act.wait_ge(s_zeros, 1)
            v_parts(0, None)
            for i, (hi, raw) in enumerate(((wq, wq_raw), (wo, wo_raw))):
                act.wait_ge(s_w[2 + i], 16)
                act.activation(hi[0][:, :, :], raw[:, :, :], ACT.Copy).then_inc(w_hi, 1)
            x_parts(0)
            q_parts(0, 0)

            def body(b, first):
                for p in range(PB):
                    n = PB * b + p
                    T = 2 * n
                    lag = not (first and p == 0)
                    x_parts(n + 1)
                    if lag:
                        if not (first and p == 1):
                            act.wait_ge(e_pv, n - 1)
                        prob_hi(T - 1, (p - 1) % 2, 1)
                    exp(T, 0)
                    if lag:
                        rt_copy(n - 1)
                        if p == 0:
                            v_parts(b, n)
                        if not (first and p == 1):
                            act.wait_ge(e_o, n - 1)
                        out_hi(n - 1)
                    if p == PB - 1:
                        k_parts(b + 1)
                    q_parts(n + 1, (p + 1) % 2)
                    if not (first and p <= 1):
                        act.wait_ge(e_pv, n - 1)
                    prob_hi(T, p % 2, 0)
                    exp(T + 1, 1)

            own.clear()
            batches(act, body, own)
            n = NP
            prob_hi(2 * n - 1, (n - 1) % 2, 1)
            rt_copy(n - 1)
            act.wait_ge(e_o, n - 1)
            out_hi(n - 1)

        @block.gpsimd
        def _(pool):
            own = Own(pool, own_p)
            own.link(pool.memset(one[:, :], 1.0))
            own.step(pool.memset(head_mask[:, :], 1.0))
            own.step(pool.affine_select(out=head_mask[:, :], in_=head_mask[:, :], compare_op=ALU.is_ge, fill=0.0,
                                        base=0, pattern=[[-dh, HC]], channel_multiplier=1))
            pool.affine_select(out=head_mask[:, :], in_=head_mask[:, :], compare_op=ALU.is_ge, fill=0.0,
                               base=dh - 1, pattern=[[dh, HC]], channel_multiplier=-1).then_inc(s_const, 1)

            def normed(n, par, at, final):
                if final and not ln2 and not (isinstance(n, int) and n < 2):
                    pool.wait_ge(e_xt, n - 1)
                newton(own, pool, rs[:, par, 1, :], rs[:, par, 2, :], rs[:, par, 3, :])
                for t in range(2):
                    src = xn[:, par, t, :] if final and ln2 else x[:, at, t, :]
                    ins = pool.tensor_scalar(xn[:, par, t, :], src, mv[:, par, t, 0:1],
                                             rs[:, par, 2, t:t + 1], ALU.subtract, ALU.mult)
                ins.then_inc(ln_done if final else ln1, 1)

            def layer_norm_1(n, par, at):
                pool.wait_ge(stat1, n + 1)
                if ln2 and not (isinstance(n, int) and n < 2):
                    pool.wait_ge(e_xt, n - 1)
                normed(n, par, at, not ln2)

            def layer_norm_2(n, par, at):
                if ln2:
                    pool.wait_ge(stat2, n + 1)
                    normed(n, par, at, True)

            def low(part, raw, ready, n, done):
                pool.wait_ge(ready, n + 1)
                pool.tensor_tensor(part[1], raw, part[0], ALU.subtract).then_inc(done, 1)

            def x_low(n):
                pool.wait_ge(xt_hi, n + 1)
                pool.tensor_tensor(xt_part[1][:, :, :], xt[:, :, :], xt_part[0][:, :, :],
                                   ALU.subtract).then_inc(xt_lo, 1)

            def q_low(n, par):
                pool.wait_ge(q_hi, n + 1)
                pool.tensor_tensor(q_part[1][:, par, :, :], qt[:, :, :], q_part[0][:, par, :, :],
                                   ALU.subtract).then_inc(q_lo, 1)

            def o_low(n):
                pool.wait_ge(o_hi, n + 1)
                pool.tensor_tensor(o_part[1][:, :, :], ot[:, :, :], o_part[0][:, :, :],
                                   ALU.subtract).then_inc(o_lo, 1)

            def widen(n, par, t):
                pool.wait_ge(d_r, 2 * n + t + 1)
                if not (isinstance(n, int) and n == 0):
                    pool.wait_ge(e_rt, n)
                pool.tensor_tensor(rwide[:, t, :].rearrange("p (h w) -> p h w", w=dh),
                                   spread(rsum[:, par, t, :].unsqueeze(2), 2, dh),
                                   one[:, :].unsqueeze(2).broadcast_to([P, H, dh]), ALU.mult).then_inc(r_wide, 1)

            def k_low(b, T):
                pool.wait_ge(kt_hi, b + 1)
                pool.tensor_tensor(kt_part[1][:, :, :], kt[:, :, :], kt_part[0][:, :, :],
                                   ALU.subtract).then_inc(kt_lo, 1)
                pool.wait_ge(kt_lo, b + 1)
                if T is not None:
                    pool.wait_ge(e_s, T)
                for c in range(C):
                    ins = pool.tensor_tensor(kblk[1][:, c, :, :], spread(kt_part[1][:, c, :].unsqueeze(1), 1, HC),
                                             spread(head_mask[:, :].unsqueeze(2), 2, S), ALU.mult)
                ins.then_inc(kb_lo, 1)

            def v_low(b):
                pool.wait_ge(v_hi, b + 1)
                for c, (hi, lo) in enumerate(zip(diag(vpad[0]), diag(vpad[1]))):
                    ins = pool.tensor_tensor(lo, vt[:, c * P:(c + 1) * P].rearrange("s (j w) -> s j w", w=dh),
                                             hi, ALU.subtract)
                ins.then_inc(v_lo, 1)

            pool.wait_ge(s_const, 1)
            layer_norm_1(0, 0, 0)
            k_low(0, None)
            pool.wait_ge(s_zeros, 1)
            v_low(0)
            layer_norm_2(0, 0, 0)
            x_low(0)
            layer_norm_1(1, 1, 1)
            q_low(0, 0)
            layer_norm_2(1, 1, 1)

            def body(b, first):
                for p in range(PB):
                    n = PB * b + p
                    lag = not (first and p == 0)
                    x_low(n + 1)
                    if lag:
                        widen(n - 1, (p - 1) % 2, 1)
                    if lag and p == 0:
                        v_low(b)
                    layer_norm_1(n + 2, p % 2, (p + 2) % RING)
                    if lag:
                        if not (first and p == 1):
                            pool.wait_ge(e_o, n - 1)
                        o_low(n - 1)
                    if p == PB - 1:
                        k_low(b + 1, 2 * n + 2)
                    q_low(n + 1, (p + 1) % 2)
                    widen(n, p % 2, 0)
                    layer_norm_2(n + 2, p % 2, (p + 2) % RING)

            own.clear()
            batches(pool, body, own)
            widen(NP - 1, (NP - 1) % 2, 1)
            pool.wait_ge(e_o, NP - 1)
            o_low(NP - 1)

        @block.vector
        def _(dve):
            own = Own(dve, own_v)

            def ln_stats(src, par, done):
                for t in range(2):
                    own.link(dve.bn_stats(stats[:, t, :], src[:, t, :]))
                own.wait()
                for t in range(2):
                    own.link(dve.bn_aggr(mv[:, par, t, :], stats[:, t, :]))
                own.wait()
                rsqrt_guess(own, dve, mv[:, par, :, 1], rs[:, par, 0, :], rs[:, par, 1, :], rs[:, par, 2, :])
                dve.tensor_scalar(rs[:, par, 2, :].bitcast(I32), rs[:, par, 2, :].bitcast(I32), -1, RSQRT_MAGIC,
                                  ALU.mult, ALU.add).then_inc(done, 1)

            def stats_1(n, par, at, times):
                dve.wait_ge(x_in[at], 16 * times)
                if not (isinstance(n, int) and n < 2):
                    dve.wait_ge(ln_done, n - 1)
                ln_stats(x[:, at, :, :], par, stat1)

            def stats_2(n, par):
                if ln2:
                    dve.wait_ge(ln1, n + 1)
                    ln_stats(xn[:, par, :, :], par, stat2)

            def v_bias(b):
                dve.wait_ge(e_v, b + 1)
                if not (isinstance(b, int) and b == 0):
                    dve.wait_ge(v_lo, b)
                if bias:
                    dve.tensor_tensor(vt[:, :], ps_m[0:S, 0:HD], vbias[:, :], ALU.add).then_inc(vt_raw, 1)
                else:
                    dve.tensor_copy(vt[:, :], ps_m[0:S, 0:HD]).then_inc(vt_raw, 1)

            def k_block(b, T):
                dve.wait_ge(kt_hi, b + 1)
                if T is not None:
                    dve.wait_ge(e_s, T)
                for c in range(C):
                    ins = dve.tensor_tensor(kblk[0][:, c, :, :], spread(kt_part[0][:, c, :].unsqueeze(1), 1, HC),
                                            spread(head_mask[:, :].unsqueeze(2), 2, S), ALU.mult)
                ins.then_inc(kb_hi, 1)

            sc = ps_s[:, :, 0:4 * S].rearrange("p g (h s) -> p g h s", h=4)

            def shift(T, t):
                dve.wait_ge(e_s, T + 1)
                own.step(dve.tensor_reduce(negmax[:, :].rearrange("p (g h) -> p g h", h=4), sc, AX.X, ALU.max,
                                           negate=True))
                if not (isinstance(T, int) and T < 2):
                    dve.wait_ge(e_t, G * (T - 1))
                dve.tensor_tensor(prob[:, t, :, :].rearrange("p (g h) s -> p g h s", h=4), sc,
                                  spread(negmax[:, :].rearrange("p (g h) -> p g h", h=4).unsqueeze(3), 3, S),
                                  ALU.add).then_inc(d_sub, 1)

            def prob_lo(T, par, t):
                for g in range(G):
                    dve.wait_ge(t_hi, G * T + g + 1)
                    cols = slice(t * TOK, (t + 1) * TOK)
                    dve.tensor_tensor(pt[1][:, par, 4 * g:4 * g + 4, cols],
                                      ps_t[0:S, g % 2, :].rearrange("s (h q) -> s h q", h=4),
                                      pt[0][:, par, 4 * g:4 * g + 4, cols], ALU.subtract).then_inc(t_lo, 1)

            def recip_sum(T, par, t):
                dve.wait_ge(a_exp, T + 1)
                own.step(dve.tensor_reduce(rsum[:, par, t, :], prob[:, t, :, :], AX.X, ALU.add))
                dve.reciprocal(rsum[:, par, t, :], rsum[:, par, t, :]).then_inc(d_r, 1)

            def normalize(n):
                dve.wait_ge(e_pv, n + 1)
                dve.wait_ge(rt_copied, n + 1)
                if not (isinstance(n, int) and n == 0):
                    dve.wait_ge(o_lo, n)
                dve.tensor_tensor(ot[:, :, :], ps_o[:, :, :], rt[:, :, :], ALU.mult).then_inc(o_raw, 1)

            def residual(n, at):
                dve.wait_ge(e_o, n + 1)
                src = ps_m[:, 0:2 * D].rearrange("p (t d) -> p t d", t=2)
                if bias:
                    own.step(dve.tensor_tensor(y[:, :, :], src, spread(obias[:, :].unsqueeze(1), 1, 2), ALU.add))
                    src = y[:, :, :]
                dve.scalar_tensor_tensor(out=x[:, at, :, :], in0=src, scalar=gate, in1=x[:, at, :, :],
                                         op0=ALU.mult, op1=ALU.add).then_inc(d_fin, 1)

            own.link(dve.memset(vpad[0][:, :].bitcast(F32), 0.0))
            own.link(dve.memset(vpad[1][:, :].bitcast(F32), 0.0))
            own.wait()
            dve.sem_inc(s_zeros, 1)
            stats_1(0, 0, 0, 1)
            dve.wait_ge(s_const, 1)
            k_block(0, None)
            if bias:
                dve.wait_ge(s_small, 16 * 4)
            v_bias(0)
            stats_2(0, 0)
            for i, (part, raw) in enumerate(((wq, wq_raw), (wo, wo_raw))):
                dve.wait_ge(w_hi, i + 1)
                dve.tensor_tensor(part[1][:, :, :], raw[:, :, :], part[0][:, :, :], ALU.subtract).then_inc(w_lo, 1)
            stats_1(1, 1, 1, 1)
            stats_2(1, 1)

            def body(b, first):
                for p in range(PB):
                    n = PB * b + p
                    T = 2 * n
                    lag = not (first and p == 0)
                    shift(T, 0)
                    if lag:
                        if not (first and p == 1):
                            dve.wait_ge(e_pv, n - 1)
                        prob_lo(T - 1, (p - 1) % 2, 1)
                    recip_sum(T, p % 2, 0)
                    stats_1(n + 2, p % 2, (p + 2) % RING, b + (1 if p < 2 else 2))
                    if lag:
                        normalize(n - 1)
                        if p == 0:
                            v_bias(b)
                    shift(T + 1, 1)
                    if p == PB - 1:
                        k_block(b + 1, 2 * n + 2)
                    prob_lo(T, p % 2, 0)
                    recip_sum(T + 1, p % 2, 1)
                    stats_2(n + 2, p % 2)
                    if lag:
                        residual(n - 1, (p - 1) % RING)

            own.clear()
            batches(dve, body, own)
            n = NP
            prob_lo(2 * n - 1, (n - 1) % 2, 1)
            normalize(n - 1)
            residual(n - 1, RING - 1)


WCH = 1024


class FfnWeights:

    def __init__(self, w1T, w2T, h1T, h2T, w3T):
        self.K = {"w1": w1T.shape[0] // P, "w2": w2T.shape[0] // P, "h1": h1T.shape[0] // P,
                  "h2": h2T.shape[0] // P, "w3": w3T.shape[0] // P}
        self.src = []
        self.at = {}
        col = 0
        for name, w in (("w1", w1T), ("w2", w2T), ("h1", h1T), ("h2", h2T), ("w3", w3T)):
            self.at[name] = (col, w.shape[1])
            per = WCH // w.shape[1]
            for k in range(0, self.K[name], per):
                self.src.append(w[k * P:(k + per) * P, :].rearrange("(k p) n -> p k n", p=P))
            col += self.K[name] * w.shape[1]
        self.cols = col
        assert col == WCH * len(self.src)

    def chunk(self, w, name, k, a, b):
        at, width = self.at[name]
        return w[:, at + k * width + a:at + k * width + b]


def feed_forward(nc, ident, gate, x_src, x_dst, fw, w, scales, s3, exact, tag):
    BT = 4
    BLK = BT * TOK
    NB = x_src.shape[0] // BLK
    HC = fw.K["h1"]
    XR = 2
    xs = x_src.rearrange("(n t p) d -> n p t d", t=BT, p=P)
    xd = x_dst.rearrange("(n t p) d -> n p t d", t=BT, p=P)
    ADT = F32R if exact else F32
    PARTS = 2 if exact else 1
    U = 2 * HC

    with semaphores(nc, tag) as sem, ExitStack() as ctx:
        def sb(name, shape, dt=F32):
            return ctx.enter_context(nc.sbuf_tensor(f"{tag}_{name}", shape, dt))

        x = sb("x", [P, XR, BT, D])
        stats = sb("stats", [P, BT, 6])
        mv = sb("mv", [P, BT, 2])
        rs = sb("rs", [P, 4, BT])
        xn = sb("xn", [P, BT, D])
        xt = sb("xt", [P, DC, BLK]) if exact else None
        xt_part = [sb(f"xt_part{i}", [P, DC, BLK], ADT) for i in range(PARTS)]
        silu = sb("silu", [P, 2, BLK])
        raw = sb("raw", [P, 2, BLK]) if exact else None
        ha = [sb(f"ha{i}", [P, HC, BLK], ADT) for i in range(PARTS)]
        hb = [sb(f"hb{i}", [P, HC, BLK], ADT) for i in range(PARTS)]
        y = sb("y", [P, 2, 2, D])
        ps = ctx.enter_context(nc.psum_tensor(f"{tag}_ps", [P, 4, 512], F32))
        ps_x = ctx.enter_context(nc.psum_tensor(f"{tag}_ps_x", [P, DC, BLK], F32))
        ps_y = ctx.enter_context(nc.psum_tensor(f"{tag}_ps_y", [P, BT, D], F32))

        x_in = [sem(f"x_in{i}") for i in range(XR)]
        x_out = [sem(f"x_out{i}") for i in range(XR)]
        stat, ln, e_xt, xt_raw, xt_hi, xt_lo = (sem(n) for n in ("stat", "ln", "pe_xt", "xt_raw", "s_xt_hi", "s_xt_lo"))
        e_a, a_silu, a_raw, a_hi, a_lo = (sem(n) for n in ("pe_a", "a_silu", "a_raw", "a_hi", "a_lo"))
        e_u, u_raw, u_hi, u_lo = (sem(n) for n in ("pe_u", "u_raw", "u_hi", "u_lo"))
        e_y, d_y = sem("pe_y"), sem("y_done")
        own_v, own_a, own_p = sem("own_v"), sem("own_a"), sem("own_p")
        if not exact:
            xt_lo, a_lo, u_lo = xt_raw, a_raw, u_raw

        def blocks(eng, body, own=None, end=NB // XR):
            def pair(i, first):
                for u in range(XR):
                    body(XR * i + u, u, i, first and u == 0)
                if own:
                    own.clear()

            pair(0, True)
            with eng.Fori(1, end) as i:
                pair(i, False)

        block = ctx.enter_context(nc.Block())

        @block.sync
        def _(sp):
            def load(b, at):
                sp.dma_start(x[:, at, :, :], xs[b]).then_inc(x_in[at], 16)

            def body(b, u, i, first, ahead=None):
                if not first:
                    sp.wait_ge(x_out[1 - u], 16 * (i + u))
                load(b + 1 if ahead is None else ahead, 1 - u)
                sp.wait_ge(d_y, 2 * b + 2)
                sp.dma_start(xd[b], x[:, u, :, :]).then_inc(x_out[u], 16)

            load(0, 0)
            blocks(sp, body, end=NB // XR - 1)
            i = NB // XR - 1
            body(NB - 2, 0, i, False)
            body(NB - 1, 1, i, False, ahead=0)
            for u in range(XR):
                sp.wait_ge(x_out[u], 16 * (NB // XR))

        @block.tensor
        def _(pe):
            def x_transpose(b):
                pe.wait_ge(ln, b + 1)
                for c in range(DC):
                    for t in range(BT):
                        mm = pe.transpose(ps_x[:, c, t * TOK:(t + 1) * TOK], xn[:, t, c * P:(c + 1) * P], ident[:, :])
                mm.then_inc(e_xt, 1)

            def product(out, name, j, parts, ready=None):
                K = fw.K[name]
                for k in range(K):
                    if ready is not None:
                        for s, v in ready(k):
                            pe.wait_ge(s, v)
                    for i, a in enumerate(parts):
                        mm = pe.matmul(out, fw.chunk(w, name, k, j * P, (j + 1) * P), a[:, k, :],
                                       start=k == 0 and i == 0, stop=k == K - 1 and i == len(parts) - 1)
                return mm

            pe.wait_ge(ln, 1)
            x_transpose(0)

            def body(b, u_, i_, first):
                for j in range(HC):
                    if j == 0:
                        pe.wait_ge(xt_hi if exact else xt_raw, b + 1)
                        pe.wait_ge(xt_lo, b + 1)
                    if j >= 2:
                        pe.wait_ge(a_raw, HC * b + j - 1)
                    elif not first:
                        pe.wait_ge(u_raw, U * b)
                    product(ps[:, 2 * (j % 2), :], "w1", j, xt_part)
                    product(ps[:, 2 * (j % 2) + 1, :], "w2", j, xt_part).then_inc(e_a, 1)
                for u in range(U):
                    if u < 4:
                        pe.wait_ge(a_raw, HC * b + HC - 1 + u // 2)
                    else:
                        pe.wait_ge(u_raw, U * b + u - 3)
                    if u < HC:
                        ready = (lambda k: ((a_hi if exact else a_raw, HC * b + k + 1), (a_lo, HC * b + k + 1)))
                        product(ps[:, u % 4, :], "h1", u, ha, ready if u == 0 else None).then_inc(e_u, 1)
                    else:
                        ready = (lambda k: ((u_hi if exact else u_raw, U * b + k + 1), (u_lo, U * b + k + 1)))
                        product(ps[:, u % 4, :], "h2", u - HC, hb, ready if u == HC else None).then_inc(e_u, 1)
                pe.wait_ge(xt_raw, b + 1)
                x_transpose(b + 1)
                for half in range(2):
                    if half == 0 and not first:
                        pe.wait_ge(d_y, 2 * b)
                    for t in range(2 * half, 2 * half + 2):
                        for k in range(HC):
                            if t == 0:
                                pe.wait_ge(u_hi if exact else u_raw, U * b + HC + k + 1)
                                pe.wait_ge(u_lo, U * b + HC + k + 1)
                            for i, a in enumerate(ha):
                                mm = pe.matmul(ps_y[:, t, :], a[:, k, t * TOK:(t + 1) * TOK],
                                               fw.chunk(w, "w3", k, 0, D), start=k == 0 and i == 0,
                                               stop=k == HC - 1 and i == PARTS - 1)
                    mm.then_inc(e_y, 1)

            blocks(pe, body)

        @block.scalar
        def _(act):
            own = Own(act, own_a)

            def x_out_of_psum(b):
                act.wait_ge(e_xt, b + 1)
                if exact:
                    if not (isinstance(b, int) and b == 0):
                        act.wait_ge(xt_lo, b)
                    act.activation(xt[:, :, :], ps_x[:, :, :], ACT.Copy).then_inc(xt_raw, 1)
                    act.wait_ge(xt_raw, b + 1)
                    act.activation(xt_part[0][:, :, :], xt[:, :, :], ACT.Copy).then_inc(xt_hi, 1)
                else:
                    act.activation(xt_part[0][:, :, :], ps_x[:, :, :], ACT.Copy).then_inc(xt_raw, 1)

            def a_high(b, j):
                if exact:
                    act.wait_ge(a_raw, HC * b + j + 1)
                    act.activation(ha[0][:, j, :], raw[:, j % 2, :], ACT.Copy).then_inc(a_hi, 1)

            x_out_of_psum(0)

            def body(b, u_, i_, first):
                for j in range(HC):
                    act.wait_ge(e_a, HC * b + j + 1)
                    if not (first and j < 2):
                        act.wait_ge(a_raw, HC * b + j - 1)
                    act.activation(silu[:, j % 2, :], ps[:, 2 * (j % 2), :], ACT.Silu,
                                   scale=scales[:, 0, j:j + 1]).then_inc(a_silu, 1)
                    if j:
                        a_high(b, j - 1)
                a_high(b, HC - 1)
                for u in range(U):
                    act.wait_ge(e_u, U * b + u + 1)
                    dst = (hb if u < HC else ha)[0][:, u % HC, :]
                    scale = scales[:, 2 + u // HC, u % HC:u % HC + 1]
                    if not exact:
                        act.activation(dst, ps[:, u % 4, :], ACT.Gelu, scale=scale).then_inc(u_raw, 1)
                        continue
                    if u < 2:
                        act.wait_ge(a_lo, HC * b + HC - 1 + u)
                    else:
                        act.wait_ge(u_lo, U * b + u - 1)
                    act.activation(raw[:, u % 2, :], ps[:, u % 4, :], ACT.Gelu, scale=scale).then_inc(u_raw, 1)
                    act.wait_ge(u_raw, U * b + u + 1)
                    act.activation(dst, raw[:, u % 2, :], ACT.Copy).then_inc(u_hi, 1)
                x_out_of_psum(b + 1)

            blocks(act, body, own)

        @block.gpsimd
        def _(pool):
            own = Own(pool, own_p)

            def layer_norm(b, at):
                pool.wait_ge(stat, b + 1)
                if not (isinstance(b, int) and b == 0):
                    pool.wait_ge(e_xt, b)
                newton(own, pool, rs[:, 1, :], rs[:, 2, :], rs[:, 3, :])
                for t in range(BT):
                    ins = pool.tensor_scalar(xn[:, t, :], x[:, at, t, :], mv[:, t, 0:1], rs[:, 2, t:t + 1],
                                             ALU.subtract, ALU.mult)
                ins.then_inc(ln, 1)

            def x_low(b):
                if exact:
                    pool.wait_ge(xt_hi, b + 1)
                    pool.tensor_tensor(xt_part[1][:, :, :], xt[:, :, :], xt_part[0][:, :, :],
                                       ALU.subtract).then_inc(xt_lo, 1)

            layer_norm(0, 0)
            x_low(0)

            def body(b, u, i, first):
                layer_norm(b + 1, 1 - u)
                x_low(b + 1)

            own.clear()
            blocks(pool, body, own)

        @block.vector
        def _(dve):
            own = Own(dve, own_v)

            def ln_stats(b, at, times):
                dve.wait_ge(x_in[at], 16 * times)
                if not (isinstance(b, int) and b == 0):
                    dve.wait_ge(ln, b)
                for t in range(BT):
                    own.link(dve.bn_stats(stats[:, t, :], x[:, at, t, :]))
                own.wait()
                for t in range(BT):
                    own.link(dve.bn_aggr(mv[:, t, :], stats[:, t, :]))
                own.wait()
                rsqrt_guess(own, dve, mv[:, :, 1], rs[:, 0, :], rs[:, 1, :], rs[:, 2, :])
                dve.tensor_scalar(rs[:, 2, :].bitcast(I32), rs[:, 2, :].bitcast(I32), -1, RSQRT_MAGIC,
                                  ALU.mult, ALU.add).then_inc(stat, 1)

            def a_low(b, j):
                if exact:
                    dve.wait_ge(a_hi, HC * b + j + 1)
                    dve.tensor_tensor(ha[1][:, j, :], raw[:, j % 2, :], ha[0][:, j, :],
                                      ALU.subtract).then_inc(a_lo, 1)

            ln_stats(0, 0, 1)

            def body(b, u_, i, first):
                for j in range(HC):
                    if j >= 2 or not first:
                        if exact and j >= 2:
                            dve.wait_ge(a_lo, HC * b + j - 1)
                    dve.wait_ge(a_silu, HC * b + j + 1)
                    dst = raw[:, j % 2, :] if exact else ha[0][:, j, :]
                    dve.scalar_tensor_tensor(out=dst, in0=ps[:, 2 * (j % 2) + 1, :], scalar=scales[:, 1, j:j + 1],
                                             in1=silu[:, j % 2, :], op0=ALU.mult, op1=ALU.mult).then_inc(a_raw, 1)
                    if j:
                        a_low(b, j - 1)
                a_low(b, HC - 1)
                for u in range(U):
                    if exact:
                        dve.wait_ge(u_hi, U * b + u + 1)
                        dst = (hb if u < HC else ha)[1][:, u % HC, :]
                        hi = (hb if u < HC else ha)[0][:, u % HC, :]
                        dve.tensor_tensor(dst, raw[:, u % 2, :], hi, ALU.subtract).then_inc(u_lo, 1)
                    if u == HC // 2:
                        ln_stats(b + 1, 1 - u_, i + 1 if u_ == 0 else i + 2)
                for half in range(2):
                    t = slice(2 * half, 2 * half + 2)
                    dve.wait_ge(e_y, 2 * b + half + 1)
                    if not first:
                        dve.wait_ge(d_y, 2 * b + half - 1)
                    own.step(dve.tensor_tensor(y[:, half, :, :], ps_y[:, t, :], spread(s3[:, :].unsqueeze(1), 1, 2), ALU.mult))
                    dve.scalar_tensor_tensor(out=x[:, u_, t, :], in0=y[:, half, :, :], scalar=gate, in1=x[:, u_, t, :],
                                             op0=ALU.mult, op1=ALU.add).then_inc(d_y, 1)

            own.clear()
            blocks(dve, body, own)


def self_attention(nc, ident, gate, x_src, x_dst, wq_src, wk_src, wv_src, ws_src, wo_src, bo_src, B, H, topk):
    N = x_src.shape[0] // B
    NT = N // TOK
    KC = N // P
    HD = wq_src.shape[1]
    dh = HD // H
    CP = H // 2
    PT_ = NT // 2
    SLOTS = H * NT
    UNITS = SLOTS // 2
    PS = 2 * NT
    SCALE = float(dh) ** -0.5
    assert dh == 64 and N == 1024 and DC == 2

    xb_src = x_src.rearrange("(b t p) d -> b p t d", b=B, p=P)
    xb_dst = x_dst.rearrange("(b t p) d -> b p t d", b=B, p=P)
    xp_src = x_src.rearrange("(b q t p) d -> b q p t d", b=B, t=2, p=P)

    items = []
    for c in range(CP):
        s = PS * c
        if c:
            items += [(s + 1, "r", (c - 1, 0)), (s + 2, "r", (c - 1, 1))]
        items += [(s + 5, "k", (c, 0)), (s + 6, "k", (c, 1))]
        items += [(s + 7 + i, "q", (c, i // 2, i % 2)) for i in range(4)]
        items += [(s + 11, "v", (c, 0)), (s + 12, "v", (c, 1))]
    items += [(2, "h", 0), (3, "h", 1), (13, "x", 0), (14, "g", 0), (15, "x", 1), (PS + 4, "g", 1),
              (PS + 13, "x", 2), (PS + 14, "g", 2), (PS + 15, "x", 3), (2 * PS + 4, "g", 3)]
    items.sort(key=lambda i: i[0])
    items += [(SLOTS + i, "r", (CP - 1, i)) for i in range(2)] + [(SLOTS + 2 + i, "o", i) for i in range(PT_)]
    AT = {}
    for m, (slot, _, _) in enumerate(items):
        assert slot not in AT
        AT[slot] = m
    M = len(items)
    READS_ACT = ("k", "q", "v", "x", "g", "h")
    READS_DVE = ("k", "q", "v", "r", "o")
    ln_at = {1: 0, 8: 1, PS + 1: 2, PS + 8: 3}

    def count(kinds, m):
        return sum(kind in kinds for _, kind, _ in items[:m])

    ACT_M, DVE_M = count(READS_ACT, M), count(READS_DVE, M)
    R_M = 2 * CP

    with semaphores(nc, "E") as sem, ExitStack() as ctx:
        def sb(name, shape, dt=F32):
            return ctx.enter_context(nc.sbuf_tensor(f"E_{name}", shape, dt))

        xp = sb("xp", [P, 2, 2, D])
        stats = sb("stats", [P, 2, 6])
        mv = sb("mv", [P, 2, 2, 2])
        rs = sb("rs", [P, 2, 4, 2])
        xn = sb("xn", [P, 2, 2, D])
        xt = sb("xt", [P, DC, N])
        xb = xt[:, :, :].rearrange("p k n -> p (k n)").rearrange("p (t d) -> p t d", d=D)
        xt_part = [sb("xt_hi", [P, DC, N], F32R), sb("xt_lo", [P, DC, N], F32R)]
        w_raw = sb("w_raw", [P, 3, DC, P])
        wq = [sb("wq_hi", [P, DC, 2, P], F32R), sb("wq_lo", [P, DC, 2, P], F32R)]
        wk = [sb("wk_hi", [P, DC, P], F32R), sb("wk_lo", [P, DC, P], F32R)]
        wv = [sb("wv_hi", [P, DC, P], F32R), sb("wv_lo", [P, DC, P], F32R)]
        wo = [sb("wo_hi", [P, CP, D], F32R), sb("wo_lo", [P, CP, D], F32R)]
        ws = sb("ws", [P, DC, H])
        bo = sb("bo", [H, D])
        kk = sb("kk", [P, 2, 2, N], F32R)
        qq = [sb("q_hi", [P, 2, 2, N], F32R), sb("q_lo", [P, 2, 2, N], F32R)]
        vv = sb("vv", [P, 2, KC, 2, P], F32R)
        prob = sb("prob", [P, 2, N])
        pt = [sb("pt_hi", [P, 2, KC, PAIR], F32R), sb("pt_lo", [P, 2, KC, PAIR], F32R)]
        negmax = sb("negmax", [P, 4])
        den = sb("den", [P, H, NT])
        wgt = sb("wgt", [P, 2, NT])
        wwide = sb("wwide", [P, 2, NT // 2, P])
        ot_other = sb("ot_other", [P, PAIR])
        ot_raw = sb("ot_raw", [P, N])
        wo_raw = ot_raw[:, :].rearrange("p (c d) -> p c d", d=D)
        ot = sb("ot", [P, 2, 512])
        o_part = [sb("o_hi", [P, CP, N], F32R), sb("o_lo", [P, CP, N], F32R)]
        logit = sb("logit", [P, NT, H])
        score = sb("score", [P, NT, H])
        before, equal = (wwide[:, :, :, :].rearrange("p n t w -> p (n t w)")[:, i * NT * H * H:(i + 1) * NT * H * H]
                         .rearrange("p (t i j) -> p t i j", i=H, j=H) for i in range(2))
        rank = sb("rank", [P, NT, H])
        one = sb("one", [P, 1])
        lower = sb("lower", [P, H, H])
        chosen = sb("chosen", [P, NT, H])
        chosenT = sb("chosenT", [H, NT, TOK])

        ps_s = ctx.enter_context(nc.psum_tensor("E_ps_s", [P, 2, N], F32))
        ps_t = ctx.enter_context(nc.psum_tensor("E_ps_t", [P, 2, 4, TOK], F32))
        ps_o = ctx.enter_context(nc.psum_tensor("E_ps_o", [P, 2, PAIR], F32))
        ps_m = ctx.enter_context(nc.psum_tensor("E_ps_m", [P, 512], F32))

        w_in, xb_in, xb_out, small = sem("w_in"), sem("xb_in"), sem("xb_out"), sem("small")
        wo_in, xb_free = sem("wo_in"), sem("xb_free")
        xp_in = [sem("xp_in0"), sem("xp_in1")]
        w_hi, w_lo, wo_hi, wo_lo = sem("s_w_hi"), sem("s_w_lo"), sem("s_wo_hi"), sem("s_wo_lo")
        stat, ln = sem("stat"), sem("ln")
        c_hi, c_lo = sem("convert_hi"), sem("convert_lo")
        e_s, e_t, e_pv, e_m = sem("pe_s"), sem("pe_t"), sem("pe_pv"), sem("pe_item")
        m_act, m_dve = sem("item_act"), sem("item_dve")
        d_max, a_exp, t_hi, t_lo = sem("max"), sem("exp"), sem("t_hi"), sem("t_lo")
        o_other, o_sum, d_wgt, p_wide = sem("o_other"), sem("o_sum"), sem("wgt"), sem("wide")
        o_hi, o_lo = sem("s_o_hi"), sem("s_o_lo")
        a_gate, d_chosen, e_chosenT, a_chosenT, s_lower = (sem(n) for n in (
            "a_gate", "chosen_done", "pe_chosenT", "a_chosenT", "lower_made"))
        batch_done = sem("batch_done")
        pre_pe, pre_act, pre_hi, pre_dve = sem("pre_pe"), sem("pre_act"), sem("pre_hi"), sem("pre_dve")
        own_v, own_a, own_p = sem("own_v"), sem("own_a"), sem("own_p")

        def batches(eng, body, own=None, waits=True):
            if own:
                own.clear()
            with eng.Fori(0, B) as b:
                if waits:
                    eng.wait_ge(batch_done, b + 1)
                body(b)
                if own:
                    own.clear()

        def head(v):
            return v // NT

        def r_item(c, n):
            return AT[(PS * (c + 1) + 1 if c < CP - 1 else SLOTS) + n]

        def at_x(q):
            return [m for m, (_, kind, arg) in enumerate(items) if kind == "x" and arg == q][0]

        first_items = ([("k", (n,)) for n in range(2)] + [("q", (j, n)) for j in range(2) for n in range(2)]
                       + [("v", (n,)) for n in range(2)])

        block = ctx.enter_context(nc.Block())

        @block.sync
        def _(sp):
            def load_w(c):
                for i, w in enumerate((wq_src, wk_src, wv_src)):
                    sp.dma_start(w_raw[:, i, :, :], w[:, c * P:(c + 1) * P].rearrange("(k p) n -> p k n", p=P)
                                 ).then_inc(w_in, 16)

            def load_xp(b, q):
                sp.dma_start(xp[:, q % 2, :, :], xp_src[b, q]).then_inc(xp_in[q % 2], 16)

            for q in range(2):
                load_xp(0, q)
            load_w(0)
            sp.dma_start(ws[:, :, :], ws_src.rearrange("(k p) n -> p k n", p=P)).then_inc(small, 16)
            sp.dma_start(bo[:, :], bo_src).then_inc(small, 16)
            for q in range(2, PT_):
                sp.wait_ge(ln, q - 1)
                load_xp(0, q)
            sp.dma_start(wo_raw, wo_src.rearrange("(c p) n -> p c n", p=P)).then_inc(wo_in, 16)

            def body(b, ahead):
                sp.wait_ge(batch_done, b + 1)
                for c in range(CP):
                    sp.wait_ge(w_lo, CP * b + c + 1)
                    load_w((c + 1) % CP)
                    if c < 2:
                        for q in (2 * c, 2 * c + 1):
                            sp.wait_ge(ln, PT_ * b + PT_ + q - 1)
                            load_xp(ahead, q)
                sp.wait_ge(c_lo, PT_ * b + 2 * PT_)
                sp.dma_start(xb, xb_src[b]).then_inc(xb_in, 16)
                for q in range(PT_):
                    sp.wait_ge(m_dve, DVE_M * b + DVE_M - PT_ + q + 1)
                    sp.dma_start(xb_dst[b][:, 2 * q:2 * q + 2, :], xb[:, 2 * q:2 * q + 2, :]).then_inc(xb_out, 16)
                sp.wait_ge(xb_out, 16 * PT_ * b + 16 * PT_)
                sp.sem_inc(xb_free, 1)

            sp.sem_inc(xb_free, 1)
            with sp.Fori(0, B - 1) as b:
                body(b, b + 1)
            body(B - 1, 0)

        @block.tensor
        def _(pe):
            def item(m, b):
                slot, kind, arg = items[m]
                if m:
                    prev = items[m - 1][1]
                    if prev in READS_DVE:
                        pe.wait_ge(m_dve, DVE_M * b + count(READS_DVE, m))
                    else:
                        pe.wait_ge(m_act, ACT_M * b + count(READS_ACT, m))
                run(kind, arg, b).then_inc(e_m, 1)

            def run(kind, arg, b):
                if kind in "kqv":
                    c = arg[0]
                    if arg[1:] in ((0,), (0, 0)) and kind == "k":
                        pe.wait_ge(w_hi, CP * b + c + 2)
                        pe.wait_ge(w_lo, CP * b + c + 2)
                        if c == CP - 1:
                            pe.wait_ge(c_hi, PT_ * b + 2 * PT_)
                            pe.wait_ge(c_lo, PT_ * b + 2 * PT_)
                    return {"k": k_proj, "q": q_proj, "v": v_proj}[kind](*arg[1:])
                if kind == "x":
                    return x_transpose(arg, PT_ * b + PT_ + arg + 1)
                if kind == "g":
                    return logits(arg)
                if kind == "h":
                    pe.wait_ge(d_chosen, b + 1)
                    for t in range(4):
                        mm = pe.transpose(ps_m[0:H, t * TOK:(t + 1) * TOK], chosen[:, 4 * arg + t, :], ident[:, :])
                    return mm
                if kind == "r":
                    c, n = arg
                    pe.wait_ge(p_wide, R_M * b + 2 * c + n + 1)
                    for t in range(4):
                        mm = pe.transpose(ps_m[:, t * TOK:(t + 1) * TOK], wwide[:, n, t, :], ident[:, :])
                    return mm
                if arg == 0:
                    pe.wait_ge(o_hi, R_M * b + R_M)
                    pe.wait_ge(o_lo, R_M * b + R_M)
                for t in range(2):
                    tile = 2 * arg + t
                    cols = slice(tile * TOK, (tile + 1) * TOK)
                    out = ps_m[:, t * D:(t + 1) * D]
                    pe.matmul(out, chosenT[:, tile, :], bo[:, :], start=True, stop=False)
                    i = 0
                    for c in range(CP):
                        for a, w in split_passes(o_part, wo):
                            i += 1
                            mm = pe.matmul(out, a[:, c, cols], w[:, c, :], start=False, stop=i == 3 * CP)
                return mm

            def x_transpose(q, done):
                pe.wait_ge(ln, done)
                for k in range(DC):
                    for t in range(2):
                        at = k * PAIR + t * TOK
                        mm = pe.transpose(ps_m[:, at:at + TOK], xn[:, q % 2, t, k * P:(k + 1) * P], ident[:, :])
                return mm

            def logits(q):
                for t in range(2):
                    for k in range(DC):
                        cols = slice((2 * q + t) * TOK, (2 * q + t + 1) * TOK)
                        mm = pe.matmul(ps_m[:, t * H:(t + 1) * H], xt[:, k, cols], ws[:, k, :],
                                       start=k == 0, stop=k == DC - 1)
                return mm

            def k_proj(n):
                for i, (k, (w, a)) in enumerate((k, x) for k in range(DC) for x in split_passes(wk, xt_part)):
                    mm = pe.matmul(ps_m[:, :], w[:, k, :], a[:, k, n * 512:(n + 1) * 512], start=i == 0,
                                   stop=i == 3 * DC - 1)
                return mm

            def q_proj(j, n):
                for i, (k, (w, a)) in enumerate((k, x) for k in range(DC) for x in split_passes(wq, xt_part)):
                    mm = pe.matmul(ps_m[:, :], w[:, k, j, :], a[:, k, n * 512:(n + 1) * 512], start=i == 0,
                                   stop=i == 3 * DC - 1)
                return mm

            def v_proj(n):
                for t in range(4):
                    cols = slice((4 * n + t) * TOK, (4 * n + t + 1) * TOK)
                    for i, (k, (a, w)) in enumerate((k, x) for k in range(DC) for x in split_passes(xt_part, wv)):
                        mm = pe.matmul(ps_m[:, t * P:(t + 1) * P], a[:, k, cols], w[:, k, :], start=i == 0,
                                       stop=i == 3 * DC - 1)
                return mm

            def scores(v):
                j, cp, cols = head(v) % 2, (head(v) // 2) % 2, slice((v % NT) * TOK, (v % NT + 1) * TOK)
                for n in range(2):
                    for i in range(2):
                        mm = pe.matmul(ps_s[:, v % 2, n * 512:(n + 1) * 512], qq[i][:, cp, j, cols],
                                       kk[:, cp, j, n * 512:(n + 1) * 512], start=i == 0, stop=i == 1)
                mm.then_inc(e_s, 1)

            def p_transpose(v, b):
                for g in range(2):
                    if v:
                        pe.wait_ge(t_lo, 2 * SLOTS * b + 2 * (v - 1) + g + 1)
                    for i in range(4):
                        at = (4 * g + i) * P
                        mm = pe.transpose(ps_t[:, g, i, :], prob[:, v % 2, at:at + P], ident[:, :])
                    mm.then_inc(e_t, 1)

            def pv(u, b):
                h = u // PT_
                pe.wait_ge(t_lo, 2 * SLOTS * b + 4 * (u + 1))
                if u >= 2:
                    pe.wait_ge(o_sum, UNITS * b + u - 1)
                for i in range(KC):
                    for n, a in enumerate(pt):
                        mm = pe.matmul(ps_o[:, u % 2, :], vv[:, (h // 2) % 2, i, h % 2, :], a[:, u % 2, i, :],
                                       start=i == 0 and n == 0, stop=i == KC - 1 and n == 1)
                mm.then_inc(e_pv, 1)

            for q in range(PT_):
                if q:
                    pe.wait_ge(pre_act, 2 * q)
                x_transpose(q, q + 1).then_inc(pre_pe, 1)
                pe.wait_ge(pre_act, 2 * q + 1)
                if q == 0:
                    pe.wait_ge(small, 32)
                logits(q).then_inc(pre_pe, 1)
            pe.wait_ge(pre_act, 2 * PT_)
            pe.wait_ge(w_hi, 1)
            pe.wait_ge(w_lo, 1)
            pe.wait_ge(c_hi, PT_)
            pe.wait_ge(c_lo, PT_)
            for i, (f, arg) in enumerate(first_items):
                if i:
                    pe.wait_ge(pre_dve, i)
                {"k": k_proj, "q": q_proj, "v": v_proj}[f](*arg).then_inc(pre_pe, 1)

            def ready(v, b):
                if v % PS == 0 and v:
                    m = AT[v - PS + 10] + 1
                    pe.wait_ge(m_dve, DVE_M * b + count(READS_DVE, m))

            def body(b):
                scores(0)
                scores(1)
                for v in range(SLOTS):
                    pe.wait_ge(a_exp, SLOTS * b + v + 1)
                    if v + 2 < SLOTS:
                        ready(v + 2, b)
                        scores(v + 2)
                    p_transpose(v, b)
                    if v % 2 == 0 and v:
                        u = v // 2 - 1
                        if u % (2 * PT_) == 0 and u:
                            m = AT[2 * u - PS + 12] + 1
                            pe.wait_ge(m_dve, DVE_M * b + count(READS_DVE, m))
                        pv(u, b)
                    if v in AT:
                        item(AT[v], b)
                pv(UNITS - 1, b)
                for m in range(AT[SLOTS], M):
                    item(m, b)

            pe.wait_ge(pre_dve, len(first_items))
            pe.wait_ge(wo_hi, 1)
            pe.wait_ge(wo_lo, 1)
            batches(pe, body)

        def act_item(act, kind, arg, ready, done, par):
            ready()
            if kind == "k":
                cols = slice(arg[-1] * 512, arg[-1] * 512 + 512)
                act.activation(kk[0:64, par, 0, cols], ps_m[0:64, :], ACT.Copy)
                ins = act.activation(kk[64:P, par, 1, cols], ps_m[64:P, :], ACT.Copy)
            elif kind == "q":
                j, n = arg[-2:]
                ins = act.activation(qq[0][:, par, j, n * 512:(n + 1) * 512], ps_m[:, :], ACT.Copy, scale=SCALE)
            elif kind == "v":
                n = arg[-1]
                ins = act.activation(vv[:, par, 4 * n:4 * n + 4, :, 0:dh],
                                     ps_m[:, :].rearrange("p (t j w) -> p t j w", t=4, j=2), ACT.Copy)
            elif kind == "x":
                ins = act.activation(xt[:, :, arg * PAIR:(arg + 1) * PAIR],
                                     ps_m[:, :].rearrange("p (k q) -> p k q", k=DC), ACT.Copy)
            elif kind == "h":
                ins = act.activation(chosenT[:, 4 * arg:4 * arg + 4, :],
                                     ps_m[0:H, :].rearrange("h (t q) -> h t q", t=4), ACT.Copy)
            else:
                ins = act.activation(logit[:, 2 * arg:2 * arg + 2, :],
                                     ps_m[:, 0:2 * H].rearrange("p (t h) -> p t h", t=2), ACT.Copy)
            ins.then_inc(done, 1)

        def dve_item(dve, kind, arg, done, par):
            if kind == "k":
                cols = slice(arg[-1] * 512, arg[-1] * 512 + 512)
                dve.tensor_tensor(kk[64:P, par, 0, cols], ps_m[0:64, :], kk[0:64, par, 0, cols], ALU.subtract)
                ins = dve.tensor_tensor(kk[0:64, par, 1, cols], ps_m[64:P, :], kk[64:P, par, 1, cols], ALU.subtract)
            elif kind == "q":
                j, n = arg[-2:]
                cols = slice(n * 512, (n + 1) * 512)
                ins = dve.scalar_tensor_tensor(out=qq[1][:, par, j, cols], in0=ps_m[:, :], scalar=SCALE,
                                               in1=qq[0][:, par, j, cols], op0=ALU.mult, op1=ALU.subtract)
            else:
                n = arg[-1]
                ins = dve.tensor_tensor(vv[:, par, 4 * n:4 * n + 4, :, dh:P],
                                        ps_m[:, :].rearrange("p (t j w) -> p t j w", t=4, j=2),
                                        vv[:, par, 4 * n:4 * n + 4, :, 0:dh], ALU.subtract)
            ins.then_inc(done, 1)

        @block.scalar
        def _(act):
            own = Own(act, own_a)

            def split_weights(n):
                act.wait_ge(w_in, 48 * n)
                for k in range(DC):
                    act.activation(wq[0][:, k, :, :].rearrange("p j (r w) -> p j r w", r=2),
                                   spread(w_raw[:, 0, k, :].rearrange("p (j w) -> p j w", j=2).unsqueeze(2), 2, 2),
                                   ACT.Copy)
                act.activation(wk[0][:, :, :], w_raw[:, 1, :, :], ACT.Copy)
                act.activation(wv[0][:, :, :], w_raw[:, 2, :, :], ACT.Copy).then_inc(w_hi, 1)

            def convert(q):
                cols = slice(q * PAIR, (q + 1) * PAIR)
                act.activation(xt_part[0][:, :, cols], xt[:, :, cols], ACT.Copy).then_inc(c_hi, 1)

            def exp(v, b):
                act.wait_ge(d_max, SLOTS * b + v + 1)
                if v >= 2:
                    act.wait_ge(e_t, 2 * SLOTS * b + 2 * (v - 1))
                act.activation(prob[:, v % 2, :], ps_s[:, v % 2, :], ACT.Exp, bias=negmax[:, v % 4:v % 4 + 1],
                               scale=1.0, accum_out=den[:, head(v), v % NT:v % NT + 1]).then_inc(a_exp, 1)

            def prob_hi(v, b):
                u = v // 2
                if u >= 2 and v % 2 == 0:
                    act.wait_ge(e_pv, UNITS * b + u - 1)
                for g in range(2):
                    act.wait_ge(e_t, 2 * SLOTS * b + 2 * v + g + 1)
                    act.activation(pt[0][:, u % 2, 4 * g:4 * g + 4, (v % 2) * TOK:(v % 2 + 1) * TOK],
                                   ps_t[:, g, :, :], ACT.Copy).then_inc(t_hi, 1)

            def other_half(u, b):
                act.wait_ge(e_pv, UNITS * b + u + 1)
                if u:
                    act.wait_ge(o_sum, UNITS * b + u)
                if (u // PT_) % 2 == 0:
                    ins = act.activation(ot_other[0:64, :], ps_o[64:P, u % 2, :], ACT.Copy)
                else:
                    ins = act.activation(ot_other[64:P, :], ps_o[0:64, u % 2, :], ACT.Copy)
                ins.then_inc(o_other, 1)

            def out_hi(c, n, b):
                act.wait_ge(m_dve, DVE_M * b + count(READS_DVE, r_item(c, n) + 1))
                act.activation(o_part[0][:, c, n * 512:(n + 1) * 512], ot[:, n, :], ACT.Copy).then_inc(o_hi, 1)

            def item(m, b):
                slot, kind, arg = items[m]
                if kind in READS_ACT:
                    c = arg[0] if kind in "kqv" else 0
                    if kind == "x" and arg == 0:
                        act.wait_ge(xb_free, b + 1)
                    act_item(act, kind, arg, lambda: act.wait_ge(e_m, M * b + m + 1), m_act, (c + 1) % 2)
                elif kind == "r":
                    out_hi(*arg, b)

            split_weights(1)
            for q in range(PT_):
                act_item(act, "x", q, lambda: act.wait_ge(pre_pe, 2 * q + 1), pre_act, 0)
                act.wait_ge(pre_act, 2 * q + 1)
                convert(q)
                act_item(act, "g", q, lambda: act.wait_ge(pre_pe, 2 * q + 2), pre_act, 0)
            for i, (kind, arg) in enumerate(first_items):
                act_item(act, kind, arg, lambda: act.wait_ge(pre_pe, 2 * PT_ + i + 1), pre_hi, 0)
            act.wait_ge(wo_in, 16)
            act.activation(wo[0][:, :, :], wo_raw, ACT.Copy).then_inc(wo_hi, 1)

            def body(b):
                act.activation(score[:, :, :], logit[:, :, :], ACT.Exp, scale=-1.0).then_inc(a_gate, 1)
                exp(0, b)
                exp(1, b)
                for v in range(SLOTS):
                    if v % 2 and v >= 3:
                        other_half((v - 3) // 2, b)
                    if v - 1 in AT:
                        item(AT[v - 1], b)
                    if v % PS == 1:
                        split_weights(CP * b + v // PS + 2)
                    if v == (CP - 1) * PS:
                        act.wait_ge(m_act, ACT_M * b + count(READS_ACT, AT[PS + 15] + 1))
                        for q in range(PT_):
                            convert(q)
                    prob_hi(v, b)
                    if v + 2 < SLOTS:
                        exp(v + 2, b)
                other_half(UNITS - 1, b)
                for m in range(AT[SLOTS], M):
                    item(m, b)

            batches(act, body, own)

        @block.gpsimd
        def _(pool):
            own = Own(pool, own_p)

            def split_weights(n):
                pool.wait_ge(w_hi, n)
                for k in range(DC):
                    pool.tensor_tensor(wq[1][:, k, :, :].rearrange("p j (r w) -> p j r w", r=2),
                                       spread(w_raw[:, 0, k, :].rearrange("p (j w) -> p j w", j=2).unsqueeze(2), 2, 2),
                                       wq[0][:, k, :, :].rearrange("p j (r w) -> p j r w", r=2), ALU.subtract)
                pool.tensor_tensor(wk[1][:, :, :], w_raw[:, 1, :, :], wk[0][:, :, :], ALU.subtract)
                pool.tensor_tensor(wv[1][:, :, :], w_raw[:, 2, :, :], wv[0][:, :, :], ALU.subtract).then_inc(w_lo, 1)

            def layer_norm(q, n, wait_xn):
                pool.wait_ge(stat, n + 1)
                wait_xn()
                newton(own, pool, rs[:, q % 2, 1, :], rs[:, q % 2, 2, :], rs[:, q % 2, 3, :])
                for t in range(2):
                    ins = pool.tensor_scalar(xn[:, q % 2, t, :], xp[:, q % 2, t, :], mv[:, q % 2, t, 0:1],
                                             rs[:, q % 2, 2, t:t + 1], ALU.subtract, ALU.mult)
                ins.then_inc(ln, 1)

            def convert(q, n):
                pool.wait_ge(c_hi, n + 1)
                cols = slice(q * PAIR, (q + 1) * PAIR)
                pool.tensor_tensor(xt_part[1][:, :, cols], xt[:, :, cols], xt_part[0][:, :, cols],
                                   ALU.subtract).then_inc(c_lo, 1)

            def widen(c, n, b):
                pool.wait_ge(d_wgt, CP * b + c + 1)
                if c:
                    pool.wait_ge(e_m, M * b + r_item(c - 1, n) + 1)
                pool.tensor_tensor(wwide[:, n, :, :].rearrange("p t (j w) -> p t j w", j=2),
                                   spread(wgt[:, :, 4 * n:4 * n + 4].rearrange("p j t -> p t j").unsqueeze(3), 3, dh),
                                   one[:, :].unsqueeze(2).unsqueeze(3).broadcast_to([P, 4, 2, dh]),
                                   ALU.mult).then_inc(p_wide, 1)

            def out_lo(c, n, b):
                pool.wait_ge(o_hi, R_M * b + 2 * c + n + 1)
                cols = slice(n * 512, (n + 1) * 512)
                pool.tensor_tensor(o_part[1][:, c, cols], ot[:, n, :], o_part[0][:, c, cols],
                                   ALU.subtract).then_inc(o_lo, 1)

            own.link(pool.memset(one[:, :], 1.0))
            own.step(pool.memset(lower[:, :, :], 1.0))
            pool.affine_select(out=lower[:, :, :], in_=lower[:, :, :], compare_op=ALU.is_gt, fill=0.0,
                               base=0, pattern=[[1, H], [-1, H]], channel_multiplier=0).then_inc(s_lower, 1)
            layer_norm(0, 0, lambda: None)
            layer_norm(1, 1, lambda: None)
            split_weights(1)
            for q in range(PT_):
                convert(q, q)
                if q + 2 < PT_:
                    layer_norm(q + 2, q + 2, lambda: pool.wait_ge(pre_pe, 2 * q + 1))
            pool.wait_ge(wo_hi, 1)
            pool.tensor_tensor(wo[1][:, :, :], wo_raw, wo[0][:, :, :], ALU.subtract).then_inc(wo_lo, 1)

            def body(b):
                for v in range(SLOTS):
                    c, s = v // PS, v % PS
                    if s == 1:
                        split_weights(CP * b + c + 2)
                    if v in ln_at:
                        q = ln_at[v]
                        layer_norm(q, PT_ * b + PT_ + q,
                                   lambda: pool.wait_ge(e_m, M * b + at_x(q - 2) + 1) if q >= 2 else None)
                    if c and s in (3, 4):
                        out_lo(c - 1, s - 3, b)
                    if v == (CP - 1) * PS + 4:
                        for q in range(PT_):
                            convert(q, PT_ * b + PT_ + q)
                    if s == PS - 1:
                        widen(c, 0, b)
                        widen(c, 1, b)
                for n in range(2):
                    out_lo(CP - 1, n, b)

            batches(pool, body, own)

        @block.vector
        def _(dve):
            own = Own(dve, own_v)

            def ln_stats(q, n, times):
                dve.wait_ge(xp_in[q % 2], 16 * times)
                if not (isinstance(n, int) and n < 2):
                    dve.wait_ge(ln, n - 1)
                for t in range(2):
                    own.link(dve.bn_stats(stats[:, t, :], xp[:, q % 2, t, :]))
                own.wait()
                for t in range(2):
                    own.link(dve.bn_aggr(mv[:, q % 2, t, :], stats[:, t, :]))
                own.wait()
                rsqrt_guess(own, dve, mv[:, q % 2, :, 1], rs[:, q % 2, 0, :], rs[:, q % 2, 1, :], rs[:, q % 2, 2, :])
                dve.tensor_scalar(rs[:, q % 2, 2, :].bitcast(I32), rs[:, q % 2, 2, :].bitcast(I32), -1, RSQRT_MAGIC,
                                  ALU.mult, ALU.add).then_inc(stat, 1)

            def row_max(v, b):
                dve.wait_ge(e_s, SLOTS * b + v + 1)
                dve.tensor_reduce(negmax[:, v % 4:v % 4 + 1], ps_s[:, v % 2, :], AX.X, ALU.max,
                                  negate=True).then_inc(d_max, 1)

            def choose(b):
                dve.wait_ge(a_gate, b + 1)
                own.step(dve.tensor_scalar(score[:, :, :], score[:, :, :], 1.0, None, ALU.add))
                own.step(dve.reciprocal(score[:, :, :], score[:, :, :]))
                other = spread(score[:, :, :].unsqueeze(2), 2, H)
                mine = spread(score[:, :, :].unsqueeze(3), 3, H)
                own.link(dve.tensor_tensor(before, other, mine, ALU.is_gt))
                own.step(dve.tensor_tensor(equal, other, mine, ALU.is_equal))
                own.step(dve.tensor_tensor(equal, equal,
                                           spread(lower[:, :, :].unsqueeze(1), 1, NT), ALU.mult))
                own.step(dve.tensor_tensor(before, before, equal, ALU.add))
                own.step(dve.tensor_reduce(rank[:, :, :], before, AX.X, ALU.add))
                dve.scalar_tensor_tensor(out=chosen[:, :, :], in0=rank[:, :, :], scalar=float(topk),
                                         in1=score[:, :, :], op0=ALU.is_lt, op1=ALU.mult).then_inc(d_chosen, 1)

            def prob_lo(v, b):
                u = v // 2
                for g in range(2):
                    dve.wait_ge(t_hi, 2 * SLOTS * b + 2 * v + g + 1)
                    at = (slice(None), u % 2, slice(4 * g, 4 * g + 4), slice((v % 2) * TOK, (v % 2 + 1) * TOK))
                    dve.tensor_tensor(pt[1][at], ps_t[:, g, :, :], pt[0][at], ALU.subtract).then_inc(t_lo, 1)

            def out_sum(u, b):
                dve.wait_ge(o_other, UNITS * b + u + 1)
                rows = slice(0, 64) if (u // PT_) % 2 == 0 else slice(64, P)
                cols = slice((u % PT_) * PAIR, (u % PT_ + 1) * PAIR)
                dve.tensor_tensor(ot_raw[rows, cols], ps_o[rows, u % 2, :], ot_other[rows, :],
                                  ALU.add).then_inc(o_sum, 1)

            def weights_of(c, b):
                dve.wait_ge(a_exp, SLOTS * b + PS * (c + 1))
                if c:
                    dve.wait_ge(p_wide, R_M * b + 2 * c)
                else:
                    dve.wait_ge(d_chosen, b + 1)
                own.step(dve.reciprocal(wgt[:, :, :], den[:, 2 * c:2 * c + 2, :]))
                dve.tensor_tensor(wgt[:, :, :], wgt[:, :, :], chosen[:, :, 2 * c:2 * c + 2].rearrange("p t j -> p j t"),
                                  ALU.mult).then_inc(d_wgt, 1)

            def item(m, b):
                slot, kind, arg = items[m]
                if kind in "kqv":
                    dve.wait_ge(m_act, ACT_M * b + count(READS_ACT, m + 1))
                    dve_item(dve, kind, arg, m_dve, (arg[0] + 1) % 2)
                elif kind == "r":
                    c, n = arg
                    dve.wait_ge(e_m, M * b + m + 1)
                    dve.wait_ge(o_sum, UNITS * b + 2 * PT_ * (c + 1))
                    if c:
                        dve.wait_ge(o_lo, R_M * b + 2 * (c - 1) + n + 1)
                    dve.tensor_tensor(ot[:, n, :], ot_raw[:, n * 512:(n + 1) * 512], ps_m[:, :],
                                      ALU.mult).then_inc(m_dve, 1)
                elif kind == "o":
                    dve.wait_ge(e_m, M * b + m + 1)
                    if arg == 0:
                        dve.wait_ge(xb_in, 16 * b + 16)
                    rows = xb[:, 2 * arg:2 * arg + 2, :]
                    dve.scalar_tensor_tensor(out=rows, in0=ps_m[:, :].rearrange("p (t d) -> p t d", t=2),
                                             scalar=gate, in1=rows, op0=ALU.mult, op1=ALU.add).then_inc(m_dve, 1)

            for q in range(PT_):
                ln_stats(q, q, q // 2 + 1)
            for i, (kind, arg) in enumerate(first_items):
                dve.wait_ge(pre_hi, i + 1)
                dve_item(dve, kind, arg, pre_dve, 0)
            dve.wait_ge(s_lower, 1)
            dve.sem_inc(batch_done, 1)

            def body(b):
                row_max(0, b)
                row_max(1, b)
                for v in range(SLOTS):
                    if v + 2 < SLOTS:
                        row_max(v + 2, b)
                    if v % 2 and v >= 3:
                        out_sum((v - 3) // 2, b)
                    if v - 1 in AT:
                        item(AT[v - 1], b)
                    prob_lo(v, b)
                    if v == 0:
                        choose(b)
                    if v in ln_at:
                        q = ln_at[v]
                        ln_stats(q, PT_ * b + PT_ + q, (b + 1) * (PT_ // 2) + q // 2 + 1)
                    if v % PS == PS - 1:
                        weights_of(v // PS, b)
                out_sum(UNITS - 1, b)
                for m in range(AT[SLOTS], M):
                    item(m, b)
                dve.wait_ge(m_dve, DVE_M * b + DVE_M)
                dve.sem_inc(batch_done, 1)

            batches(dve, body, own)


def ffn_weights(nc, fw, w, scales, s3, scale_src, s3_src, inexact, ident, tag):
    N = len(fw.src)
    RING = 4
    with semaphores(nc, tag) as sem, ExitStack() as ctx:
        stage = ctx.enter_context(nc.sbuf_tensor(f"{tag}_stage", [P, RING, WCH], F32))
        rest = ctx.enter_context(nc.sbuf_tensor(f"{tag}_rest", [P, 2, WCH], F32))
        worst = ctx.enter_context(nc.sbuf_tensor(f"{tag}_worst", [P, N + 1], F32))
        ps = ctx.enter_context(nc.psum_tensor(f"{tag}_ps", [P, 512], F32))
        loaded = [sem(f"loaded{i}") for i in range(RING)]
        small, rounded, diffed, worst_of, transposed = (sem(n) for n in (
            "small", "rounded", "diffed", "worst_of", "transposed"))
        block = ctx.enter_context(nc.Block())

        @block.sync
        def _(sp):
            for i, src in enumerate(fw.src):
                if i >= RING:
                    sp.wait_ge(diffed, i - RING + 1)
                sp.dma_start(stage[:, i % RING, :].rearrange("p (k n) -> p k n", n=src.shape[2]),
                             src).then_inc(loaded[i % RING], 16)
            for i, v in enumerate(scale_src):
                sp.dma_start(scales[:, i, :], v).then_inc(small, 16)
            sp.dma_start(s3[:, :], spread(s3_src.rearrange("(a n) -> a n", a=1), 0, P)).then_inc(small, 16)
            sp.wait_ge(small, 16 * (len(scale_src) + 1))

        @block.scalar
        def _(act):
            for i in range(N):
                act.wait_ge(loaded[i % RING], 16 * (i // RING + 1))
                act.activation(w[:, i * WCH:(i + 1) * WCH], stage[:, i % RING, :], ACT.Copy).then_inc(rounded, 1)

        @block.gpsimd
        def _(pool):
            for i in range(N):
                pool.wait_ge(rounded, i + 1)
                if i >= 2:
                    pool.wait_ge(worst_of, i - 1)
                pool.tensor_tensor(rest[:, i % 2, :], stage[:, i % RING, :], w[:, i * WCH:(i + 1) * WCH],
                                   ALU.subtract).then_inc(diffed, 1)

        @block.vector
        def _(dve):
            for i in range(N):
                dve.wait_ge(diffed, i + 1)
                dve.tensor_reduce(worst[:, i:i + 1], rest[:, i % 2, :], AX.X, ALU.max,
                                  apply_absolute_value=True).then_inc(worst_of, 1)
            dve.wait_ge(worst_of, N)
            dve.tensor_reduce(worst[:, N:N + 1], worst[:, 0:N], AX.X, ALU.max).then_inc(worst_of, 1)
            dve.wait_ge(transposed, 1)
            dve.tensor_reduce(inexact[0:1, 0:1], ps[0:1, 0:P], AX.X, ALU.max).then_inc(worst_of, 1)
            dve.wait_ge(worst_of, N + 2)

        @block.tensor
        def _(pe):
            pe.wait_ge(worst_of, N + 1)
            pe.transpose(ps[0:1, 0:P], worst[:, N:N + 1], ident[:, :]).then_inc(transposed, 1)


def load_full(nc, fw, w):
    with semaphores(nc, "G") as sem, nc.Block() as block:
        loaded = sem("full_loaded")

        @block.sync
        def _(sp):
            for i, src in enumerate(fw.src):
                sp.dma_start(w[:, i * WCH:(i + 1) * WCH].rearrange("p (k n) -> p k n", n=src.shape[2]),
                             src).then_inc(loaded, 16)
            sp.wait_ge(loaded, 16 * len(fw.src))


def ffn_either_way(nc, ident, gate, x_src, x_dst, t):
    fw = FfnWeights(*(t[f"L0_ffn_{n}T"] for n in ("w1_w", "w2_w", "h1_w", "h2_w", "w3_w")))
    scale_src = [t[f"L0_ffn_{n}_s"] for n in ("w1", "w2", "h1", "h2")]
    with ExitStack() as ctx:
        scales = ctx.enter_context(nc.sbuf_tensor("ffn_scales", [P, 4, fw.K["h1"]], F32))
        s3 = ctx.enter_context(nc.sbuf_tensor("ffn_s3", [P, D], F32))
        inexact = ctx.enter_context(nc.sbuf_tensor("ffn_inexact", [1, 1], F32))
        with nc.sbuf_tensor("ffn_w_rounded", [P, fw.cols], F32R) as w:
            ffn_weights(nc, fw, w, scales, s3, scale_src, t["L0_ffn_w3_s"], inexact, ident, "W")
            flag = nc.values_load(inexact[0:1, 0:1].bitcast(I32))
            with nc.If_eq(flag.val, 0):
                feed_forward(nc, ident, gate, x_src, x_dst, fw, w, scales, s3, True, "F")
        with nc.Else():
            with nc.sbuf_tensor("ffn_w_full", [P, fw.cols], F32) as w:
                load_full(nc, fw, w)
                feed_forward(nc, ident, gate, x_src, x_dst, fw, w, scales, s3, False, "G")


def constants(nc, ident, gates, g_xattn, g_ffn):
    with semaphores(nc, "S") as sem, nc.Block() as block:
        gates_in, tanh_done, ident_zero, ident_made = (sem(n) for n in (
            "gates_in", "tanh_done", "ident_zero", "ident_made"))

        @block.sync
        def _(sp):
            for i, g in enumerate((g_xattn, g_ffn)):
                sp.dma_start(gates[:, i, :], spread(g.rearrange("(a n) -> a n", a=1), 0, P)).then_inc(gates_in, 16)

        @block.scalar
        def _(act):
            act.wait_ge(gates_in, 32)
            act.activation(gates[:, :, :], gates[:, :, :], ACT.Tanh).then_inc(tanh_done, 1)
            act.wait_ge(tanh_done, 1)

        @block.gpsimd
        def _(pool):
            pool.memset(ident[:, :], 0.0).then_inc(ident_zero, 1)
            pool.wait_ge(ident_zero, 1)
            pool.affine_select(out=ident[:, :], in_=ident[:, :], compare_op=ALU.not_equal, fill=1.0,
                               base=0, pattern=[[-1, P]], channel_multiplier=1).then_inc(ident_made, 1)
            pool.wait_ge(ident_made, 1)


def gated_layers(nc, t, only=None):
    T = t["x"].shape[0]
    x1, x2, x3 = (nc.dram_tensor(f"x{i}", [T, D], F32, kind="Internal").ap() for i in range(1, 4))
    with ExitStack() as ctx:
        ident = ctx.enter_context(nc.sbuf_tensor("ident", [P, P], F32))
        gates = ctx.enter_context(nc.sbuf_tensor("gates", [P, 2, 2], F32))
        constants(nc, ident, gates, t["g_xattn"], t["g_ffn"])
        layers = [
            lambda src, dst: cross_attention(
                nc, ident, gates[:, 0, 0:1], src, dst, t["ctxT"],
                *(t[f"L0_xattn_{n}T"] for n in ("wq", "wk", "wv", "wo")),
                tuple(t[f"L0_xattn_{n}"] for n in ("bq", "bk", "bv", "bo")), None, 16, "A"),
            lambda src, dst: ffn_either_way(nc, ident, gates[:, 1, 0:1], src, dst, t),
            lambda src, dst: cross_attention(
                nc, ident, gates[:, 0, 1:2], src, dst, t["ctxT"],
                *(t[f"L1_xattn_{n}"] for n in ("Wq", "Wk", "Wv", "Wo")),
                None, (t["L1_xattn_ln_scale"], t["L1_xattn_ln_bias"]), 8, "C"),
            lambda src, dst: self_attention(
                nc, ident, gates[:, 1, 1:2], src, dst, *(t[f"L1_ffn_{n}"] for n in ("Wq", "Wk", "Wv", "Ws")),
                t["L1_ffn_Wo"].rearrange("h e d -> (h e) d"), t["L1_ffn_bo"], t["ctxT"].shape[0],
                t["L1_ffn_Ws"].shape[1], 3),
        ]
        if only is not None:
            layers[only](t["x"], t["out"])
            return
        for layer, src, dst in zip(layers, (t["x"], x1, x2, x3), (x1, x2, x3, t["out"])):
            layer(src, dst)


def laid_out(inputs):
    import numpy as np

    def cols(v):
        return v.reshape(-1, P).T

    a = {}
    for name, v in inputs.items():
        v = np.asarray(v)
        if name == "x":
            a[name] = v.reshape(-1, v.shape[-1])
        elif name == "ctx_1024":
            a["ctxT"] = v.transpose(0, 2, 1)
        elif name.startswith("L0_xattn_w") or (name.startswith("L0_ffn_") and name.endswith("_w")):
            a[name + "T"] = v.T
        elif name.endswith("Wkv"):
            half = v.shape[1] // 2
            a[name[:-3] + "Wk"], a[name[:-3] + "Wv"] = v[:, :half], v[:, half:]
        elif name in ("L0_xattn_bq", "L0_xattn_bk", "L1_xattn_ln_scale", "L1_xattn_ln_bias", "L0_ffn_w1_s",
                      "L0_ffn_w2_s", "L0_ffn_h1_s", "L0_ffn_h2_s"):
            a[name] = cols(v)
        else:
            a[name] = v
    return {name: np.ascontiguousarray(v) for name, v in a.items()}


def kernel(**inputs):
    import concourse.bacc as bacc
    from concourse.bass_utils import run_bass_kernel_spmd

    arrays = laid_out(inputs)
    nc = bacc.Bacc("TRN2", target_bir_lowering=False, num_devices=1)
    tensors = {n: nc.dram_tensor(f"in_{n}", list(v.shape), mybir.dt.from_np(v.dtype), kind="ExternalInput").ap()
               for n, v in arrays.items()}
    tensors["out"] = nc.dram_tensor("out_x", list(arrays["x"].shape), F32, kind="ExternalOutput").ap()
    gated_layers(nc, tensors)
    r = run_bass_kernel_spmd(nc, [{f"in_{n}": v for n, v in arrays.items()}], core_ids=[0])
    return r.results[0]["out_x"].reshape(inputs["x"].shape)
```

```python
from contextlib import ExitStack, contextmanager

import concourse.bass as bass
from concourse import mybir

F32 = mybir.dt.float32
F32R = mybir.dt.float32r
I32 = mybir.dt.int32
ALU = mybir.AluOpType
ACT = mybir.ActivationFunctionType
AX = mybir.AxisListType

P = 128
D = 256
DC = D // P
TOK = 128
PAIR = 2 * TOK
EPS = 1e-5
RSQRT_MAGIC = 0x5F3759DF


@contextmanager
def semaphores(nc, tag):
    made = []

    def sem(name):
        made.append(nc.alloc_semaphore(name=f"{tag}_{name}"))
        return made[-1]

    yield sem
    nc.clear_and_free_semaphores(made)
    nc.all_engine_barrier()


class Own:

    def __init__(self, eng, sem):
        self.eng, self.sem, self.n = eng, sem, 0

    def link(self, ins):
        ins.then_inc(self.sem, 1)
        self.n += 1

    def wait(self):
        self.eng.wait_ge(self.sem, self.n)

    def step(self, ins):
        self.link(ins)
        self.wait()

    def clear(self):
        if self.n:
            self.wait()
            self.eng.sem_clear(self.sem)
            self.n = 0


def spread(ap, dim, n):
    shape = list(ap.shape)
    shape[dim] = n
    return ap.broadcast_to(shape)


def split_passes(hi_lo_a, hi_lo_b):
    (ah, al), (bh, bl) = hi_lo_a, hi_lo_b
    return ((ah, bh), (ah, bl), (al, bh))


def rsqrt_guess(own, eng, var, v_eps, half, y):
    own.step(eng.tensor_scalar(v_eps, var, EPS, None, ALU.add))
    own.link(eng.tensor_scalar(half, v_eps, -0.5, None, ALU.mult))
    own.step(eng.tensor_scalar(y.bitcast(I32), v_eps.bitcast(I32), 1, None, ALU.logical_shift_right))


def newton(own, eng, half, y, t):
    for _ in range(3):
        own.step(eng.tensor_tensor(t, y, y, ALU.mult))
        own.step(eng.tensor_tensor(t, t, half, ALU.mult))
        own.step(eng.tensor_scalar(t, t, 1.5, None, ALU.add))
        own.step(eng.tensor_tensor(y, y, t, ALU.mult))


def cross_attention(nc, ident, gate, x_src, x_dst, ctxT, wqT, wkT, wvT, woT, bias, ln2, H, tag):
    B, _, S = ctxT.shape
    HD = wqT.shape[1]
    dh = HD // H
    C = HD // P
    HC = H // C
    G = H // 4
    S2 = S + S % 2
    SCALE = float(dh) ** -0.5
    NP = x_src.shape[0] // PAIR
    PB = NP // B
    TB = 2 * PB
    RING = 4
    MANY = H > 8
    Q_ON_DVE = C > 2
    AHEAD = 3 if ln2 else 2
    QW = C * PAIR
    xs = x_src.rearrange("(n t p) d -> n p t d", t=2, p=P)
    xd = x_dst.rearrange("(n t p) d -> n p t d", t=2, p=P)
    assert PB == RING and 4 * S <= 512 and H % 8 == 0

    with semaphores(nc, tag) as sem, ExitStack() as ctx:
        def sb(name, shape, dt=F32):
            return ctx.enter_context(nc.sbuf_tensor(f"{tag}_{name}", shape, dt))

        wq_raw = sb("wq_raw", [P, DC, HD])
        wq = [sb("wq_hi", [P, DC, HD], F32R), sb("wq_lo", [P, DC, HD], F32R)]
        wo_raw = sb("wo_raw", [P, C, D])
        wo = [sb("wo_hi", [P, C, D], F32R), sb("wo_lo", [P, C, D], F32R)]
        wk = sb("wk", [P, DC, HD])
        wv = sb("wv", [P, DC, HD])
        cx = sb("cx", [P, DC, S])
        one = sb("one", [P, 1])
        head_mask = sb("head_mask", [P, HC])
        qbias = sb("qbias", [P, C])
        kbias = sb("kbias", [P, C])
        vbias = sb("vbias", [S, HD])
        obias = sb("obias", [P, D])
        ln_sb = sb("ln_sb", [P, 2, DC])
        kt = sb("kt", [P, C, S])
        kt_part = [sb("kt_hi", [P, C, S], F32R), sb("kt_lo", [P, C, S], F32R)]
        kblk = [sb("kblk_hi", [P, C, HC, S], F32R), sb("kblk_lo", [P, C, HC, S], F32R)]
        vt = sb("vt", [S, HD])
        vpad = [sb("vpad_hi", [P, H * P + P], F32R), sb("vpad_lo", [P, H * P + P], F32R)]
        x = sb("x", [P, RING, 2, D])
        res = sb("res", [P, RING, 2, D])
        stats = sb("stats", [P, 4, 6])
        mv = sb("mv", [P, 2, 2, 2])
        rs = sb("rs", [P, 2, 4, 2])
        xn = sb("xn", [P, 2, 2, D])
        xt = sb("xt", [P, DC, PAIR])
        xt_part = [sb("xt_hi", [P, DC, PAIR], F32R), sb("xt_lo", [P, DC, PAIR], F32R)]
        qt = sb("qt", [P, C, PAIR])
        q_part = [sb("q_hi", [P, 2, C, PAIR], F32R), sb("q_lo", [P, 2, C, PAIR], F32R)]
        prob = sb("prob", [P, 2, H, S2])
        half_sum = sb("half_sum", [P, 2, H, S2 // 2])
        negmax = sb("negmax", [P, H])
        rsum = sb("rsum", [P, 2, 2, H])
        rwide = sb("rwide", [P, 2, HD])
        pt = [sb("pt_hi", [P, 2, H, PAIR], F32R), sb("pt_lo", [P, 2, H, PAIR], F32R)]
        ot = sb("ot", [P, C, PAIR])
        rt = sb("rt", [P, C, PAIR])
        o_part = [sb("o_hi", [P, C, PAIR], F32R), sb("o_lo", [P, C, PAIR], F32R)]

        ps_s = ctx.enter_context(nc.psum_tensor(f"{tag}_ps_s", [P, G, 512], F32))
        ps_t = ctx.enter_context(nc.psum_tensor(f"{tag}_ps_t", [P, 2, 512], F32))
        ps_o = ctx.enter_context(nc.psum_tensor(f"{tag}_ps_o", [P, C, PAIR], F32))
        ps_m = ctx.enter_context(nc.psum_tensor(f"{tag}_ps_m", [P, 512 * max(1, C // 2)], F32))

        def diag(v):
            step = P + dh
            return [v[0:S, c * HC * P:c * HC * P + HC * step].rearrange("s (j w) -> s j w", w=step)[:, :, 0:dh]
                    for c in range(C)]

        s_w = [sem(f"w{i}") for i in range(6)]
        s_small = sem("small")
        s_ctx = sem("ctx")
        x_in = [sem(f"x_in{i}") for i in range(RING)]
        r_in = [sem(f"r_in{i}") for i in range(RING)]
        x_out = [sem(f"x_out{i}") for i in range(RING)]
        s_const, s_zeros = sem("head_mask_made"), sem("vpad_zeroed")
        w_hi, w_lo, s_qb = sem("w_hi"), sem("w_lo"), sem("qb")
        stat, root_done, ln1, ln2_done = (sem(n) for n in ("stat", "root", "ln1", "ln2_done"))
        ln_done = ln2_done if ln2 else ln1
        e_xt, e_q, e_s, e_t, e_pv, e_rt, e_o, e_k, e_v = (sem(n) for n in (
            "pe_xt", "pe_q", "pe_s", "pe_t", "pe_pv", "pe_rt", "pe_o", "pe_k", "pe_v"))
        xt_raw, xt_hi, xt_lo = sem("xt_raw"), sem("s_xt_hi"), sem("s_xt_lo")
        qt_raw, q_hi, q_lo = sem("qt_raw"), sem("s_q_hi"), sem("s_q_lo")
        kt_raw, kt_hi, kt_lo, kb_hi, kb_lo = (sem(n) for n in ("s_kt", "s_kt_hi", "s_kt_lo", "s_kb_hi", "s_kb_lo"))
        vt_raw, v_hi, v_lo = sem("s_vt"), sem("s_v_hi"), sem("s_v_lo")
        d_sub, a_exp, d_r = sem("sub"), sem("exp"), sem("r")
        p_sum, r_biased = sem("p_sum"), sem("r_biased")
        t_hi, t_lo = sem("t_hi"), sem("t_lo")
        r_wide, rt_copied = sem("r_wide"), sem("rt_copied")
        o_raw, o_hi, o_lo, d_fin = sem("o_raw"), sem("s_o_hi"), sem("s_o_lo"), sem("fin")
        own_v, own_a, own_p = sem("own_v"), sem("own_a"), sem("own_p")

        def batches(eng, body, own=None):
            body(0, True)
            if own:
                own.clear()
            with eng.Fori(1, B) as b:
                body(b, False)
                if own:
                    own.clear()

        def q_low(eng, n, par):
            eng.wait_ge(q_hi, n + 1)
            eng.tensor_tensor(q_part[1][:, par, :, :], qt[:, :, :], q_part[0][:, par, :, :],
                              ALU.subtract).then_inc(q_lo, 1)

        block = ctx.enter_context(nc.Block())

        @block.sync
        def _(sp):
            def load_x(n, at):
                sp.dma_start(x[:, at % RING, :, :], xs[n]).then_inc(x_in[at % RING], 16)

            def load_ctx(b):
                sp.dma_start(cx[:, :, :], ctxT[b].rearrange("(c p) s -> p c s", p=P)).then_inc(s_ctx, 16)

            load_x(0, 0)
            load_ctx(0)
            for i, (dst, src) in enumerate(((wk, wkT), (wv, wvT), (wq_raw, wqT), (wo_raw, woT))):
                sp.dma_start(dst[:, :, :], src.rearrange("(c p) n -> p c n", p=P)).then_inc(s_w[i], 16)
            small = []
            if bias:
                bq, bk, bv, bo = bias
                small += [(qbias[:, :], bq),
                          (kbias[:, :], bk),
                          (vbias[:, :], spread(bv.rearrange("(a n) -> a n", a=1), 0, S)),
                          (obias[:, :], spread(bo.rearrange("(a n) -> a n", a=1), 0, P))]
            if ln2:
                small += [(ln_sb[:, i, :], v) for i, v in enumerate(ln2)]
            for dst, src in small:
                sp.dma_start(dst, src).then_inc(s_small, 16)
            for n in range(1, AHEAD + 1):
                load_x(n, n)

            def store(n, p):
                sp.wait_ge(d_fin, n + 1)
                sp.dma_start(xd[n], res[:, p % RING, :, :]).then_inc(x_out[p % RING], 16)

            def body(b, first, last=False):
                for p in range(PB):
                    n = PB * b + p
                    if p == 1:
                        sp.wait_ge(e_v, b + 1)
                        load_ctx(0 if last else b + 1)
                    if not first:
                        sp.wait_ge(x_out[p], 16 * b)
                    sp.dma_start(res[:, p, :, :], xs[n]).then_inc(r_in[p], 16)
                    m = p + AHEAD + 1
                    if not (first and m < RING):
                        sp.wait_ge(ln1, n + AHEAD - 2)
                    load_x(m - PB if last and m >= PB else n + AHEAD + 1, m)
                    if not (first and p < 2):
                        store(n - 2, p - 2)

            body(0, True)
            with sp.Fori(1, B - 1) as b:
                body(b, False)
            body(B - 1, False, True)
            for n in (NP - 2, NP - 1):
                store(n, n)
            for i in range(RING):
                sp.wait_ge(x_out[i], 16 * B)
                sp.wait_ge(x_in[i], 16 * len(range(i, NP + AHEAD + 1, RING)))

        @block.tensor
        def _(pe):
            def k_proj(b, t):
                pe.wait_ge(s_ctx, 16 * b + 16)
                for c in range(C):
                    for k in range(DC):
                        mm = pe.matmul(ps_m[:, c * S:(c + 1) * S], wk[:, k, c * P:(c + 1) * P], cx[:, k, :],
                                       start=k == 0, stop=k == DC - 1)
                mm.then_inc(e_k, 1)

            def v_proj():
                for k in range(DC):
                    mm = pe.matmul(ps_m[0:S, 0:HD], cx[:, k, :], wv[:, k, :], start=k == 0, stop=k == DC - 1)
                mm.then_inc(e_v, 1)

            def x_transpose(n, par):
                pe.wait_ge(ln_done, n + 1)
                for c in range(DC):
                    for t in range(2):
                        at = c * PAIR + t * TOK
                        mm = pe.transpose(ps_m[:, at:at + TOK], xn[:, par, t, c * P:(c + 1) * P], ident[:, :])
                mm.then_inc(e_xt, 1)

            def q_proj(n):
                pe.wait_ge(xt_hi, n + 1)
                pe.wait_ge(xt_lo, n + 1)
                for c in range(C):
                    i = 0
                    for k in range(DC):
                        for w, a in split_passes(wq, xt_part):
                            mm = pe.matmul(ps_m[:, c * PAIR:(c + 1) * PAIR], w[:, k, c * P:(c + 1) * P],
                                           a[:, k, :], start=i == 0, stop=i == 3 * DC - 1)
                            i += 1
                mm.then_inc(e_q, 1)

            def scores(n, t, T):
                par = (t // 2) % 2
                cols = slice((t % 2) * TOK, (t % 2) * TOK + TOK)
                for g in range(G):
                    per = min(HC, 4)
                    for j in range(4 // per):
                        h = 4 * g + j * per
                        c = h // HC
                        for i, (a, kk) in enumerate(split_passes(q_part, kblk)):
                            mm = pe.matmul(ps_s[:, g, j * per * S:(j + 1) * per * S], a[:, par, c, cols],
                                           kk[:, c, h % HC:h % HC + per, :],
                                           start=i == 0, stop=i == 2)
                mm.then_inc(e_s, 1)

            def p_transpose(T, t, half):
                pe.wait_ge(a_exp, T + 1)
                for g in range(G // 2 * half, G // 2 * (half + 1)):
                    u = G * T + g
                    if not (isinstance(u, int) and u < 2):
                        pe.wait_ge(t_lo, u - 1)
                    for j in range(4):
                        mm = pe.transpose(ps_t[0:S, g % 2, j * TOK:(j + 1) * TOK],
                                          prob[:, t % 2, 4 * g + j, 0:S], ident[:, :])
                    mm.then_inc(e_t, 1)

            def pv(n, par, part):
                if part == 0:
                    pe.wait_ge(t_lo, G * (2 * n + 1) + G // 2)
                elif part == 2:
                    pe.wait_ge(t_lo, G * (2 * n + 2))
                for h in range(H // 4 * part, H // 4 * (part + 1)):
                    c, j = divmod(h, HC)
                    for i, (v, a) in enumerate(split_passes(vpad, pt)):
                        mm = pe.matmul(ps_o[:, c, :], v[:, h * P:(h + 1) * P], a[:, par, h, :],
                                       start=j == 0 and i == 0, stop=j == HC - 1 and i == 2)
                if part == 3:
                    mm.then_inc(e_pv, 1)

            def r_transpose(n):
                pe.wait_ge(r_wide, 2 * n + 2)
                for c in range(C):
                    for t in range(2):
                        at = c * PAIR + t * TOK
                        mm = pe.transpose(ps_m[:, at:at + TOK], rwide[:, t, c * P:(c + 1) * P], ident[:, :])
                mm.then_inc(e_rt, 1)

            def out_proj(n):
                pe.wait_ge(o_hi, n + 1)
                pe.wait_ge(o_lo, n + 1)
                for t in range(2):
                    i = 0
                    for c in range(C):
                        for a, w in split_passes(o_part, wo):
                            mm = pe.matmul(ps_m[:, t * D:(t + 1) * D], a[:, c, t * TOK:(t + 1) * TOK],
                                           w[:, c, :], start=i == 0, stop=i == 3 * C - 1)
                            i += 1
                mm.then_inc(e_o, 1)

            pe.wait_ge(s_w[0], 16)
            k_proj(0, 0)
            pe.wait_ge(kt_raw, 1)
            pe.wait_ge(s_w[1], 16)
            v_proj()
            pe.wait_ge(vt_raw, 1)
            x_transpose(0, 0)
            pe.wait_ge(xt_raw, 1)
            pe.wait_ge(w_hi, 2)
            pe.wait_ge(w_lo, 2)
            q_proj(0)

            def body(b, first):
                for p in range(PB):
                    n = PB * b + p
                    T = 2 * n
                    one_before, two_before = not first or p >= 1, not first or p >= 2
                    if one_before:
                        p_transpose(T - 1, 1, 0)
                    if p == 0:
                        pe.wait_ge(kb_hi, b + 1)
                        pe.wait_ge(kb_lo, b + 1)
                    pe.wait_ge(q_hi, n + 1)
                    pe.wait_ge(q_lo, n + 1)
                    if one_before:
                        pe.wait_ge(d_sub, T)
                    scores(n, 2 * p, T)
                    if p == 1 and not first:
                        pe.wait_ge(vt_raw, b + 1)
                    elif two_before:
                        pe.wait_ge(rt_copied, n - 1)
                    else:
                        pe.wait_ge(qt_raw, n + 1)
                    x_transpose(n + 1, (p + 1) % 2)
                    if one_before:
                        if two_before:
                            pe.wait_ge(o_raw, n - 1)
                        if p == 1:
                            pe.wait_ge(v_hi, b + 1)
                            pe.wait_ge(v_lo, b + 1)
                        pv(n - 1, (p - 1) % 2, 0)
                        p_transpose(T - 1, 1, 1)
                    if p == PB - 1:
                        pe.wait_ge(xt_raw, n + 2)
                        k_proj(b + 1, n)
                    if one_before:
                        pv(n - 1, (p - 1) % 2, 1)
                    if two_before:
                        if p == PB - 1:
                            pe.wait_ge(kt_raw, b + 2)
                        else:
                            pe.wait_ge(xt_raw, n + 2)
                        out_proj(n - 2)
                    p_transpose(T, 0, 0)
                    pe.wait_ge(d_sub, T + 1)
                    scores(n, 2 * p + 1, T + 1)
                    if two_before:
                        pe.wait_ge(d_fin, n - 1)
                    else:
                        pe.wait_ge(xt_raw, n + 2)
                    q_proj(n + 1)
                    if one_before:
                        pv(n - 1, (p - 1) % 2, 2)
                    p_transpose(T, 0, 1)
                    if one_before:
                        pe.wait_ge(qt_raw, n + 2)
                        r_transpose(n - 1)
                        pv(n - 1, (p - 1) % 2, 3)
                    if p == 0 and not first:
                        pe.wait_ge(rt_copied, n)
                        v_proj()

            batches(pe, body)
            n = NP
            p_transpose(2 * n - 1, 1, 0)
            pe.wait_ge(o_raw, n - 1)
            pv(n - 1, (n - 1) % 2, 0)
            p_transpose(2 * n - 1, 1, 1)
            pv(n - 1, (n - 1) % 2, 1)
            pe.wait_ge(rt_copied, n - 1)
            out_proj(n - 2)
            pv(n - 1, (n - 1) % 2, 2)
            pe.wait_ge(d_fin, n - 1)
            r_transpose(n - 1)
            pv(n - 1, (n - 1) % 2, 3)
            pe.wait_ge(rt_copied, n)
            out_proj(n - 1)

        @block.scalar
        def _(act):
            own = Own(act, own_a)

            def x_parts(n):
                act.wait_ge(e_xt, n + 1)
                if not (isinstance(n, int) and n == 0):
                    act.wait_ge(xt_lo, n)
                for c in range(DC):
                    src = ps_m[:, c * PAIR:(c + 1) * PAIR]
                    if ln2:
                        ins = act.activation(xt[:, c, :], src, ACT.Identity, bias=ln_sb[:, 1, c:c + 1],
                                             scale=ln_sb[:, 0, c:c + 1])
                    else:
                        ins = act.activation(xt[:, c, :], src, ACT.Copy)
                ins.then_inc(xt_raw, 1)
                act.wait_ge(xt_raw, n + 1)
                if not (isinstance(n, int) and n == 0):
                    act.wait_ge(e_q, n)
                act.activation(xt_part[0][:, :, :], xt[:, :, :], ACT.Copy).then_inc(xt_hi, 1)

            def q_parts(n, par):
                act.wait_ge(e_q, n + 1)
                if not (isinstance(n, int) and n == 0):
                    act.wait_ge(q_lo, n)
                for c in range(C):
                    src = ps_m[:, c * PAIR:(c + 1) * PAIR]
                    if bias:
                        ins = act.activation(qt[:, c, :], src, ACT.Identity, bias=qbias[:, c:c + 1], scale=SCALE)
                    else:
                        ins = act.activation(qt[:, c, :], src, ACT.Copy, scale=SCALE)
                ins.then_inc(qt_raw, 1)
                act.wait_ge(qt_raw, n + 1)
                act.activation(q_part[0][:, par, :, :], qt[:, :, :], ACT.Copy).then_inc(q_hi, 1)

            def k_parts(b):
                act.wait_ge(e_k, b + 1)
                if not (isinstance(b, int) and b == 0):
                    act.wait_ge(kt_lo, b)
                    act.wait_ge(kb_hi, b)
                for c in range(C):
                    src = ps_m[:, c * S:(c + 1) * S]
                    if bias:
                        ins = act.activation(kt[:, c, :], src, ACT.Identity, bias=kbias[:, c:c + 1], scale=1.0)
                    else:
                        ins = act.activation(kt[:, c, :], src, ACT.Copy)
                ins.then_inc(kt_raw, 1)
                act.wait_ge(kt_raw, b + 1)
                act.activation(kt_part[0][:, :, :], kt[:, :, :], ACT.Copy).then_inc(kt_hi, 1)

            def v_parts(b, n):
                act.wait_ge(vt_raw, b + 1)
                if n is not None:
                    act.wait_ge(e_pv, n)
                for c, dst in enumerate(diag(vpad[0])):
                    ins = act.activation(dst, vt[:, c * P:(c + 1) * P].rearrange("s (j w) -> s j w", w=dh), ACT.Copy)
                ins.then_inc(v_hi, 1)

            def prob_hi(T, par, t, half):
                for g in range(G // 2 * half, G // 2 * (half + 1)):
                    act.wait_ge(e_t, G * T + g + 1)
                    dst = pt[0][0:S, par, 4 * g:4 * g + 4, t * TOK:(t + 1) * TOK]
                    act.activation(dst, ps_t[0:S, g % 2, :].rearrange("s (h q) -> s h q", h=4),
                                   ACT.Copy).then_inc(t_hi, 1)

            def exp(T, t):
                act.wait_ge(d_sub, T + 1)
                act.activation(prob[:, t, :, 0:S], prob[:, t, :, 0:S], ACT.Exp).then_inc(a_exp, 1)

            def rt_copy(n):
                act.wait_ge(e_rt, n + 1)
                if not (isinstance(n, int) and n == 0):
                    act.wait_ge(o_raw, n)
                act.activation(rt[:, :, :], ps_m[:, 0:QW].rearrange("p (c q) -> p c q", c=C),
                               ACT.Copy).then_inc(rt_copied, 1)

            def out_hi(n):
                act.wait_ge(o_raw, n + 1)
                if not (isinstance(n, int) and n == 0):
                    act.wait_ge(e_o, n)
                act.activation(o_part[0][:, :, :], ot[:, :, :], ACT.Copy).then_inc(o_hi, 1)

            if small_n := 16 * ((4 if bias else 0) + (2 if ln2 else 0)):
                act.wait_ge(s_small, small_n)
            if bias:
                own.step(act.activation(qbias[:, :], qbias[:, :], ACT.Copy, scale=SCALE))
            k_parts(0)
            act.wait_ge(s_zeros, 2)
            v_parts(0, None)
            for i, (hi, raw) in enumerate(((wq, wq_raw), (wo, wo_raw))):
                act.wait_ge(s_w[2 + i], 16)
                act.activation(hi[0][:, :, :], raw[:, :, :], ACT.Copy).then_inc(w_hi, 1)
            x_parts(0)
            q_parts(0, 0)

            def body(b, first):
                for p in range(PB):
                    n = PB * b + p
                    T = 2 * n
                    one_before, two_before = not first or p >= 1, not first or p >= 2
                    if one_before:
                        if not first or p >= 3:
                            act.wait_ge(e_pv, n - 2)
                        prob_hi(T - 1, (p - 1) % 2, 1, 0)
                    if two_before:
                        out_hi(n - 2)
                    x_parts(n + 1)
                    if one_before:
                        prob_hi(T - 1, (p - 1) % 2, 1, 1)
                    if p == PB - 1:
                        k_parts(b + 1)
                    exp(T, 0)
                    if two_before:
                        act.wait_ge(e_pv, n - 1)
                    prob_hi(T, p % 2, 0, 0)
                    if not MANY:
                        exp(T + 1, 1)
                    q_parts(n + 1, (p + 1) % 2)
                    prob_hi(T, p % 2, 0, 1)
                    if one_before:
                        rt_copy(n - 1)
                    if MANY:
                        exp(T + 1, 1)
                    if p == 0 and not first:
                        v_parts(b, n)

            own.clear()
            batches(act, body, own)
            n = NP
            prob_hi(2 * n - 1, (n - 1) % 2, 1, 0)
            out_hi(n - 2)
            prob_hi(2 * n - 1, (n - 1) % 2, 1, 1)
            rt_copy(n - 1)
            out_hi(n - 1)

        @block.gpsimd
        def _(pool):
            own = Own(pool, own_p)
            own.link(pool.memset(one[:, :], 1.0))
            own.step(pool.memset(head_mask[:, :], 1.0))
            own.step(pool.affine_select(out=head_mask[:, :], in_=head_mask[:, :], compare_op=ALU.is_ge, fill=0.0,
                                        base=0, pattern=[[-dh, HC]], channel_multiplier=1))
            pool.affine_select(out=head_mask[:, :], in_=head_mask[:, :], compare_op=ALU.is_ge, fill=0.0,
                               base=dh - 1, pattern=[[dh, HC]], channel_multiplier=-1).then_inc(s_const, 1)

            def root(n, par):
                pool.wait_ge(stat, n + 1)
                at = slice(0, 2) if ln2 else slice(par, par + 1)
                newton(own, pool, rs[:, at, 1, :], rs[:, at, 2, :], rs[:, at, 3, :])
                pool.sem_inc(root_done, 1)

            def x_low(n):
                pool.wait_ge(xt_hi, n + 1)
                pool.tensor_tensor(xt_part[1][:, :, :], xt[:, :, :], xt_part[0][:, :, :],
                                   ALU.subtract).then_inc(xt_lo, 1)

            def o_low(n):
                pool.wait_ge(o_hi, n + 1)
                if not (isinstance(n, int) and n == 0):
                    pool.wait_ge(e_o, n)
                pool.tensor_tensor(o_part[1][:, :, :], ot[:, :, :], o_part[0][:, :, :],
                                   ALU.subtract).then_inc(o_lo, 1)

            def widen(n, par, t):
                pool.wait_ge(d_r, 2 * n + t + 1)
                if not (isinstance(n, int) and n == 0):
                    pool.wait_ge(e_rt, n)
                pool.tensor_tensor(rwide[:, t, :].rearrange("p (h w) -> p h w", w=dh),
                                   spread(rsum[:, par, t, :].unsqueeze(2), 2, dh),
                                   one[:, :].unsqueeze(2).broadcast_to([P, H, dh]), ALU.mult).then_inc(r_wide, 1)

            def k_low(b):
                pool.wait_ge(kt_hi, b + 1)
                if not (isinstance(b, int) and b == 0):
                    pool.wait_ge(kb_lo, b)
                pool.tensor_tensor(kt_part[1][:, :, :], kt[:, :, :], kt_part[0][:, :, :],
                                   ALU.subtract).then_inc(kt_lo, 1)

            def k_block_low(b, T):
                pool.wait_ge(kt_lo, b + 1)
                if T is not None:
                    pool.wait_ge(e_s, T)
                for c in range(C):
                    ins = pool.tensor_tensor(kblk[1][:, c, :, :], spread(kt_part[1][:, c, :].unsqueeze(1), 1, HC),
                                             spread(head_mask[:, :].unsqueeze(2), 2, S), ALU.mult)
                ins.then_inc(kb_lo, 1)

            def fold(T, t):
                if MANY:
                    pool.wait_ge(a_exp, T + 1)
                    if not (isinstance(T, int) and T < 2):
                        pool.wait_ge(d_r, T - 1)
                    pool.tensor_tensor(half_sum[:, t, :, :], prob[:, t, :, 0:S2 // 2], prob[:, t, :, S2 // 2:S2],
                                       ALU.add).then_inc(p_sum, 1)

            def add_bias(n, at, times):
                if bias:
                    pool.wait_ge(r_in[at], 16 * times)
                    pool.tensor_tensor(res[:, at, :, :], res[:, at, :, :], spread(obias[:, :].unsqueeze(1), 1, 2),
                                       ALU.add).then_inc(r_biased, 1)

            def v_low(b):
                pool.wait_ge(v_hi, b + 1)
                for c, (hi, lo) in enumerate(zip(diag(vpad[0]), diag(vpad[1]))):
                    ins = pool.tensor_tensor(lo, vt[:, c * P:(c + 1) * P].rearrange("s (j w) -> s j w", w=dh),
                                             hi, ALU.subtract)
                ins.then_inc(v_lo, 1)

            pool.wait_ge(s_const, 1)
            root(0, 0)
            k_low(0)
            k_block_low(0, None)
            v_low(0)
            root(1, 1)
            x_low(0)
            if not Q_ON_DVE:
                q_low(pool, 0, 0)
            if ln2:
                root(2, 0)

            def body(b, first):
                for p in range(PB):
                    n = PB * b + p
                    T = 2 * n
                    one_before, two_before = not first or p >= 1, not first or p >= 2
                    if two_before:
                        o_low(n - 2)
                    if one_before:
                        widen(n - 1, (p - 1) % 2, 0)
                        fold(T - 1, 1)
                    x_low(n + 1)
                    if one_before:
                        widen(n - 1, (p - 1) % 2, 1)
                    root(n + AHEAD, (p + AHEAD) % 2)
                    if p == PB - 1:
                        k_low(b + 1)
                    fold(T, 0)
                    if not Q_ON_DVE:
                        q_low(pool, n + 1, (p + 1) % 2)
                    if p == PB - 1:
                        k_block_low(b + 1, 2 * n + 2)
                    if p == 0 and not first:
                        v_low(b)
                    if one_before:
                        add_bias(n - 1, (p - 1) % RING, b + (1 if p else 0))

            if bias:
                pool.wait_ge(s_small, 16 * 4)
                own.step(pool.tensor_scalar(obias[:, :], obias[:, :], gate, None, ALU.mult))
            own.clear()
            batches(pool, body, own)
            o_low(NP - 2)
            widen(NP - 1, (NP - 1) % 2, 0)
            fold(2 * NP - 1, 1)
            widen(NP - 1, (NP - 1) % 2, 1)
            add_bias(NP - 1, RING - 1, B)
            o_low(NP - 1)

        @block.vector
        def _(dve):
            own = Own(dve, own_v)

            def ln_stats(n, par, at, times, second=True):
                dve.wait_ge(x_in[at], 16 * times)
                second = second and ln2
                sources = [(x[:, at, :, :], par)]
                if second:
                    dve.wait_ge(ln1, n)
                    sources.append((xn[:, 1 - par, :, :], 1 - par))
                if not (isinstance(n, int) and n < 2):
                    dve.wait_ge(ln_done, n - 1)
                for i, (src, _) in enumerate(sources):
                    for t in range(2):
                        own.link(dve.bn_stats(stats[:, 2 * i + t, :], src[:, t, :]))
                own.wait()
                for i, (_, q) in enumerate(sources):
                    for t in range(2):
                        own.link(dve.bn_aggr(mv[:, q, t, :], stats[:, 2 * i + t, :]))
                own.wait()
                q = slice(0, 2) if second else slice(par, par + 1)
                rsqrt_guess(own, dve, mv[:, q, :, 1], rs[:, q, 0, :], rs[:, q, 1, :], rs[:, q, 2, :])
                dve.tensor_scalar(rs[:, q, 2, :].bitcast(I32), rs[:, q, 2, :].bitcast(I32), -1, RSQRT_MAGIC,
                                  ALU.mult, ALU.add).then_inc(stat, 1)

            def layer_norm(n, par, src, done):
                for t in range(2):
                    ins = dve.tensor_scalar(xn[:, par, t, :], src[:, t, :], mv[:, par, t, 0:1],
                                            rs[:, par, 2, t:t + 1], ALU.subtract, ALU.mult)
                ins.then_inc(done, 1)

            def layer_norm_1(n, par, at):
                dve.wait_ge(root_done, n + 1)
                if not (isinstance(n, int) and n < 2):
                    dve.wait_ge(e_xt, n - 1)
                layer_norm(n, par, x[:, at, :, :], ln1)

            def layer_norm_2(n, par):
                if ln2:
                    dve.wait_ge(root_done, n + 2)
                    layer_norm(n, par, xn[:, par, :, :], ln2_done)

            def v_bias(b):
                dve.wait_ge(e_v, b + 1)
                if not (isinstance(b, int) and b == 0):
                    dve.wait_ge(v_lo, b)
                if bias:
                    dve.tensor_tensor(vt[:, :], ps_m[0:S, 0:HD], vbias[:, :], ALU.add).then_inc(vt_raw, 1)
                else:
                    dve.tensor_copy(vt[:, :], ps_m[0:S, 0:HD]).then_inc(vt_raw, 1)

            def k_block(b, T):
                dve.wait_ge(kt_hi, b + 1)
                if T is not None:
                    dve.wait_ge(e_s, T)
                for c in range(C):
                    ins = dve.tensor_tensor(kblk[0][:, c, :, :], spread(kt_part[0][:, c, :].unsqueeze(1), 1, HC),
                                            spread(head_mask[:, :].unsqueeze(2), 2, S), ALU.mult)
                ins.then_inc(kb_hi, 1)

            sc = ps_s[:, :, 0:4 * S].rearrange("p g (h s) -> p g h s", h=4)

            def shift(T, t):
                dve.wait_ge(e_s, T + 1)
                own.step(dve.tensor_reduce(negmax[:, :].rearrange("p (g h) -> p g h", h=4), sc, AX.X, ALU.max,
                                           negate=True))
                if not (isinstance(T, int) and T < 2):
                    dve.wait_ge(e_t, G * (T - 1))
                dve.tensor_tensor(prob[:, t, :, 0:S].rearrange("p (g h) s -> p g h s", h=4), sc,
                                  spread(negmax[:, :].rearrange("p (g h) -> p g h", h=4).unsqueeze(3), 3, S),
                                  ALU.add).then_inc(d_sub, 1)

            def prob_lo(T, par, t, half):
                for g in range(G // 2 * half, G // 2 * (half + 1)):
                    dve.wait_ge(t_hi, G * T + g + 1)
                    cols = slice(t * TOK, (t + 1) * TOK)
                    dve.tensor_tensor(pt[1][0:S, par, 4 * g:4 * g + 4, cols],
                                      ps_t[0:S, g % 2, :].rearrange("s (h q) -> s h q", h=4),
                                      pt[0][0:S, par, 4 * g:4 * g + 4, cols], ALU.subtract).then_inc(t_lo, 1)

            def recip_sum(T, par, t):
                if MANY:
                    dve.wait_ge(p_sum, T + 1)
                else:
                    dve.wait_ge(a_exp, T + 1)
                own.step(dve.tensor_reduce(rsum[:, par, t, :], half_sum[:, t, :, :] if MANY else prob[:, t, :, 0:S],
                                           AX.X, ALU.add))
                dve.reciprocal(rsum[:, par, t, :], rsum[:, par, t, :]).then_inc(d_r, 1)

            def normalize(n):
                dve.wait_ge(e_pv, n + 1)
                dve.wait_ge(rt_copied, n + 1)
                if not (isinstance(n, int) and n == 0):
                    dve.wait_ge(o_lo, n)
                dve.tensor_tensor(ot[:, :, :], ps_o[:, :, :], rt[:, :, :], ALU.mult).then_inc(o_raw, 1)

            def residual(n, at, times):
                dve.wait_ge(e_o, n + 1)
                if bias:
                    dve.wait_ge(r_biased, n + 1)
                else:
                    dve.wait_ge(r_in[at], 16 * times)
                src = ps_m[:, 0:2 * D].rearrange("p (t d) -> p t d", t=2)
                dve.scalar_tensor_tensor(out=res[:, at, :, :], in0=src, scalar=gate, in1=res[:, at, :, :],
                                         op0=ALU.mult, op1=ALU.add).then_inc(d_fin, 1)

            own.link(dve.memset(rs[:, :, :, :], 1.0))
            own.link(dve.memset(vpad[0][:, :].bitcast(F32), 0.0))
            own.link(dve.memset(vpad[1][:, :].bitcast(F32), 0.0))
            own.wait()
            dve.sem_inc(s_zeros, 1)
            ln_stats(0, 0, 0, 1, second=False)
            own.link(dve.memset(prob[:, :, :, S:S2], 0.0))
            for part in pt:
                own.link(dve.memset(part[S // 32 * 32:P, :, :, :].bitcast(F32), 0.0))
            own.wait()
            dve.sem_inc(s_zeros, 1)
            layer_norm_1(0, 0, 0)
            dve.wait_ge(s_const, 1)
            k_block(0, None)
            if bias:
                dve.wait_ge(s_small, 16 * 4)
            v_bias(0)
            ln_stats(1, 1, 1, 1)
            layer_norm_2(0, 0)
            for i, (part, raw) in enumerate(((wq, wq_raw), (wo, wo_raw))):
                dve.wait_ge(w_hi, i + 1)
                dve.tensor_tensor(part[1][:, :, :], raw[:, :, :], part[0][:, :, :], ALU.subtract).then_inc(w_lo, 1)
            layer_norm_1(1, 1, 1)
            if Q_ON_DVE:
                q_low(dve, 0, 0)
            if ln2:
                ln_stats(2, 0, 2, 1)
                layer_norm_1(2, 0, 2)

            def body(b, first):
                for p in range(PB):
                    n = PB * b + p
                    T = 2 * n
                    m = p + AHEAD
                    one_before, two_before = not first or p >= 1, not first or p >= 2
                    layer_norm_2(n + 1, (p + 1) % 2)
                    if two_before:
                        normalize(n - 2)
                    if one_before:
                        if not first or p >= 3:
                            dve.wait_ge(e_pv, n - 2)
                        prob_lo(T - 1, (p - 1) % 2, 1, 0)
                    shift(T, 0)
                    if one_before and MANY:
                        recip_sum(T - 1, (p - 1) % 2, 1)
                    if one_before:
                        prob_lo(T - 1, (p - 1) % 2, 1, 1)
                    if not MANY:
                        recip_sum(T, p % 2, 0)
                    ln_stats(n + AHEAD, m % 2, m % RING, b + 1 + m // RING)
                    if two_before:
                        residual(n - 2, (p - 2) % RING, b + p // 2)
                        dve.wait_ge(e_pv, n - 1)
                    prob_lo(T, p % 2, 0, 0)
                    shift(T + 1, 1)
                    if MANY:
                        recip_sum(T, p % 2, 0)
                    if p == PB - 1:
                        k_block(b + 1, 2 * n + 2)
                    if Q_ON_DVE:
                        q_low(dve, n + 1, (p + 1) % 2)
                    prob_lo(T, p % 2, 0, 1)
                    layer_norm_1(n + AHEAD, m % 2, m % RING)
                    if not MANY:
                        recip_sum(T + 1, p % 2, 1)
                    if p == 0 and not first:
                        v_bias(b)

            own.clear()
            batches(dve, body, own)
            n = NP
            normalize(n - 2)
            if MANY:
                recip_sum(2 * n - 1, (n - 1) % 2, 1)
            prob_lo(2 * n - 1, (n - 1) % 2, 1, 0)
            prob_lo(2 * n - 1, (n - 1) % 2, 1, 1)
            residual(n - 2, RING - 2, B)
            normalize(n - 1)
            residual(n - 1, RING - 1, B)


WCH = 1024


class FfnWeights:

    def __init__(self, w1T, w2T, h1T, h2T, w3T):
        self.K = {"w1": w1T.shape[0] // P, "w2": w2T.shape[0] // P, "h1": h1T.shape[0] // P,
                  "h2": h2T.shape[0] // P, "w3": w3T.shape[0] // P}
        self.src = []
        self.at = {}
        col = 0
        for name, w in (("w1", w1T), ("w2", w2T), ("h1", h1T), ("h2", h2T), ("w3", w3T)):
            self.at[name] = (col, w.shape[1])
            per = WCH // w.shape[1]
            for k in range(0, self.K[name], per):
                self.src.append(w[k * P:(k + per) * P, :].rearrange("(k p) n -> p k n", p=P))
            col += self.K[name] * w.shape[1]
        self.cols = col
        assert col == WCH * len(self.src)

    def chunk(self, w, name, k, a, b):
        at, width = self.at[name]
        return w[:, at + k * width + a:at + k * width + b]


def feed_forward(nc, ident, gate, x_src, x_dst, fw, w, scales, s3, exact, tag):
    BT = 4
    BLK = BT * TOK
    NB = x_src.shape[0] // BLK
    HC = fw.K["h1"]
    XR = 2
    xs = x_src.rearrange("(n t p) d -> n p t d", t=BT, p=P)
    xd = x_dst.rearrange("(n t p) d -> n p t d", t=BT, p=P)
    ADT = F32R if exact else F32
    PARTS = 2 if exact else 1
    U = 2 * HC

    with semaphores(nc, tag) as sem, ExitStack() as ctx:
        def sb(name, shape, dt=F32):
            return ctx.enter_context(nc.sbuf_tensor(f"{tag}_{name}", shape, dt))

        x = sb("x", [P, XR, BT, D])
        stats = sb("stats", [P, BT, 6])
        mv = sb("mv", [P, BT, 2])
        rs = sb("rs", [P, 4, BT])
        xn = sb("xn", [P, BT, D])
        xt = sb("xt", [P, DC, BLK]) if exact else None
        xt_part = [sb(f"xt_part{i}", [P, DC, BLK], ADT) for i in range(PARTS)]
        silu = sb("silu", [P, 2, BLK])
        raw = sb("raw", [P, 2, BLK]) if exact else None
        ha = [sb(f"ha{i}", [P, HC, BLK], ADT) for i in range(PARTS)]
        hb = [sb(f"hb{i}", [P, HC, BLK], ADT) for i in range(PARTS)]
        y = sb("y", [P, 2, 2, D])
        ps = ctx.enter_context(nc.psum_tensor(f"{tag}_ps", [P, 4, 512], F32))
        ps_x = ctx.enter_context(nc.psum_tensor(f"{tag}_ps_x", [P, DC, BLK], F32))
        ps_y = ctx.enter_context(nc.psum_tensor(f"{tag}_ps_y", [P, BT, D], F32))

        x_in = [sem(f"x_in{i}") for i in range(XR)]
        x_out = [sem(f"x_out{i}") for i in range(XR)]
        stat, ln, e_xt, xt_raw, xt_hi, xt_lo = (sem(n) for n in ("stat", "ln", "pe_xt", "xt_raw", "s_xt_hi", "s_xt_lo"))
        e_a, a_silu, a_raw, a_hi, a_lo = (sem(n) for n in ("pe_a", "a_silu", "a_raw", "a_hi", "a_lo"))
        e_u, u_raw, u_hi, u_lo = (sem(n) for n in ("pe_u", "u_raw", "u_hi", "u_lo"))
        e_y, d_y = sem("pe_y"), sem("y_done")
        own_v, own_a, own_p = sem("own_v"), sem("own_a"), sem("own_p")
        if not exact:
            xt_lo, a_lo, u_lo = xt_raw, a_raw, u_raw

        def blocks(eng, body, own=None, end=NB // XR):
            def pair(i, first):
                for u in range(XR):
                    body(XR * i + u, u, i, first and u == 0)
                if own:
                    own.clear()

            pair(0, True)
            with eng.Fori(1, end) as i:
                pair(i, False)

        block = ctx.enter_context(nc.Block())

        @block.sync
        def _(sp):
            def load(b, at):
                sp.dma_start(x[:, at, :, :], xs[b]).then_inc(x_in[at], 16)

            def body(b, u, i, first, ahead=None):
                if not first:
                    sp.wait_ge(x_out[1 - u], 16 * (i + u))
                load(b + 1 if ahead is None else ahead, 1 - u)
                sp.wait_ge(d_y, 2 * b + 2)
                sp.dma_start(xd[b], x[:, u, :, :]).then_inc(x_out[u], 16)

            load(0, 0)
            blocks(sp, body, end=NB // XR - 1)
            i = NB // XR - 1
            body(NB - 2, 0, i, False)
            body(NB - 1, 1, i, False, ahead=0)
            for u in range(XR):
                sp.wait_ge(x_out[u], 16 * (NB // XR))

        @block.tensor
        def _(pe):
            def x_transpose(b):
                pe.wait_ge(ln, b + 1)
                for c in range(DC):
                    for t in range(BT):
                        mm = pe.transpose(ps_x[:, c, t * TOK:(t + 1) * TOK], xn[:, t, c * P:(c + 1) * P], ident[:, :])
                mm.then_inc(e_xt, 1)

            def product(out, name, j, parts, ready=None):
                K = fw.K[name]
                for k in range(K):
                    if ready is not None:
                        for s, v in ready(k):
                            pe.wait_ge(s, v)
                    for i, a in enumerate(parts):
                        mm = pe.matmul(out, fw.chunk(w, name, k, j * P, (j + 1) * P), a[:, k, :],
                                       start=k == 0 and i == 0, stop=k == K - 1 and i == len(parts) - 1)
                return mm

            pe.wait_ge(ln, 1)
            x_transpose(0)

            def body(b, u_, i_, first):
                for j in range(HC):
                    if j == 0:
                        pe.wait_ge(xt_hi if exact else xt_raw, b + 1)
                        pe.wait_ge(xt_lo, b + 1)
                    if j >= 2:
                        pe.wait_ge(a_raw, HC * b + j - 1)
                    elif not first:
                        pe.wait_ge(u_raw, U * b)
                    product(ps[:, 2 * (j % 2), :], "w1", j, xt_part)
                    product(ps[:, 2 * (j % 2) + 1, :], "w2", j, xt_part).then_inc(e_a, 1)
                for u in range(U):
                    if u < 4:
                        pe.wait_ge(a_raw, HC * b + HC - 1 + u // 2)
                    else:
                        pe.wait_ge(u_raw, U * b + u - 3)
                    if u < HC:
                        ready = (lambda k: ((a_hi if exact else a_raw, HC * b + k + 1), (a_lo, HC * b + k + 1)))
                        product(ps[:, u % 4, :], "h1", u, ha, ready if u == 0 else None).then_inc(e_u, 1)
                    else:
                        ready = (lambda k: ((u_hi if exact else u_raw, U * b + k + 1), (u_lo, U * b + k + 1)))
                        product(ps[:, u % 4, :], "h2", u - HC, hb, ready if u == HC else None).then_inc(e_u, 1)
                pe.wait_ge(xt_raw, b + 1)
                x_transpose(b + 1)
                for half in range(2):
                    if half == 0 and not first:
                        pe.wait_ge(d_y, 2 * b)
                    for t in range(2 * half, 2 * half + 2):
                        for k in range(HC):
                            if t == 0:
                                pe.wait_ge(u_hi if exact else u_raw, U * b + HC + k + 1)
                                pe.wait_ge(u_lo, U * b + HC + k + 1)
                            for i, a in enumerate(ha):
                                mm = pe.matmul(ps_y[:, t, :], a[:, k, t * TOK:(t + 1) * TOK],
                                               fw.chunk(w, "w3", k, 0, D), start=k == 0 and i == 0,
                                               stop=k == HC - 1 and i == PARTS - 1)
                    mm.then_inc(e_y, 1)

            blocks(pe, body)

        @block.scalar
        def _(act):
            own = Own(act, own_a)

            def x_out_of_psum(b):
                act.wait_ge(e_xt, b + 1)
                if exact:
                    if not (isinstance(b, int) and b == 0):
                        act.wait_ge(xt_lo, b)
                    act.activation(xt[:, :, :], ps_x[:, :, :], ACT.Copy).then_inc(xt_raw, 1)
                    act.wait_ge(xt_raw, b + 1)
                    act.activation(xt_part[0][:, :, :], xt[:, :, :], ACT.Copy).then_inc(xt_hi, 1)
                else:
                    act.activation(xt_part[0][:, :, :], ps_x[:, :, :], ACT.Copy).then_inc(xt_raw, 1)

            def a_high(b, j):
                if exact:
                    act.wait_ge(a_raw, HC * b + j + 1)
                    act.activation(ha[0][:, j, :], raw[:, j % 2, :], ACT.Copy).then_inc(a_hi, 1)

            x_out_of_psum(0)

            def body(b, u_, i_, first):
                for j in range(HC):
                    act.wait_ge(e_a, HC * b + j + 1)
                    if not (first and j < 2):
                        act.wait_ge(a_raw, HC * b + j - 1)
                    act.activation(silu[:, j % 2, :], ps[:, 2 * (j % 2), :], ACT.Silu,
                                   scale=scales[:, 0, j:j + 1]).then_inc(a_silu, 1)
                    if j:
                        a_high(b, j - 1)
                a_high(b, HC - 1)
                for u in range(U):
                    act.wait_ge(e_u, U * b + u + 1)
                    dst = (hb if u < HC else ha)[0][:, u % HC, :]
                    scale = scales[:, 2 + u // HC, u % HC:u % HC + 1]
                    if not exact:
                        act.activation(dst, ps[:, u % 4, :], ACT.Gelu, scale=scale).then_inc(u_raw, 1)
                        continue
                    if u < 2:
                        act.wait_ge(a_lo, HC * b + HC - 1 + u)
                    else:
                        act.wait_ge(u_lo, U * b + u - 1)
                    act.activation(raw[:, u % 2, :], ps[:, u % 4, :], ACT.Gelu, scale=scale).then_inc(u_raw, 1)
                    act.wait_ge(u_raw, U * b + u + 1)
                    act.activation(dst, raw[:, u % 2, :], ACT.Copy).then_inc(u_hi, 1)
                x_out_of_psum(b + 1)

            blocks(act, body, own)

        @block.gpsimd
        def _(pool):
            own = Own(pool, own_p)

            def layer_norm(b, at):
                pool.wait_ge(stat, b + 1)
                if not (isinstance(b, int) and b == 0):
                    pool.wait_ge(e_xt, b)
                newton(own, pool, rs[:, 1, :], rs[:, 2, :], rs[:, 3, :])
                for t in range(BT):
                    ins = pool.tensor_scalar(xn[:, t, :], x[:, at, t, :], mv[:, t, 0:1], rs[:, 2, t:t + 1],
                                             ALU.subtract, ALU.mult)
                ins.then_inc(ln, 1)

            def x_low(b):
                if exact:
                    pool.wait_ge(xt_hi, b + 1)
                    pool.tensor_tensor(xt_part[1][:, :, :], xt[:, :, :], xt_part[0][:, :, :],
                                       ALU.subtract).then_inc(xt_lo, 1)

            layer_norm(0, 0)
            x_low(0)

            def body(b, u, i, first):
                layer_norm(b + 1, 1 - u)
                x_low(b + 1)

            own.clear()
            blocks(pool, body, own)

        @block.vector
        def _(dve):
            own = Own(dve, own_v)

            def ln_stats(b, at, times):
                dve.wait_ge(x_in[at], 16 * times)
                if not (isinstance(b, int) and b == 0):
                    dve.wait_ge(ln, b)
                for t in range(BT):
                    own.link(dve.bn_stats(stats[:, t, :], x[:, at, t, :]))
                own.wait()
                for t in range(BT):
                    own.link(dve.bn_aggr(mv[:, t, :], stats[:, t, :]))
                own.wait()
                rsqrt_guess(own, dve, mv[:, :, 1], rs[:, 0, :], rs[:, 1, :], rs[:, 2, :])
                dve.tensor_scalar(rs[:, 2, :].bitcast(I32), rs[:, 2, :].bitcast(I32), -1, RSQRT_MAGIC,
                                  ALU.mult, ALU.add).then_inc(stat, 1)

            def a_low(b, j):
                if exact:
                    dve.wait_ge(a_hi, HC * b + j + 1)
                    dve.tensor_tensor(ha[1][:, j, :], raw[:, j % 2, :], ha[0][:, j, :],
                                      ALU.subtract).then_inc(a_lo, 1)

            ln_stats(0, 0, 1)

            def body(b, u_, i, first):
                for j in range(HC):
                    if j >= 2 or not first:
                        if exact and j >= 2:
                            dve.wait_ge(a_lo, HC * b + j - 1)
                    dve.wait_ge(a_silu, HC * b + j + 1)
                    dst = raw[:, j % 2, :] if exact else ha[0][:, j, :]
                    dve.scalar_tensor_tensor(out=dst, in0=ps[:, 2 * (j % 2) + 1, :], scalar=scales[:, 1, j:j + 1],
                                             in1=silu[:, j % 2, :], op0=ALU.mult, op1=ALU.mult).then_inc(a_raw, 1)
                    if j:
                        a_low(b, j - 1)
                a_low(b, HC - 1)
                for u in range(U):
                    if exact:
                        dve.wait_ge(u_hi, U * b + u + 1)
                        dst = (hb if u < HC else ha)[1][:, u % HC, :]
                        hi = (hb if u < HC else ha)[0][:, u % HC, :]
                        dve.tensor_tensor(dst, raw[:, u % 2, :], hi, ALU.subtract).then_inc(u_lo, 1)
                    if u == HC // 2:
                        ln_stats(b + 1, 1 - u_, i + 1 if u_ == 0 else i + 2)
                for half in range(2):
                    t = slice(2 * half, 2 * half + 2)
                    dve.wait_ge(e_y, 2 * b + half + 1)
                    if not first:
                        dve.wait_ge(d_y, 2 * b + half - 1)
                    own.step(dve.tensor_tensor(y[:, half, :, :], ps_y[:, t, :], spread(s3[:, :].unsqueeze(1), 1, 2), ALU.mult))
                    dve.scalar_tensor_tensor(out=x[:, u_, t, :], in0=y[:, half, :, :], scalar=gate, in1=x[:, u_, t, :],
                                             op0=ALU.mult, op1=ALU.add).then_inc(d_y, 1)

            own.clear()
            blocks(dve, body, own)


def self_attention(nc, ident, gate, x_src, x_dst, wq_src, wk_src, wv_src, ws_src, wo_src, bo_src, B, H, topk):
    N = x_src.shape[0] // B
    NT = N // TOK
    KC = N // P
    HD = wq_src.shape[1]
    dh = HD // H
    CP = H // 2
    PT_ = NT // 2
    SLOTS = H * NT
    UNITS = SLOTS // 2
    PS = 2 * NT
    SCALE = float(dh) ** -0.5
    assert dh == 64 and N == 1024 and DC == 2

    xb_src = x_src.rearrange("(b t p) d -> b p t d", b=B, p=P)
    xb_dst = x_dst.rearrange("(b t p) d -> b p t d", b=B, p=P)
    xp_src = x_src.rearrange("(b q t p) d -> b q p t d", b=B, t=2, p=P)

    items = []
    for c in range(CP):
        s = PS * c
        if c:
            items += [(s + 1, "r", (c - 1, 0)), (s + 2, "r", (c - 1, 1))]
        items += [(s + 5, "k", (c, 0)), (s + 6, "k", (c, 1))]
        items += [(s + 7 + i, "q", (c, i // 2, i % 2)) for i in range(4)]
        items += [(s + 11, "v", (c, 0)), (s + 12, "v", (c, 1))]
    items += [(2, "h", 0), (3, "h", 1), (13, "x", 0), (14, "g", 0), (15, "x", 1), (PS + 4, "g", 1),
              (PS + 13, "x", 2), (PS + 14, "g", 2), (PS + 15, "x", 3), (2 * PS + 4, "g", 3)]
    items.sort(key=lambda i: i[0])
    items += [(SLOTS + i, "r", (CP - 1, i)) for i in range(2)] + [(SLOTS + 2 + i, "o", i) for i in range(PT_)]
    AT = {}
    for m, (slot, _, _) in enumerate(items):
        assert slot not in AT
        AT[slot] = m
    M = len(items)
    READS_ACT = ("k", "q", "v", "x", "g", "h")
    READS_DVE = ("k", "q", "v", "r", "o")
    ln_at = {1: 0, 8: 1, PS + 1: 2, PS + 8: 3}

    def count(kinds, m):
        return sum(kind in kinds for _, kind, _ in items[:m])

    ACT_M, DVE_M = count(READS_ACT, M), count(READS_DVE, M)
    R_M = 2 * CP

    with semaphores(nc, "E") as sem, ExitStack() as ctx:
        def sb(name, shape, dt=F32):
            return ctx.enter_context(nc.sbuf_tensor(f"E_{name}", shape, dt))

        xp = sb("xp", [P, 2, 2, D])
        stats = sb("stats", [P, 2, 6])
        mv = sb("mv", [P, 2, 2, 2])
        rs = sb("rs", [P, 2, 4, 2])
        xn = sb("xn", [P, 2, 2, D])
        xt = sb("xt", [P, DC, N])
        xb = xt[:, :, :].rearrange("p k n -> p (k n)").rearrange("p (t d) -> p t d", d=D)
        xt_part = [sb("xt_hi", [P, DC, N], F32R), sb("xt_lo", [P, DC, N], F32R)]
        w_raw = sb("w_raw", [P, 3, DC, P])
        wq = [sb("wq_hi", [P, DC, 2, P], F32R), sb("wq_lo", [P, DC, 2, P], F32R)]
        wk = [sb("wk_hi", [P, DC, P], F32R), sb("wk_lo", [P, DC, P], F32R)]
        wv = [sb("wv_hi", [P, DC, P], F32R), sb("wv_lo", [P, DC, P], F32R)]
        wo = [sb("wo_hi", [P, CP, D], F32R), sb("wo_lo", [P, CP, D], F32R)]
        ws = sb("ws", [P, DC, H])
        bo = sb("bo", [H, D])
        kk = sb("kk", [P, 2, 2, N], F32R)
        qq = [sb("q_hi", [P, 2, 2, N], F32R), sb("q_lo", [P, 2, 2, N], F32R)]
        vv = sb("vv", [P, 2, KC, 2, P], F32R)
        prob = sb("prob", [P, 2, N])
        pt = [sb("pt_hi", [P, 2, KC, PAIR], F32R), sb("pt_lo", [P, 2, KC, PAIR], F32R)]
        negmax = sb("negmax", [P, 4])
        den = sb("den", [P, H, NT])
        wgt = sb("wgt", [P, 2, NT])
        wwide = sb("wwide", [P, 2, NT // 2, P])
        ot_other = sb("ot_other", [P, PAIR])
        ot_raw = sb("ot_raw", [P, N])
        wo_raw = ot_raw[:, :].rearrange("p (c d) -> p c d", d=D)
        ot = sb("ot", [P, 2, 512])
        o_part = [sb("o_hi", [P, CP, N], F32R), sb("o_lo", [P, CP, N], F32R)]
        logit = sb("logit", [P, NT, H])
        score = sb("score", [P, NT, H])
        before, equal = (wwide[:, :, :, :].rearrange("p n t w -> p (n t w)")[:, i * NT * H * H:(i + 1) * NT * H * H]
                         .rearrange("p (t i j) -> p t i j", i=H, j=H) for i in range(2))
        rank = sb("rank", [P, NT, H])
        one = sb("one", [P, 1])
        lower = sb("lower", [P, H, H])
        chosen = sb("chosen", [P, NT, H])
        chosenT = sb("chosenT", [H, NT, TOK])

        ps_s = ctx.enter_context(nc.psum_tensor("E_ps_s", [P, 2, N], F32))
        ps_t = ctx.enter_context(nc.psum_tensor("E_ps_t", [P, 2, 4, TOK], F32))
        ps_o = ctx.enter_context(nc.psum_tensor("E_ps_o", [P, 2, PAIR], F32))
        ps_m = ctx.enter_context(nc.psum_tensor("E_ps_m", [P, 512], F32))

        w_in, xb_in, xb_out, small = sem("w_in"), sem("xb_in"), sem("xb_out"), sem("small")
        wo_in, xb_free = sem("wo_in"), sem("xb_free")
        xp_in = [sem("xp_in0"), sem("xp_in1")]
        w_hi, w_lo, wo_hi, wo_lo = sem("s_w_hi"), sem("s_w_lo"), sem("s_wo_hi"), sem("s_wo_lo")
        stat, ln = sem("stat"), sem("ln")
        c_hi, c_lo = sem("convert_hi"), sem("convert_lo")
        e_s, e_t, e_pv, e_m = sem("pe_s"), sem("pe_t"), sem("pe_pv"), sem("pe_item")
        m_act, m_dve = sem("item_act"), sem("item_dve")
        d_max, a_exp, t_hi, t_lo = sem("max"), sem("exp"), sem("t_hi"), sem("t_lo")
        o_other, o_sum, d_wgt, p_wide = sem("o_other"), sem("o_sum"), sem("wgt"), sem("wide")
        o_hi, o_lo = sem("s_o_hi"), sem("s_o_lo")
        a_gate, d_chosen, e_chosenT, a_chosenT, s_lower = (sem(n) for n in (
            "a_gate", "chosen_done", "pe_chosenT", "a_chosenT", "lower_made"))
        batch_done = sem("batch_done")
        pre_pe, pre_act, pre_hi, pre_dve = sem("pre_pe"), sem("pre_act"), sem("pre_hi"), sem("pre_dve")
        own_v, own_a, own_p = sem("own_v"), sem("own_a"), sem("own_p")

        def batches(eng, body, own=None, waits=True):
            if own:
                own.clear()
            with eng.Fori(0, B) as b:
                if waits:
                    eng.wait_ge(batch_done, b + 1)
                body(b)
                if own:
                    own.clear()

        def head(v):
            return v // NT

        def r_item(c, n):
            return AT[(PS * (c + 1) + 1 if c < CP - 1 else SLOTS) + n]

        def at_x(q):
            return [m for m, (_, kind, arg) in enumerate(items) if kind == "x" and arg == q][0]

        first_items = ([("k", (n,)) for n in range(2)] + [("q", (j, n)) for j in range(2) for n in range(2)]
                       + [("v", (n,)) for n in range(2)])

        block = ctx.enter_context(nc.Block())

        @block.sync
        def _(sp):
            def load_w(c):
                for i, w in enumerate((wq_src, wk_src, wv_src)):
                    sp.dma_start(w_raw[:, i, :, :], w[:, c * P:(c + 1) * P].rearrange("(k p) n -> p k n", p=P)
                                 ).then_inc(w_in, 16)

            def load_xp(b, q):
                sp.dma_start(xp[:, q % 2, :, :], xp_src[b, q]).then_inc(xp_in[q % 2], 16)

            for q in range(2):
                load_xp(0, q)
            load_w(0)
            sp.dma_start(ws[:, :, :], ws_src.rearrange("(k p) n -> p k n", p=P)).then_inc(small, 16)
            sp.dma_start(bo[:, :], bo_src).then_inc(small, 16)
            for q in range(2, PT_):
                sp.wait_ge(ln, q - 1)
                load_xp(0, q)
            sp.dma_start(wo_raw, wo_src.rearrange("(c p) n -> p c n", p=P)).then_inc(wo_in, 16)

            def body(b, ahead):
                sp.wait_ge(batch_done, b + 1)
                for c in range(CP):
                    sp.wait_ge(w_lo, CP * b + c + 1)
                    load_w((c + 1) % CP)
                    if c < 2:
                        for q in (2 * c, 2 * c + 1):
                            sp.wait_ge(ln, PT_ * b + PT_ + q - 1)
                            load_xp(ahead, q)
                sp.wait_ge(c_lo, PT_ * b + 2 * PT_)
                sp.dma_start(xb, xb_src[b]).then_inc(xb_in, 16)
                for q in range(PT_):
                    sp.wait_ge(m_dve, DVE_M * b + DVE_M - PT_ + q + 1)
                    sp.dma_start(xb_dst[b][:, 2 * q:2 * q + 2, :], xb[:, 2 * q:2 * q + 2, :]).then_inc(xb_out, 16)
                sp.wait_ge(xb_out, 16 * PT_ * b + 16 * PT_)
                sp.sem_inc(xb_free, 1)

            sp.sem_inc(xb_free, 1)
            with sp.Fori(0, B - 1) as b:
                body(b, b + 1)
            body(B - 1, 0)

        @block.tensor
        def _(pe):
            def item(m, b):
                slot, kind, arg = items[m]
                if m:
                    prev = items[m - 1][1]
                    if prev in READS_DVE:
                        pe.wait_ge(m_dve, DVE_M * b + count(READS_DVE, m))
                    else:
                        pe.wait_ge(m_act, ACT_M * b + count(READS_ACT, m))
                run(kind, arg, b).then_inc(e_m, 1)

            def run(kind, arg, b):
                if kind in "kqv":
                    c = arg[0]
                    if arg[1:] in ((0,), (0, 0)) and kind == "k":
                        pe.wait_ge(w_hi, CP * b + c + 2)
                        pe.wait_ge(w_lo, CP * b + c + 2)
                        if c == CP - 1:
                            pe.wait_ge(c_hi, PT_ * b + 2 * PT_)
                            pe.wait_ge(c_lo, PT_ * b + 2 * PT_)
                    return {"k": k_proj, "q": q_proj, "v": v_proj}[kind](*arg[1:])
                if kind == "x":
                    return x_transpose(arg, PT_ * b + PT_ + arg + 1)
                if kind == "g":
                    return logits(arg)
                if kind == "h":
                    pe.wait_ge(d_chosen, b + 1)
                    for t in range(4):
                        mm = pe.transpose(ps_m[0:H, t * TOK:(t + 1) * TOK], chosen[:, 4 * arg + t, :], ident[:, :])
                    return mm
                if kind == "r":
                    c, n = arg
                    pe.wait_ge(p_wide, R_M * b + 2 * c + n + 1)
                    for t in range(4):
                        mm = pe.transpose(ps_m[:, t * TOK:(t + 1) * TOK], wwide[:, n, t, :], ident[:, :])
                    return mm
                if arg == 0:
                    pe.wait_ge(o_hi, R_M * b + R_M)
                    pe.wait_ge(o_lo, R_M * b + R_M)
                for t in range(2):
                    tile = 2 * arg + t
                    cols = slice(tile * TOK, (tile + 1) * TOK)
                    out = ps_m[:, t * D:(t + 1) * D]
                    pe.matmul(out, chosenT[:, tile, :], bo[:, :], start=True, stop=False)
                    i = 0
                    for c in range(CP):
                        for a, w in split_passes(o_part, wo):
                            i += 1
                            mm = pe.matmul(out, a[:, c, cols], w[:, c, :], start=False, stop=i == 3 * CP)
                return mm

            def x_transpose(q, done):
                pe.wait_ge(ln, done)
                for k in range(DC):
                    for t in range(2):
                        at = k * PAIR + t * TOK
                        mm = pe.transpose(ps_m[:, at:at + TOK], xn[:, q % 2, t, k * P:(k + 1) * P], ident[:, :])
                return mm

            def logits(q):
                for t in range(2):
                    for k in range(DC):
                        cols = slice((2 * q + t) * TOK, (2 * q + t + 1) * TOK)
                        mm = pe.matmul(ps_m[:, t * H:(t + 1) * H], xt[:, k, cols], ws[:, k, :],
                                       start=k == 0, stop=k == DC - 1)
                return mm

            def k_proj(n):
                for i, (k, (w, a)) in enumerate((k, x) for k in range(DC) for x in split_passes(wk, xt_part)):
                    mm = pe.matmul(ps_m[:, :], w[:, k, :], a[:, k, n * 512:(n + 1) * 512], start=i == 0,
                                   stop=i == 3 * DC - 1)
                return mm

            def q_proj(j, n):
                for i, (k, (w, a)) in enumerate((k, x) for k in range(DC) for x in split_passes(wq, xt_part)):
                    mm = pe.matmul(ps_m[:, :], w[:, k, j, :], a[:, k, n * 512:(n + 1) * 512], start=i == 0,
                                   stop=i == 3 * DC - 1)
                return mm

            def v_proj(n):
                for t in range(4):
                    cols = slice((4 * n + t) * TOK, (4 * n + t + 1) * TOK)
                    for i, (k, (a, w)) in enumerate((k, x) for k in range(DC) for x in split_passes(xt_part, wv)):
                        mm = pe.matmul(ps_m[:, t * P:(t + 1) * P], a[:, k, cols], w[:, k, :], start=i == 0,
                                       stop=i == 3 * DC - 1)
                return mm

            def scores(v):
                j, cp, cols = head(v) % 2, (head(v) // 2) % 2, slice((v % NT) * TOK, (v % NT + 1) * TOK)
                for n in range(2):
                    for i in range(2):
                        mm = pe.matmul(ps_s[:, v % 2, n * 512:(n + 1) * 512], qq[i][:, cp, j, cols],
                                       kk[:, cp, j, n * 512:(n + 1) * 512], start=i == 0, stop=i == 1)
                mm.then_inc(e_s, 1)

            def p_transpose(v, b):
                for g in range(2):
                    if v:
                        pe.wait_ge(t_lo, 2 * SLOTS * b + 2 * (v - 1) + g + 1)
                    for i in range(4):
                        at = (4 * g + i) * P
                        mm = pe.transpose(ps_t[:, g, i, :], prob[:, v % 2, at:at + P], ident[:, :])
                    mm.then_inc(e_t, 1)

            def pv(u, b):
                h = u // PT_
                pe.wait_ge(t_lo, 2 * SLOTS * b + 4 * (u + 1))
                if u >= 2:
                    pe.wait_ge(o_sum, UNITS * b + u - 1)
                for i in range(KC):
                    for n, a in enumerate(pt):
                        mm = pe.matmul(ps_o[:, u % 2, :], vv[:, (h // 2) % 2, i, h % 2, :], a[:, u % 2, i, :],
                                       start=i == 0 and n == 0, stop=i == KC - 1 and n == 1)
                mm.then_inc(e_pv, 1)

            for q in range(PT_):
                if q:
                    pe.wait_ge(pre_act, 2 * q)
                x_transpose(q, q + 1).then_inc(pre_pe, 1)
                pe.wait_ge(pre_act, 2 * q + 1)
                if q == 0:
                    pe.wait_ge(small, 32)
                logits(q).then_inc(pre_pe, 1)
            pe.wait_ge(pre_act, 2 * PT_)
            pe.wait_ge(w_hi, 1)
            pe.wait_ge(w_lo, 1)
            pe.wait_ge(c_hi, PT_)
            pe.wait_ge(c_lo, PT_)
            for i, (f, arg) in enumerate(first_items):
                if i:
                    pe.wait_ge(pre_dve, i)
                {"k": k_proj, "q": q_proj, "v": v_proj}[f](*arg).then_inc(pre_pe, 1)

            def ready(v, b):
                if v % PS == 0 and v:
                    m = AT[v - PS + 10] + 1
                    pe.wait_ge(m_dve, DVE_M * b + count(READS_DVE, m))

            def body(b):
                scores(0)
                scores(1)
                for v in range(SLOTS):
                    pe.wait_ge(a_exp, SLOTS * b + v + 1)
                    if v + 2 < SLOTS:
                        ready(v + 2, b)
                        scores(v + 2)
                    p_transpose(v, b)
                    if v % 2 == 0 and v:
                        u = v // 2 - 1
                        if u % (2 * PT_) == 0 and u:
                            m = AT[2 * u - PS + 12] + 1
                            pe.wait_ge(m_dve, DVE_M * b + count(READS_DVE, m))
                        pv(u, b)
                    if v in AT:
                        item(AT[v], b)
                pv(UNITS - 1, b)
                for m in range(AT[SLOTS], M):
                    item(m, b)

            pe.wait_ge(pre_dve, len(first_items))
            pe.wait_ge(wo_hi, 1)
            pe.wait_ge(wo_lo, 1)
            batches(pe, body)

        def act_item(act, kind, arg, ready, done, par):
            ready()
            if kind == "k":
                cols = slice(arg[-1] * 512, arg[-1] * 512 + 512)
                act.activation(kk[0:64, par, 0, cols], ps_m[0:64, :], ACT.Copy)
                ins = act.activation(kk[64:P, par, 1, cols], ps_m[64:P, :], ACT.Copy)
            elif kind == "q":
                j, n = arg[-2:]
                ins = act.activation(qq[0][:, par, j, n * 512:(n + 1) * 512], ps_m[:, :], ACT.Copy, scale=SCALE)
            elif kind == "v":
                n = arg[-1]
                ins = act.activation(vv[:, par, 4 * n:4 * n + 4, :, 0:dh],
                                     ps_m[:, :].rearrange("p (t j w) -> p t j w", t=4, j=2), ACT.Copy)
            elif kind == "x":
                ins = act.activation(xt[:, :, arg * PAIR:(arg + 1) * PAIR],
                                     ps_m[:, :].rearrange("p (k q) -> p k q", k=DC), ACT.Copy)
            elif kind == "h":
                ins = act.activation(chosenT[:, 4 * arg:4 * arg + 4, :],
                                     ps_m[0:H, :].rearrange("h (t q) -> h t q", t=4), ACT.Copy)
            else:
                ins = act.activation(logit[:, 2 * arg:2 * arg + 2, :],
                                     ps_m[:, 0:2 * H].rearrange("p (t h) -> p t h", t=2), ACT.Copy)
            ins.then_inc(done, 1)

        def dve_item(dve, kind, arg, done, par):
            if kind == "k":
                cols = slice(arg[-1] * 512, arg[-1] * 512 + 512)
                dve.tensor_tensor(kk[64:P, par, 0, cols], ps_m[0:64, :], kk[0:64, par, 0, cols], ALU.subtract)
                ins = dve.tensor_tensor(kk[0:64, par, 1, cols], ps_m[64:P, :], kk[64:P, par, 1, cols], ALU.subtract)
            elif kind == "q":
                j, n = arg[-2:]
                cols = slice(n * 512, (n + 1) * 512)
                ins = dve.scalar_tensor_tensor(out=qq[1][:, par, j, cols], in0=ps_m[:, :], scalar=SCALE,
                                               in1=qq[0][:, par, j, cols], op0=ALU.mult, op1=ALU.subtract)
            else:
                n = arg[-1]
                ins = dve.tensor_tensor(vv[:, par, 4 * n:4 * n + 4, :, dh:P],
                                        ps_m[:, :].rearrange("p (t j w) -> p t j w", t=4, j=2),
                                        vv[:, par, 4 * n:4 * n + 4, :, 0:dh], ALU.subtract)
            ins.then_inc(done, 1)

        @block.scalar
        def _(act):
            own = Own(act, own_a)

            def split_weights(n):
                act.wait_ge(w_in, 48 * n)
                for k in range(DC):
                    act.activation(wq[0][:, k, :, :].rearrange("p j (r w) -> p j r w", r=2),
                                   spread(w_raw[:, 0, k, :].rearrange("p (j w) -> p j w", j=2).unsqueeze(2), 2, 2),
                                   ACT.Copy)
                act.activation(wk[0][:, :, :], w_raw[:, 1, :, :], ACT.Copy)
                act.activation(wv[0][:, :, :], w_raw[:, 2, :, :], ACT.Copy).then_inc(w_hi, 1)

            def convert(q):
                cols = slice(q * PAIR, (q + 1) * PAIR)
                act.activation(xt_part[0][:, :, cols], xt[:, :, cols], ACT.Copy).then_inc(c_hi, 1)

            def exp(v, b):
                act.wait_ge(d_max, SLOTS * b + v + 1)
                if v >= 2:
                    act.wait_ge(e_t, 2 * SLOTS * b + 2 * (v - 1))
                act.activation(prob[:, v % 2, :], ps_s[:, v % 2, :], ACT.Exp, bias=negmax[:, v % 4:v % 4 + 1],
                               scale=1.0, accum_out=den[:, head(v), v % NT:v % NT + 1]).then_inc(a_exp, 1)

            def prob_hi(v, b):
                u = v // 2
                if u >= 2 and v % 2 == 0:
                    act.wait_ge(e_pv, UNITS * b + u - 1)
                for g in range(2):
                    act.wait_ge(e_t, 2 * SLOTS * b + 2 * v + g + 1)
                    act.activation(pt[0][:, u % 2, 4 * g:4 * g + 4, (v % 2) * TOK:(v % 2 + 1) * TOK],
                                   ps_t[:, g, :, :], ACT.Copy).then_inc(t_hi, 1)

            def other_half(u, b):
                act.wait_ge(e_pv, UNITS * b + u + 1)
                if u:
                    act.wait_ge(o_sum, UNITS * b + u)
                if (u // PT_) % 2 == 0:
                    ins = act.activation(ot_other[0:64, :], ps_o[64:P, u % 2, :], ACT.Copy)
                else:
                    ins = act.activation(ot_other[64:P, :], ps_o[0:64, u % 2, :], ACT.Copy)
                ins.then_inc(o_other, 1)

            def out_hi(c, n, b):
                act.wait_ge(m_dve, DVE_M * b + count(READS_DVE, r_item(c, n) + 1))
                act.activation(o_part[0][:, c, n * 512:(n + 1) * 512], ot[:, n, :], ACT.Copy).then_inc(o_hi, 1)

            def item(m, b):
                slot, kind, arg = items[m]
                if kind in READS_ACT:
                    c = arg[0] if kind in "kqv" else 0
                    if kind == "x" and arg == 0:
                        act.wait_ge(xb_free, b + 1)
                    act_item(act, kind, arg, lambda: act.wait_ge(e_m, M * b + m + 1), m_act, (c + 1) % 2)
                elif kind == "r":
                    out_hi(*arg, b)

            split_weights(1)
            for q in range(PT_):
                act_item(act, "x", q, lambda: act.wait_ge(pre_pe, 2 * q + 1), pre_act, 0)
                act.wait_ge(pre_act, 2 * q + 1)
                convert(q)
                act_item(act, "g", q, lambda: act.wait_ge(pre_pe, 2 * q + 2), pre_act, 0)
            for i, (kind, arg) in enumerate(first_items):
                act_item(act, kind, arg, lambda: act.wait_ge(pre_pe, 2 * PT_ + i + 1), pre_hi, 0)
            act.wait_ge(wo_in, 16)
            act.activation(wo[0][:, :, :], wo_raw, ACT.Copy).then_inc(wo_hi, 1)

            def body(b):
                act.activation(score[:, :, :], logit[:, :, :], ACT.Exp, scale=-1.0).then_inc(a_gate, 1)
                exp(0, b)
                exp(1, b)
                for v in range(SLOTS):
                    if v % 2 and v >= 3:
                        other_half((v - 3) // 2, b)
                    if v - 1 in AT:
                        item(AT[v - 1], b)
                    if v % PS == 1:
                        split_weights(CP * b + v // PS + 2)
                    if v == (CP - 1) * PS:
                        act.wait_ge(m_act, ACT_M * b + count(READS_ACT, AT[PS + 15] + 1))
                        for q in range(PT_):
                            convert(q)
                    prob_hi(v, b)
                    if v + 2 < SLOTS:
                        exp(v + 2, b)
                other_half(UNITS - 1, b)
                for m in range(AT[SLOTS], M):
                    item(m, b)

            batches(act, body, own)

        @block.gpsimd
        def _(pool):
            own = Own(pool, own_p)

            def split_weights(n):
                pool.wait_ge(w_hi, n)
                for k in range(DC):
                    pool.tensor_tensor(wq[1][:, k, :, :].rearrange("p j (r w) -> p j r w", r=2),
                                       spread(w_raw[:, 0, k, :].rearrange("p (j w) -> p j w", j=2).unsqueeze(2), 2, 2),
                                       wq[0][:, k, :, :].rearrange("p j (r w) -> p j r w", r=2), ALU.subtract)
                pool.tensor_tensor(wk[1][:, :, :], w_raw[:, 1, :, :], wk[0][:, :, :], ALU.subtract)
                pool.tensor_tensor(wv[1][:, :, :], w_raw[:, 2, :, :], wv[0][:, :, :], ALU.subtract).then_inc(w_lo, 1)

            def layer_norm(q, n, wait_xn):
                pool.wait_ge(stat, n + 1)
                wait_xn()
                newton(own, pool, rs[:, q % 2, 1, :], rs[:, q % 2, 2, :], rs[:, q % 2, 3, :])
                for t in range(2):
                    ins = pool.tensor_scalar(xn[:, q % 2, t, :], xp[:, q % 2, t, :], mv[:, q % 2, t, 0:1],
                                             rs[:, q % 2, 2, t:t + 1], ALU.subtract, ALU.mult)
                ins.then_inc(ln, 1)

            def convert(q, n):
                pool.wait_ge(c_hi, n + 1)
                cols = slice(q * PAIR, (q + 1) * PAIR)
                pool.tensor_tensor(xt_part[1][:, :, cols], xt[:, :, cols], xt_part[0][:, :, cols],
                                   ALU.subtract).then_inc(c_lo, 1)

            def widen(c, n, b):
                pool.wait_ge(d_wgt, CP * b + c + 1)
                if c:
                    pool.wait_ge(e_m, M * b + r_item(c - 1, n) + 1)
                pool.tensor_tensor(wwide[:, n, :, :].rearrange("p t (j w) -> p t j w", j=2),
                                   spread(wgt[:, :, 4 * n:4 * n + 4].rearrange("p j t -> p t j").unsqueeze(3), 3, dh),
                                   one[:, :].unsqueeze(2).unsqueeze(3).broadcast_to([P, 4, 2, dh]),
                                   ALU.mult).then_inc(p_wide, 1)

            def out_lo(c, n, b):
                pool.wait_ge(o_hi, R_M * b + 2 * c + n + 1)
                cols = slice(n * 512, (n + 1) * 512)
                pool.tensor_tensor(o_part[1][:, c, cols], ot[:, n, :], o_part[0][:, c, cols],
                                   ALU.subtract).then_inc(o_lo, 1)

            own.link(pool.memset(one[:, :], 1.0))
            own.step(pool.memset(lower[:, :, :], 1.0))
            pool.affine_select(out=lower[:, :, :], in_=lower[:, :, :], compare_op=ALU.is_gt, fill=0.0,
                               base=0, pattern=[[1, H], [-1, H]], channel_multiplier=0).then_inc(s_lower, 1)
            layer_norm(0, 0, lambda: None)
            layer_norm(1, 1, lambda: None)
            split_weights(1)
            for q in range(PT_):
                convert(q, q)
                if q + 2 < PT_:
                    layer_norm(q + 2, q + 2, lambda: pool.wait_ge(pre_pe, 2 * q + 1))
            pool.wait_ge(wo_hi, 1)
            pool.tensor_tensor(wo[1][:, :, :], wo_raw, wo[0][:, :, :], ALU.subtract).then_inc(wo_lo, 1)

            def body(b):
                for v in range(SLOTS):
                    c, s = v // PS, v % PS
                    if s == 1:
                        split_weights(CP * b + c + 2)
                    if v in ln_at:
                        q = ln_at[v]
                        layer_norm(q, PT_ * b + PT_ + q,
                                   lambda: pool.wait_ge(e_m, M * b + at_x(q - 2) + 1) if q >= 2 else None)
                    if c and s in (3, 4):
                        out_lo(c - 1, s - 3, b)
                    if v == (CP - 1) * PS + 4:
                        for q in range(PT_):
                            convert(q, PT_ * b + PT_ + q)
                    if s == PS - 1:
                        widen(c, 0, b)
                        widen(c, 1, b)
                for n in range(2):
                    out_lo(CP - 1, n, b)

            batches(pool, body, own)

        @block.vector
        def _(dve):
            own = Own(dve, own_v)

            def ln_stats(q, n, times):
                dve.wait_ge(xp_in[q % 2], 16 * times)
                if not (isinstance(n, int) and n < 2):
                    dve.wait_ge(ln, n - 1)
                for t in range(2):
                    own.link(dve.bn_stats(stats[:, t, :], xp[:, q % 2, t, :]))
                own.wait()
                for t in range(2):
                    own.link(dve.bn_aggr(mv[:, q % 2, t, :], stats[:, t, :]))
                own.wait()
                rsqrt_guess(own, dve, mv[:, q % 2, :, 1], rs[:, q % 2, 0, :], rs[:, q % 2, 1, :], rs[:, q % 2, 2, :])
                dve.tensor_scalar(rs[:, q % 2, 2, :].bitcast(I32), rs[:, q % 2, 2, :].bitcast(I32), -1, RSQRT_MAGIC,
                                  ALU.mult, ALU.add).then_inc(stat, 1)

            def row_max(v, b):
                dve.wait_ge(e_s, SLOTS * b + v + 1)
                dve.tensor_reduce(negmax[:, v % 4:v % 4 + 1], ps_s[:, v % 2, :], AX.X, ALU.max,
                                  negate=True).then_inc(d_max, 1)

            def choose(b):
                dve.wait_ge(a_gate, b + 1)
                own.step(dve.tensor_scalar(score[:, :, :], score[:, :, :], 1.0, None, ALU.add))
                own.step(dve.reciprocal(score[:, :, :], score[:, :, :]))
                other = spread(score[:, :, :].unsqueeze(2), 2, H)
                mine = spread(score[:, :, :].unsqueeze(3), 3, H)
                own.link(dve.tensor_tensor(before, other, mine, ALU.is_gt))
                own.step(dve.tensor_tensor(equal, other, mine, ALU.is_equal))
                own.step(dve.tensor_tensor(equal, equal,
                                           spread(lower[:, :, :].unsqueeze(1), 1, NT), ALU.mult))
                own.step(dve.tensor_tensor(before, before, equal, ALU.add))
                own.step(dve.tensor_reduce(rank[:, :, :], before, AX.X, ALU.add))
                dve.scalar_tensor_tensor(out=chosen[:, :, :], in0=rank[:, :, :], scalar=float(topk),
                                         in1=score[:, :, :], op0=ALU.is_lt, op1=ALU.mult).then_inc(d_chosen, 1)

            def prob_lo(v, b):
                u = v // 2
                for g in range(2):
                    dve.wait_ge(t_hi, 2 * SLOTS * b + 2 * v + g + 1)
                    at = (slice(None), u % 2, slice(4 * g, 4 * g + 4), slice((v % 2) * TOK, (v % 2 + 1) * TOK))
                    dve.tensor_tensor(pt[1][at], ps_t[:, g, :, :], pt[0][at], ALU.subtract).then_inc(t_lo, 1)

            def out_sum(u, b):
                dve.wait_ge(o_other, UNITS * b + u + 1)
                rows = slice(0, 64) if (u // PT_) % 2 == 0 else slice(64, P)
                cols = slice((u % PT_) * PAIR, (u % PT_ + 1) * PAIR)
                dve.tensor_tensor(ot_raw[rows, cols], ps_o[rows, u % 2, :], ot_other[rows, :],
                                  ALU.add).then_inc(o_sum, 1)

            def weights_of(c, b):
                dve.wait_ge(a_exp, SLOTS * b + PS * (c + 1))
                if c:
                    dve.wait_ge(p_wide, R_M * b + 2 * c)
                else:
                    dve.wait_ge(d_chosen, b + 1)
                own.step(dve.reciprocal(wgt[:, :, :], den[:, 2 * c:2 * c + 2, :]))
                dve.tensor_tensor(wgt[:, :, :], wgt[:, :, :], chosen[:, :, 2 * c:2 * c + 2].rearrange("p t j -> p j t"),
                                  ALU.mult).then_inc(d_wgt, 1)

            def item(m, b):
                slot, kind, arg = items[m]
                if kind in "kqv":
                    dve.wait_ge(m_act, ACT_M * b + count(READS_ACT, m + 1))
                    dve_item(dve, kind, arg, m_dve, (arg[0] + 1) % 2)
                elif kind == "r":
                    c, n = arg
                    dve.wait_ge(e_m, M * b + m + 1)
                    dve.wait_ge(o_sum, UNITS * b + 2 * PT_ * (c + 1))
                    if c:
                        dve.wait_ge(o_lo, R_M * b + 2 * (c - 1) + n + 1)
                    dve.tensor_tensor(ot[:, n, :], ot_raw[:, n * 512:(n + 1) * 512], ps_m[:, :],
                                      ALU.mult).then_inc(m_dve, 1)
                elif kind == "o":
                    dve.wait_ge(e_m, M * b + m + 1)
                    if arg == 0:
                        dve.wait_ge(xb_in, 16 * b + 16)
                    rows = xb[:, 2 * arg:2 * arg + 2, :]
                    dve.scalar_tensor_tensor(out=rows, in0=ps_m[:, :].rearrange("p (t d) -> p t d", t=2),
                                             scalar=gate, in1=rows, op0=ALU.mult, op1=ALU.add).then_inc(m_dve, 1)

            for q in range(PT_):
                ln_stats(q, q, q // 2 + 1)
            for i, (kind, arg) in enumerate(first_items):
                dve.wait_ge(pre_hi, i + 1)
                dve_item(dve, kind, arg, pre_dve, 0)
            dve.wait_ge(s_lower, 1)
            dve.sem_inc(batch_done, 1)

            def body(b):
                row_max(0, b)
                row_max(1, b)
                for v in range(SLOTS):
                    if v + 2 < SLOTS:
                        row_max(v + 2, b)
                    if v % 2 and v >= 3:
                        out_sum((v - 3) // 2, b)
                    if v - 1 in AT:
                        item(AT[v - 1], b)
                    prob_lo(v, b)
                    if v == 0:
                        choose(b)
                    if v in ln_at:
                        q = ln_at[v]
                        ln_stats(q, PT_ * b + PT_ + q, (b + 1) * (PT_ // 2) + q // 2 + 1)
                    if v % PS == PS - 1:
                        weights_of(v // PS, b)
                out_sum(UNITS - 1, b)
                for m in range(AT[SLOTS], M):
                    item(m, b)
                dve.wait_ge(m_dve, DVE_M * b + DVE_M)
                dve.sem_inc(batch_done, 1)

            batches(dve, body, own)


def ffn_weights(nc, fw, w, scales, s3, scale_src, s3_src, inexact, ident, tag):
    N = len(fw.src)
    RING = 4
    with semaphores(nc, tag) as sem, ExitStack() as ctx:
        stage = ctx.enter_context(nc.sbuf_tensor(f"{tag}_stage", [P, RING, WCH], F32))
        rest = ctx.enter_context(nc.sbuf_tensor(f"{tag}_rest", [P, 2, WCH], F32))
        worst = ctx.enter_context(nc.sbuf_tensor(f"{tag}_worst", [P, N + 1], F32))
        ps = ctx.enter_context(nc.psum_tensor(f"{tag}_ps", [P, 512], F32))
        loaded = [sem(f"loaded{i}") for i in range(RING)]
        small, rounded, diffed, worst_of, transposed = (sem(n) for n in (
            "small", "rounded", "diffed", "worst_of", "transposed"))
        block = ctx.enter_context(nc.Block())

        @block.sync
        def _(sp):
            for i, src in enumerate(fw.src):
                if i >= RING:
                    sp.wait_ge(diffed, i - RING + 1)
                sp.dma_start(stage[:, i % RING, :].rearrange("p (k n) -> p k n", n=src.shape[2]),
                             src).then_inc(loaded[i % RING], 16)
            for i, v in enumerate(scale_src):
                sp.dma_start(scales[:, i, :], v).then_inc(small, 16)
            sp.dma_start(s3[:, :], spread(s3_src.rearrange("(a n) -> a n", a=1), 0, P)).then_inc(small, 16)
            sp.wait_ge(small, 16 * (len(scale_src) + 1))

        @block.scalar
        def _(act):
            for i in range(N):
                act.wait_ge(loaded[i % RING], 16 * (i // RING + 1))
                act.activation(w[:, i * WCH:(i + 1) * WCH], stage[:, i % RING, :], ACT.Copy).then_inc(rounded, 1)

        @block.gpsimd
        def _(pool):
            for i in range(N):
                pool.wait_ge(rounded, i + 1)
                if i >= 2:
                    pool.wait_ge(worst_of, i - 1)
                pool.tensor_tensor(rest[:, i % 2, :], stage[:, i % RING, :], w[:, i * WCH:(i + 1) * WCH],
                                   ALU.subtract).then_inc(diffed, 1)

        @block.vector
        def _(dve):
            for i in range(N):
                dve.wait_ge(diffed, i + 1)
                dve.tensor_reduce(worst[:, i:i + 1], rest[:, i % 2, :], AX.X, ALU.max,
                                  apply_absolute_value=True).then_inc(worst_of, 1)
            dve.wait_ge(worst_of, N)
            dve.tensor_reduce(worst[:, N:N + 1], worst[:, 0:N], AX.X, ALU.max).then_inc(worst_of, 1)
            dve.wait_ge(transposed, 1)
            dve.tensor_reduce(inexact[0:1, 0:1], ps[0:1, 0:P], AX.X, ALU.max).then_inc(worst_of, 1)
            dve.wait_ge(worst_of, N + 2)

        @block.tensor
        def _(pe):
            pe.wait_ge(worst_of, N + 1)
            pe.transpose(ps[0:1, 0:P], worst[:, N:N + 1], ident[:, :]).then_inc(transposed, 1)


def load_full(nc, fw, w):
    with semaphores(nc, "G") as sem, nc.Block() as block:
        loaded = sem("full_loaded")

        @block.sync
        def _(sp):
            for i, src in enumerate(fw.src):
                sp.dma_start(w[:, i * WCH:(i + 1) * WCH].rearrange("p (k n) -> p k n", n=src.shape[2]),
                             src).then_inc(loaded, 16)
            sp.wait_ge(loaded, 16 * len(fw.src))


def ffn_either_way(nc, ident, gate, x_src, x_dst, t):
    fw = FfnWeights(*(t[f"L0_ffn_{n}T"] for n in ("w1_w", "w2_w", "h1_w", "h2_w", "w3_w")))
    scale_src = [t[f"L0_ffn_{n}_s"] for n in ("w1", "w2", "h1", "h2")]
    with ExitStack() as ctx:
        scales = ctx.enter_context(nc.sbuf_tensor("ffn_scales", [P, 4, fw.K["h1"]], F32))
        s3 = ctx.enter_context(nc.sbuf_tensor("ffn_s3", [P, D], F32))
        inexact = ctx.enter_context(nc.sbuf_tensor("ffn_inexact", [1, 1], F32))
        with nc.sbuf_tensor("ffn_w_rounded", [P, fw.cols], F32R) as w:
            ffn_weights(nc, fw, w, scales, s3, scale_src, t["L0_ffn_w3_s"], inexact, ident, "W")
            flag = nc.values_load(inexact[0:1, 0:1].bitcast(I32))
            with nc.If_eq(flag.val, 0):
                feed_forward(nc, ident, gate, x_src, x_dst, fw, w, scales, s3, True, "F")
        with nc.Else():
            with nc.sbuf_tensor("ffn_w_full", [P, fw.cols], F32) as w:
                load_full(nc, fw, w)
                feed_forward(nc, ident, gate, x_src, x_dst, fw, w, scales, s3, False, "G")


def constants(nc, ident, gates, g_xattn, g_ffn):
    with semaphores(nc, "S") as sem, nc.Block() as block:
        gates_in, tanh_done, ident_zero, ident_made = (sem(n) for n in (
            "gates_in", "tanh_done", "ident_zero", "ident_made"))

        @block.sync
        def _(sp):
            for i, g in enumerate((g_xattn, g_ffn)):
                sp.dma_start(gates[:, i, :], spread(g.rearrange("(a n) -> a n", a=1), 0, P)).then_inc(gates_in, 16)

        @block.scalar
        def _(act):
            act.wait_ge(gates_in, 32)
            act.activation(gates[:, :, :], gates[:, :, :], ACT.Tanh).then_inc(tanh_done, 1)
            act.wait_ge(tanh_done, 1)

        @block.gpsimd
        def _(pool):
            pool.memset(ident[:, :], 0.0).then_inc(ident_zero, 1)
            pool.wait_ge(ident_zero, 1)
            pool.affine_select(out=ident[:, :], in_=ident[:, :], compare_op=ALU.not_equal, fill=1.0,
                               base=0, pattern=[[-1, P]], channel_multiplier=1).then_inc(ident_made, 1)
            pool.wait_ge(ident_made, 1)


def gated_layers(nc, t, only=None):
    T = t["x"].shape[0]
    x1, x2, x3 = (nc.dram_tensor(f"x{i}", [T, D], F32, kind="Internal").ap() for i in range(1, 4))
    with ExitStack() as ctx:
        ident = ctx.enter_context(nc.sbuf_tensor("ident", [P, P], F32))
        gates = ctx.enter_context(nc.sbuf_tensor("gates", [P, 2, 2], F32))
        constants(nc, ident, gates, t["g_xattn"], t["g_ffn"])
        layers = [
            lambda src, dst: cross_attention(
                nc, ident, gates[:, 0, 0:1], src, dst, t["ctxT"],
                *(t[f"L0_xattn_{n}T"] for n in ("wq", "wk", "wv", "wo")),
                tuple(t[f"L0_xattn_{n}"] for n in ("bq", "bk", "bv", "bo")), None, 16, "A"),
            lambda src, dst: ffn_either_way(nc, ident, gates[:, 1, 0:1], src, dst, t),
            lambda src, dst: cross_attention(
                nc, ident, gates[:, 0, 1:2], src, dst, t["ctxT"],
                *(t[f"L1_xattn_{n}"] for n in ("Wq", "Wk", "Wv", "Wo")),
                None, (t["L1_xattn_ln_scale"], t["L1_xattn_ln_bias"]), 8, "C"),
            lambda src, dst: self_attention(
                nc, ident, gates[:, 1, 1:2], src, dst, *(t[f"L1_ffn_{n}"] for n in ("Wq", "Wk", "Wv", "Ws")),
                t["L1_ffn_Wo"].rearrange("h e d -> (h e) d"), t["L1_ffn_bo"], t["ctxT"].shape[0],
                t["L1_ffn_Ws"].shape[1], 3),
        ]
        if only is not None:
            layers[only](t["x"], t["out"])
            return
        for layer, src, dst in zip(layers, (t["x"], x1, x2, x3), (x1, x2, x3, t["out"])):
            layer(src, dst)


def laid_out(inputs):
    import numpy as np

    def cols(v):
        return v.reshape(-1, P).T

    a = {}
    for name, v in inputs.items():
        v = np.asarray(v)
        if name == "x":
            a[name] = v.reshape(-1, v.shape[-1])
        elif name == "ctx_1024":
            a["ctxT"] = v.transpose(0, 2, 1)
        elif name.startswith("L0_xattn_w") or (name.startswith("L0_ffn_") and name.endswith("_w")):
            a[name + "T"] = v.T
        elif name.endswith("Wkv"):
            half = v.shape[1] // 2
            a[name[:-3] + "Wk"], a[name[:-3] + "Wv"] = v[:, :half], v[:, half:]
        elif name in ("L0_xattn_bq", "L0_xattn_bk", "L1_xattn_ln_scale", "L1_xattn_ln_bias", "L0_ffn_w1_s",
                      "L0_ffn_w2_s", "L0_ffn_h1_s", "L0_ffn_h2_s"):
            a[name] = cols(v)
        else:
            a[name] = v
    return {name: np.ascontiguousarray(v) for name, v in a.items()}


def kernel(**inputs):
    import concourse.bacc as bacc
    from concourse.bass_utils import run_bass_kernel_spmd

    arrays = laid_out(inputs)
    nc = bacc.Bacc("TRN2", target_bir_lowering=False, num_devices=1)
    tensors = {n: nc.dram_tensor(f"in_{n}", list(v.shape), mybir.dt.from_np(v.dtype), kind="ExternalInput").ap()
               for n, v in arrays.items()}
    tensors["out"] = nc.dram_tensor("out_x", list(arrays["x"].shape), F32, kind="ExternalOutput").ap()
    gated_layers(nc, tensors)
    r = run_bass_kernel_spmd(nc, [{f"in_{n}": v for n, v in arrays.items()}], core_ids=[0])
    return r.results[0]["out_x"].reshape(inputs["x"].shape)
```

```python
from contextlib import ExitStack, contextmanager

import concourse.bass as bass
from concourse import mybir

F32 = mybir.dt.float32
F32R = mybir.dt.float32r
I32 = mybir.dt.int32
ALU = mybir.AluOpType
ACT = mybir.ActivationFunctionType
AX = mybir.AxisListType

P = 128
D = 256
DC = D // P
TOK = 128
PAIR = 2 * TOK
EPS = 1e-5
RSQRT_MAGIC = 0x5F3759DF


@contextmanager
def semaphores(nc, tag):
    made = []

    def sem(name):
        made.append(nc.alloc_semaphore(name=f"{tag}_{name}"))
        return made[-1]

    yield sem
    nc.clear_and_free_semaphores(made)
    nc.all_engine_barrier()


class Own:

    def __init__(self, eng, sem):
        self.eng, self.sem, self.n = eng, sem, 0

    def link(self, ins):
        ins.then_inc(self.sem, 1)
        self.n += 1

    def wait(self):
        self.eng.wait_ge(self.sem, self.n)

    def step(self, ins):
        self.link(ins)
        self.wait()

    def clear(self):
        if self.n:
            self.wait()
            self.eng.sem_clear(self.sem)
            self.n = 0


def spread(ap, dim, n):
    shape = list(ap.shape)
    shape[dim] = n
    return ap.broadcast_to(shape)


def split_passes(hi_lo_a, hi_lo_b):
    (ah, al), (bh, bl) = hi_lo_a, hi_lo_b
    return ((ah, bh), (ah, bl), (al, bh))


def rsqrt_guess(own, eng, var, v_eps, half, y):
    own.step(eng.tensor_scalar(v_eps, var, EPS, None, ALU.add))
    own.link(eng.tensor_scalar(half, v_eps, -0.5, None, ALU.mult))
    own.step(eng.tensor_scalar(y.bitcast(I32), v_eps.bitcast(I32), 1, None, ALU.logical_shift_right))


def newton(own, eng, half, y, t):
    for _ in range(3):
        own.step(eng.tensor_tensor(t, y, y, ALU.mult))
        own.step(eng.tensor_tensor(t, t, half, ALU.mult))
        own.step(eng.tensor_scalar(t, t, 1.5, None, ALU.add))
        own.step(eng.tensor_tensor(y, y, t, ALU.mult))


def cross_attention(nc, ident, gate, x_src, x_dst, ctxT, wqT, wkT, wvT, woT, bias, ln2, H, tag):
    B, _, S = ctxT.shape
    HD = wqT.shape[1]
    dh = HD // H
    C = HD // P
    HC = H // C
    G = H // 4
    S2 = S + S % 2
    SCALE = float(dh) ** -0.5
    NP = x_src.shape[0] // PAIR
    PB = NP // B
    RING = 4
    MANY = H > 8
    Q_ON_DVE = not MANY
    AHEAD = 3 if ln2 else 2
    QW = C * PAIR
    xs = x_src.rearrange("(n t p) d -> n p t d", t=2, p=P)
    xd = x_dst.rearrange("(n t p) d -> n p t d", t=2, p=P)
    assert PB == RING and 4 * S <= 512 and H % 8 == 0

    with semaphores(nc, tag) as sem, ExitStack() as ctx:
        def sb(name, shape, dt=F32):
            return ctx.enter_context(nc.sbuf_tensor(f"{tag}_{name}", shape, dt))

        wq_raw = sb("wq_raw", [P, DC, HD])
        wq = [sb("wq_hi", [P, DC, HD], F32R), sb("wq_lo", [P, DC, HD], F32R)]
        wo_raw = sb("wo_raw", [P, C, D])
        wo = [sb("wo_hi", [P, C, D], F32R), sb("wo_lo", [P, C, D], F32R)]
        wk = sb("wk", [P, DC, HD])
        wv = sb("wv", [P, DC, HD])
        cx = sb("cx", [P, DC, S])
        one = sb("one", [P, 1])
        head_mask = sb("head_mask", [P, HC])
        qbias = sb("qbias", [P, C])
        kbias = sb("kbias", [P, C])
        vbias = sb("vbias", [S, HD])
        obias = sb("obias", [P, D])
        ln_sb = sb("ln_sb", [P, 2, DC])
        kt = sb("kt", [P, C, S])
        kt_part = [sb("kt_hi", [P, C, S], F32R), sb("kt_lo", [P, C, S], F32R)]
        kblk = [sb("kblk_hi", [P, C, HC, S], F32R), sb("kblk_lo", [P, C, HC, S], F32R)]
        vt = sb("vt", [S, HD])
        vpad = [sb("vpad_hi", [P, H * P + P], F32R), sb("vpad_lo", [P, H * P + P], F32R)]
        x = sb("x", [P, RING, 2, D])
        res = sb("res", [P, RING, 2, D])
        stats = sb("stats", [P, 4, 6])
        mv = sb("mv", [P, 2, 2, 2])
        rs = sb("rs", [P, 2, 4, 2])
        xn = sb("xn", [P, 2, 2, D])
        xt = sb("xt", [P, DC, PAIR])
        xt_part = [sb("xt_hi", [P, DC, PAIR], F32R), sb("xt_lo", [P, DC, PAIR], F32R)]
        qt = sb("qt", [P, C, PAIR])
        q_part = [sb("q_hi", [P, 2, C, PAIR], F32R), sb("q_lo", [P, 2, C, PAIR], F32R)]
        prob = sb("prob", [P, 2, H, S2])
        half_sum = sb("half_sum", [P, 2, H, S2 // 2])
        negmax = sb("negmax", [P, H])
        rsum = sb("rsum", [P, 2, 2, H])
        rwide = sb("rwide", [P, 2, HD])
        pt = [sb("pt_hi", [P, 2, H, PAIR], F32R), sb("pt_lo", [P, 2, H, PAIR], F32R)]
        ot = sb("ot", [P, C, PAIR])
        rt = sb("rt", [P, C, PAIR])
        o_part = [sb("o_hi", [P, C, PAIR], F32R), sb("o_lo", [P, C, PAIR], F32R)]

        ps_s = ctx.enter_context(nc.psum_tensor(f"{tag}_ps_s", [P, G, 512], F32))
        ps_t = ctx.enter_context(nc.psum_tensor(f"{tag}_ps_t", [P, 2, 512], F32))
        ps_o = ctx.enter_context(nc.psum_tensor(f"{tag}_ps_o", [P, C, PAIR], F32))
        ps_m = ctx.enter_context(nc.psum_tensor(f"{tag}_ps_m", [P, 512 * max(1, C // 2)], F32))

        def diag(v):
            step = P + dh
            return [v[0:S, c * HC * P:c * HC * P + HC * step].rearrange("s (j w) -> s j w", w=step)[:, :, 0:dh]
                    for c in range(C)]

        s_w = [sem(f"w{i}") for i in range(6)]
        s_small = sem("small")
        s_ctx = sem("ctx")
        x_in = [sem(f"x_in{i}") for i in range(RING)]
        r_in = [sem(f"r_in{i}") for i in range(RING)]
        x_out = [sem(f"x_out{i}") for i in range(RING)]
        s_pt_zeros = [sem("pt_hi_zeroed"), sem("pt_lo_zeroed")]
        s_const, s_zeros = sem("head_mask_made"), sem("vpad_zeroed")
        w_hi, w_lo = sem("w_hi"), sem("w_lo")
        stat, root_done, ln1, ln2_done = (sem(n) for n in ("stat", "root", "ln1", "ln2_done"))
        ln_done = ln2_done if ln2 else ln1
        e_xt, e_q, e_s, e_t, e_pv, e_rt, e_o, e_k, e_v = (sem(n) for n in (
            "pe_xt", "pe_q", "pe_s", "pe_t", "pe_pv", "pe_rt", "pe_o", "pe_k", "pe_v"))
        xt_raw, xt_hi, xt_lo = sem("xt_raw"), sem("s_xt_hi"), sem("s_xt_lo")
        qt_raw, q_hi, q_lo = sem("qt_raw"), sem("s_q_hi"), sem("s_q_lo")
        kt_raw, kt_hi, kt_lo, kb_hi, kb_lo = (sem(n) for n in ("s_kt", "s_kt_hi", "s_kt_lo", "s_kb_hi", "s_kb_lo"))
        vt_raw, v_hi, v_lo = sem("s_vt"), sem("s_v_hi"), sem("s_v_lo")
        d_sub, a_exp, d_r = sem("sub"), sem("exp"), sem("r")
        p_sum, r_biased = sem("p_sum"), sem("r_biased")
        t_hi, t_lo = sem("t_hi"), sem("t_lo")
        r_wide, rt_copied = sem("r_wide"), sem("rt_copied")
        o_raw, o_hi, o_lo, d_fin = sem("o_raw"), sem("s_o_hi"), sem("s_o_lo"), sem("fin")
        own_v, own_a, own_p = sem("own_v"), sem("own_a"), sem("own_p")

        def batches(eng, body, own=None):
            body(0, True)
            if own:
                own.clear()
            with eng.Fori(1, B) as b:
                body(b, False)
                if own:
                    own.clear()

        def q_low(eng, n, par):
            eng.wait_ge(q_hi, n + 1)
            eng.tensor_tensor(q_part[1][:, par, :, :], qt[:, :, :], q_part[0][:, par, :, :],
                              ALU.subtract).then_inc(q_lo, 1)

        block = ctx.enter_context(nc.Block())

        @block.sync
        def _(sp):
            def load_x(n, at):
                sp.dma_start(x[:, at % RING, :, :], xs[n]).then_inc(x_in[at % RING], 16)

            def load_ctx(b):
                sp.dma_start(cx[:, :, :], ctxT[b].rearrange("(c p) s -> p c s", p=P)).then_inc(s_ctx, 16)

            load_x(0, 0)
            load_ctx(0)
            for i, (dst, src) in enumerate(((wk, wkT), (wv, wvT), (wq_raw, wqT), (wo_raw, woT))):
                sp.dma_start(dst[:, :, :], src.rearrange("(c p) n -> p c n", p=P)).then_inc(s_w[i], 16)
            small = []
            if bias:
                bq, bk, bv, bo = bias
                small += [(qbias[:, :], bq),
                          (kbias[:, :], bk),
                          (vbias[:, :], spread(bv.rearrange("(a n) -> a n", a=1), 0, S)),
                          (obias[:, :], spread(bo.rearrange("(a n) -> a n", a=1), 0, P))]
            if ln2:
                small += [(ln_sb[:, i, :], v) for i, v in enumerate(ln2)]
            for dst, src in small:
                sp.dma_start(dst, src).then_inc(s_small, 16)
            for n in range(1, AHEAD + 1):
                load_x(n, n)

            def store(n, p):
                sp.wait_ge(d_fin, n + 1)
                sp.dma_start(xd[n], res[:, p % RING, :, :]).then_inc(x_out[p % RING], 16)

            def body(b, first, last=False):
                for p in range(PB):
                    n = PB * b + p
                    if p == 1:
                        sp.wait_ge(e_v, b + 1)
                        load_ctx(0 if last else b + 1)
                    if not first:
                        sp.wait_ge(x_out[p], 16 * b)
                    sp.dma_start(res[:, p, :, :], xs[n]).then_inc(r_in[p], 16)
                    m = p + AHEAD + 1
                    if not (first and m < RING):
                        sp.wait_ge(ln1, n + AHEAD - 2)
                    load_x(m - PB if last and m >= PB else n + AHEAD + 1, m)
                    if not (first and p < 2):
                        store(n - 2, p - 2)

            body(0, True)
            with sp.Fori(1, B - 1) as b:
                body(b, False)
            body(B - 1, False, True)
            for n in (NP - 2, NP - 1):
                store(n, n)
            for i in range(RING):
                sp.wait_ge(x_out[i], 16 * B)
                sp.wait_ge(x_in[i], 16 * len(range(i, NP + AHEAD + 1, RING)))

        @block.tensor
        def _(pe):
            def k_proj(b, t):
                pe.wait_ge(s_ctx, 16 * b + 16)
                for c in range(C):
                    for k in range(DC):
                        mm = pe.matmul(ps_m[:, c * S:(c + 1) * S], wk[:, k, c * P:(c + 1) * P], cx[:, k, :],
                                       start=k == 0, stop=k == DC - 1)
                mm.then_inc(e_k, 1)

            def v_proj():
                for k in range(DC):
                    mm = pe.matmul(ps_m[0:S, 0:HD], cx[:, k, :], wv[:, k, :], start=k == 0, stop=k == DC - 1)
                mm.then_inc(e_v, 1)

            def x_transpose(n, par):
                pe.wait_ge(ln_done, n + 1)
                for c in range(DC):
                    for t in range(2):
                        at = c * PAIR + t * TOK
                        mm = pe.transpose(ps_m[:, at:at + TOK], xn[:, par, t, c * P:(c + 1) * P], ident[:, :])
                mm.then_inc(e_xt, 1)

            def q_proj(n):
                pe.wait_ge(xt_hi, n + 1)
                pe.wait_ge(xt_lo, n + 1)
                for c in range(C):
                    i = 0
                    for k in range(DC):
                        for w, a in split_passes(wq, xt_part):
                            mm = pe.matmul(ps_m[:, c * PAIR:(c + 1) * PAIR], w[:, k, c * P:(c + 1) * P],
                                           a[:, k, :], start=i == 0, stop=i == 3 * DC - 1)
                            i += 1
                mm.then_inc(e_q, 1)

            def scores(n, t, T):
                par = (t // 2) % 2
                cols = slice((t % 2) * TOK, (t % 2) * TOK + TOK)
                for g in range(G):
                    per = min(HC, 4)
                    for j in range(4 // per):
                        h = 4 * g + j * per
                        c = h // HC
                        for i, (a, kk) in enumerate(split_passes(q_part, kblk)):
                            mm = pe.matmul(ps_s[:, g, j * per * S:(j + 1) * per * S], a[:, par, c, cols],
                                           kk[:, c, h % HC:h % HC + per, :],
                                           start=i == 0, stop=i == 2)
                mm.then_inc(e_s, 1)

            def p_transpose(T, t, half):
                pe.wait_ge(a_exp, T + 1)
                for g in range(G // 2 * half, G // 2 * (half + 1)):
                    u = G * T + g
                    if not (isinstance(u, int) and u < 2):
                        pe.wait_ge(t_lo, u - 1)
                    for j in range(4):
                        mm = pe.transpose(ps_t[0:S, g % 2, j * TOK:(j + 1) * TOK],
                                          prob[:, t % 2, 4 * g + j, 0:S], ident[:, :])
                    mm.then_inc(e_t, 1)

            def pv(n, par, part):
                if part == 0:
                    pe.wait_ge(t_lo, G * (2 * n + 1) + G // 2)
                elif part == 2:
                    pe.wait_ge(t_lo, G * (2 * n + 2))
                for h in range(H // 4 * part, H // 4 * (part + 1)):
                    c, j = divmod(h, HC)
                    for i, (v, a) in enumerate(split_passes(vpad, pt)):
                        mm = pe.matmul(ps_o[:, c, :], v[:, h * P:(h + 1) * P], a[:, par, h, :],
                                       start=j == 0 and i == 0, stop=j == HC - 1 and i == 2)
                if part == 3:
                    mm.then_inc(e_pv, 1)

            def r_transpose(n):
                pe.wait_ge(r_wide, 2 * n + 2)
                for c in range(C):
                    for t in range(2):
                        at = c * PAIR + t * TOK
                        mm = pe.transpose(ps_m[:, at:at + TOK], rwide[:, t, c * P:(c + 1) * P], ident[:, :])
                mm.then_inc(e_rt, 1)

            def out_proj(n):
                pe.wait_ge(o_hi, n + 1)
                pe.wait_ge(o_lo, n + 1)
                for t in range(2):
                    i = 0
                    for c in range(C):
                        for a, w in split_passes(o_part, wo):
                            mm = pe.matmul(ps_m[:, t * D:(t + 1) * D], a[:, c, t * TOK:(t + 1) * TOK],
                                           w[:, c, :], start=i == 0, stop=i == 3 * C - 1)
                            i += 1
                mm.then_inc(e_o, 1)

            pe.wait_ge(s_w[0], 16)
            k_proj(0, 0)
            pe.wait_ge(kt_raw, 1)
            pe.wait_ge(s_w[1], 16)
            v_proj()
            pe.wait_ge(vt_raw, 1)
            x_transpose(0, 0)
            pe.wait_ge(xt_raw, 1)
            pe.wait_ge(w_hi, 2)
            pe.wait_ge(w_lo, 2)
            q_proj(0)

            def body(b, first):
                for p in range(PB):
                    n = PB * b + p
                    T = 2 * n
                    one_before, two_before = not first or p >= 1, not first or p >= 2
                    if one_before:
                        p_transpose(T - 1, 1, 0)
                    if p == 0:
                        pe.wait_ge(kb_hi, b + 1)
                        pe.wait_ge(kb_lo, b + 1)
                    pe.wait_ge(q_hi, n + 1)
                    pe.wait_ge(q_lo, n + 1)
                    if one_before:
                        pe.wait_ge(d_sub, T)
                    scores(n, 2 * p, T)
                    if p == 1 and not first:
                        pe.wait_ge(vt_raw, b + 1)
                    elif two_before:
                        pe.wait_ge(rt_copied, n - 1)
                    else:
                        pe.wait_ge(qt_raw, n + 1)
                    x_transpose(n + 1, (p + 1) % 2)
                    if one_before:
                        if two_before:
                            pe.wait_ge(o_raw, n - 1)
                        if p == 1:
                            pe.wait_ge(v_hi, b + 1)
                            pe.wait_ge(v_lo, b + 1)
                        pv(n - 1, (p - 1) % 2, 0)
                        p_transpose(T - 1, 1, 1)
                    if p == PB - 1:
                        pe.wait_ge(xt_raw, n + 2)
                        k_proj(b + 1, n)
                    if one_before:
                        pv(n - 1, (p - 1) % 2, 1)
                    if two_before:
                        if p == PB - 1:
                            pe.wait_ge(kt_raw, b + 2)
                        else:
                            pe.wait_ge(xt_raw, n + 2)
                        out_proj(n - 2)
                    p_transpose(T, 0, 0)
                    pe.wait_ge(d_sub, T + 1)
                    scores(n, 2 * p + 1, T + 1)
                    if two_before:
                        pe.wait_ge(d_fin, n - 1)
                    else:
                        pe.wait_ge(xt_raw, n + 2)
                    q_proj(n + 1)
                    if one_before:
                        pv(n - 1, (p - 1) % 2, 2)
                    p_transpose(T, 0, 1)
                    if one_before:
                        pe.wait_ge(qt_raw, n + 2)
                        r_transpose(n - 1)
                        pv(n - 1, (p - 1) % 2, 3)
                    if p == 0 and not first:
                        pe.wait_ge(rt_copied, n)
                        v_proj()

            batches(pe, body)
            n = NP
            p_transpose(2 * n - 1, 1, 0)
            pe.wait_ge(o_raw, n - 1)
            pv(n - 1, (n - 1) % 2, 0)
            p_transpose(2 * n - 1, 1, 1)
            pv(n - 1, (n - 1) % 2, 1)
            pe.wait_ge(rt_copied, n - 1)
            out_proj(n - 2)
            pv(n - 1, (n - 1) % 2, 2)
            pe.wait_ge(d_fin, n - 1)
            r_transpose(n - 1)
            pv(n - 1, (n - 1) % 2, 3)
            pe.wait_ge(rt_copied, n)
            out_proj(n - 1)

        @block.scalar
        def _(act):
            own = Own(act, own_a)

            def x_parts(n):
                act.wait_ge(e_xt, n + 1)
                if not (isinstance(n, int) and n == 0):
                    act.wait_ge(xt_lo, n)
                for c in range(DC):
                    src = ps_m[:, c * PAIR:(c + 1) * PAIR]
                    if ln2:
                        ins = act.activation(xt[:, c, :], src, ACT.Identity, bias=ln_sb[:, 1, c:c + 1],
                                             scale=ln_sb[:, 0, c:c + 1])
                    else:
                        ins = act.activation(xt[:, c, :], src, ACT.Copy)
                ins.then_inc(xt_raw, 1)
                act.wait_ge(xt_raw, n + 1)
                if not (isinstance(n, int) and n == 0):
                    act.wait_ge(e_q, n)
                act.activation(xt_part[0][:, :, :], xt[:, :, :], ACT.Copy).then_inc(xt_hi, 1)

            def q_parts(n, par):
                act.wait_ge(e_q, n + 1)
                if not (isinstance(n, int) and n == 0):
                    act.wait_ge(q_lo, n)
                for c in range(C):
                    src = ps_m[:, c * PAIR:(c + 1) * PAIR]
                    if bias:
                        ins = act.activation(qt[:, c, :], src, ACT.Identity, bias=qbias[:, c:c + 1], scale=SCALE)
                    else:
                        ins = act.activation(qt[:, c, :], src, ACT.Copy, scale=SCALE)
                ins.then_inc(qt_raw, 1)
                act.wait_ge(qt_raw, n + 1)
                act.activation(q_part[0][:, par, :, :], qt[:, :, :], ACT.Copy).then_inc(q_hi, 1)

            def k_parts(b):
                act.wait_ge(e_k, b + 1)
                if not (isinstance(b, int) and b == 0):
                    act.wait_ge(kt_lo, b)
                    act.wait_ge(kb_hi, b)
                for c in range(C):
                    src = ps_m[:, c * S:(c + 1) * S]
                    if bias:
                        ins = act.activation(kt[:, c, :], src, ACT.Identity, bias=kbias[:, c:c + 1], scale=1.0)
                    else:
                        ins = act.activation(kt[:, c, :], src, ACT.Copy)
                ins.then_inc(kt_raw, 1)
                act.wait_ge(kt_raw, b + 1)
                act.activation(kt_part[0][:, :, :], kt[:, :, :], ACT.Copy).then_inc(kt_hi, 1)

            def v_parts(b, n):
                act.wait_ge(vt_raw, b + 1)
                if n is not None:
                    act.wait_ge(e_pv, n)
                for c, dst in enumerate(diag(vpad[0])):
                    ins = act.activation(dst, vt[:, c * P:(c + 1) * P].rearrange("s (j w) -> s j w", w=dh), ACT.Copy)
                ins.then_inc(v_hi, 1)

            def prob_hi(T, par, t, half):
                for g in range(G // 2 * half, G // 2 * (half + 1)):
                    act.wait_ge(e_t, G * T + g + 1)
                    dst = pt[0][0:S, par, 4 * g:4 * g + 4, t * TOK:(t + 1) * TOK]
                    act.activation(dst, ps_t[0:S, g % 2, :].rearrange("s (h q) -> s h q", h=4),
                                   ACT.Copy).then_inc(t_hi, 1)

            def exp(T, t):
                act.wait_ge(d_sub, T + 1)
                act.activation(prob[:, t, :, 0:S], prob[:, t, :, 0:S], ACT.Exp).then_inc(a_exp, 1)

            def rt_copy(n):
                act.wait_ge(e_rt, n + 1)
                if not (isinstance(n, int) and n == 0):
                    act.wait_ge(o_raw, n)
                act.activation(rt[:, :, :], ps_m[:, 0:QW].rearrange("p (c q) -> p c q", c=C),
                               ACT.Copy).then_inc(rt_copied, 1)

            def out_hi(n):
                act.wait_ge(o_raw, n + 1)
                if not (isinstance(n, int) and n == 0):
                    act.wait_ge(e_o, n)
                act.activation(o_part[0][:, :, :], ot[:, :, :], ACT.Copy).then_inc(o_hi, 1)

            if small_n := 16 * ((4 if bias else 0) + (2 if ln2 else 0)):
                act.wait_ge(s_small, small_n)
            if bias:
                own.step(act.activation(qbias[:, :], qbias[:, :], ACT.Copy, scale=SCALE))
            k_parts(0)
            act.wait_ge(s_zeros, 1)
            v_parts(0, None)
            for i, (hi, raw) in enumerate(((wq, wq_raw), (wo, wo_raw))):
                act.wait_ge(s_w[2 + i], 16)
                act.activation(hi[0][:, :, :], raw[:, :, :], ACT.Copy).then_inc(w_hi, 1)
            x_parts(0)
            q_parts(0, 0)

            def body(b, first):
                for p in range(PB):
                    n = PB * b + p
                    T = 2 * n
                    one_before, two_before = not first or p >= 1, not first or p >= 2
                    if one_before:
                        if not first or p >= 3:
                            act.wait_ge(e_pv, n - 2)
                        prob_hi(T - 1, (p - 1) % 2, 1, 0)
                    if two_before:
                        out_hi(n - 2)
                    x_parts(n + 1)
                    if one_before:
                        prob_hi(T - 1, (p - 1) % 2, 1, 1)
                    if p == PB - 1:
                        k_parts(b + 1)
                    exp(T, 0)
                    if two_before:
                        act.wait_ge(e_pv, n - 1)
                    prob_hi(T, p % 2, 0, 0)
                    if not MANY:
                        exp(T + 1, 1)
                    q_parts(n + 1, (p + 1) % 2)
                    prob_hi(T, p % 2, 0, 1)
                    if one_before:
                        rt_copy(n - 1)
                    if MANY:
                        exp(T + 1, 1)
                    if p == 0 and not first:
                        v_parts(b, n)

            own.clear()
            act.wait_ge(s_pt_zeros[0], 1)
            batches(act, body, own)
            n = NP
            prob_hi(2 * n - 1, (n - 1) % 2, 1, 0)
            out_hi(n - 2)
            prob_hi(2 * n - 1, (n - 1) % 2, 1, 1)
            rt_copy(n - 1)
            out_hi(n - 1)

        @block.gpsimd
        def _(pool):
            own = Own(pool, own_p)
            own.link(pool.memset(one[:, :], 1.0))
            own.step(pool.memset(head_mask[:, :], 1.0))
            own.step(pool.affine_select(out=head_mask[:, :], in_=head_mask[:, :], compare_op=ALU.is_ge, fill=0.0,
                                        base=0, pattern=[[-dh, HC]], channel_multiplier=1))
            pool.affine_select(out=head_mask[:, :], in_=head_mask[:, :], compare_op=ALU.is_ge, fill=0.0,
                               base=dh - 1, pattern=[[dh, HC]], channel_multiplier=-1).then_inc(s_const, 1)

            def root(n, par):
                pool.wait_ge(stat, n + 1)
                at = slice(0, 2) if ln2 else slice(par, par + 1)
                newton(own, pool, rs[:, at, 1, :], rs[:, at, 2, :], rs[:, at, 3, :])
                pool.sem_inc(root_done, 1)

            def x_low(n):
                pool.wait_ge(xt_hi, n + 1)
                pool.tensor_tensor(xt_part[1][:, :, :], xt[:, :, :], xt_part[0][:, :, :],
                                   ALU.subtract).then_inc(xt_lo, 1)

            def o_low(n):
                pool.wait_ge(o_hi, n + 1)
                if not (isinstance(n, int) and n == 0):
                    pool.wait_ge(e_o, n)
                pool.tensor_tensor(o_part[1][:, :, :], ot[:, :, :], o_part[0][:, :, :],
                                   ALU.subtract).then_inc(o_lo, 1)

            def widen(n, par, t):
                pool.wait_ge(d_r, 2 * n + t + 1)
                if not (isinstance(n, int) and n == 0):
                    pool.wait_ge(e_rt, n)
                pool.tensor_tensor(rwide[:, t, :].rearrange("p (h w) -> p h w", w=dh),
                                   spread(rsum[:, par, t, :].unsqueeze(2), 2, dh),
                                   one[:, :].unsqueeze(2).broadcast_to([P, H, dh]), ALU.mult).then_inc(r_wide, 1)

            def k_low(b):
                pool.wait_ge(kt_hi, b + 1)
                if not (isinstance(b, int) and b == 0):
                    pool.wait_ge(kb_lo, b)
                pool.tensor_tensor(kt_part[1][:, :, :], kt[:, :, :], kt_part[0][:, :, :],
                                   ALU.subtract).then_inc(kt_lo, 1)

            def k_block_low(b, T):
                pool.wait_ge(kt_lo, b + 1)
                if T is not None:
                    pool.wait_ge(e_s, T)
                for c in range(C):
                    ins = pool.tensor_tensor(kblk[1][:, c, :, :], spread(kt_part[1][:, c, :].unsqueeze(1), 1, HC),
                                             spread(head_mask[:, :].unsqueeze(2), 2, S), ALU.mult)
                ins.then_inc(kb_lo, 1)

            def fold(T, t):
                if MANY:
                    pool.wait_ge(a_exp, T + 1)
                    if not (isinstance(T, int) and T < 2):
                        pool.wait_ge(d_r, T - 1)
                    pool.tensor_tensor(half_sum[:, t, :, :], prob[:, t, :, 0:S2 // 2], prob[:, t, :, S2 // 2:S2],
                                       ALU.add).then_inc(p_sum, 1)

            def add_bias(n, at, times):
                if bias:
                    pool.wait_ge(r_in[at], 16 * times)
                    pool.tensor_tensor(res[:, at, :, :], res[:, at, :, :], spread(obias[:, :].unsqueeze(1), 1, 2),
                                       ALU.add).then_inc(r_biased, 1)

            def v_low(b):
                pool.wait_ge(v_hi, b + 1)
                for c, (hi, lo) in enumerate(zip(diag(vpad[0]), diag(vpad[1]))):
                    ins = pool.tensor_tensor(lo, vt[:, c * P:(c + 1) * P].rearrange("s (j w) -> s j w", w=dh),
                                             hi, ALU.subtract)
                ins.then_inc(v_lo, 1)

            pool.wait_ge(s_const, 1)
            pool.memset(pt[1][S // 32 * 32:P, :, :, :].bitcast(F32), 0.0).then_inc(s_pt_zeros[1], 1)
            pool.wait_ge(s_pt_zeros[1], 1)
            root(0, 0)
            k_low(0)
            k_block_low(0, None)
            v_low(0)
            root(1, 1)
            x_low(0)
            if ln2:
                root(2, 0)
            if not Q_ON_DVE:
                q_low(pool, 0, 0)

            def body(b, first):
                for p in range(PB):
                    n = PB * b + p
                    T = 2 * n
                    one_before, two_before = not first or p >= 1, not first or p >= 2
                    if two_before:
                        o_low(n - 2)
                    if one_before:
                        widen(n - 1, (p - 1) % 2, 0)
                        fold(T - 1, 1)
                    x_low(n + 1)
                    if one_before:
                        widen(n - 1, (p - 1) % 2, 1)
                    root(n + AHEAD, (p + AHEAD) % 2)
                    if p == PB - 1:
                        k_low(b + 1)
                    fold(T, 0)
                    if not Q_ON_DVE:
                        q_low(pool, n + 1, (p + 1) % 2)
                    if p == PB - 1:
                        k_block_low(b + 1, 2 * n + 2)
                    if p == 0 and not first:
                        v_low(b)
                    if one_before:
                        add_bias(n - 1, (p - 1) % RING, b + (1 if p else 0))

            if bias:
                pool.wait_ge(s_small, 16 * 4)
                own.step(pool.tensor_scalar(obias[:, :], obias[:, :], gate, None, ALU.mult))
            own.clear()
            batches(pool, body, own)
            o_low(NP - 2)
            widen(NP - 1, (NP - 1) % 2, 0)
            fold(2 * NP - 1, 1)
            widen(NP - 1, (NP - 1) % 2, 1)
            add_bias(NP - 1, RING - 1, B)
            o_low(NP - 1)

        @block.vector
        def _(dve):
            own = Own(dve, own_v)

            def ln_stats(n, par, at, times, second=True):
                dve.wait_ge(x_in[at], 16 * times)
                second = second and ln2
                sources = [(x[:, at, :, :], par)]
                if second:
                    dve.wait_ge(ln1, n)
                    sources.append((xn[:, 1 - par, :, :], 1 - par))
                if not (isinstance(n, int) and n < 2):
                    dve.wait_ge(ln_done, n - 1)
                for i, (src, _) in enumerate(sources):
                    for t in range(2):
                        own.link(dve.bn_stats(stats[:, 2 * i + t, :], src[:, t, :]))
                own.wait()
                for i, (_, q) in enumerate(sources):
                    for t in range(2):
                        own.link(dve.bn_aggr(mv[:, q, t, :], stats[:, 2 * i + t, :]))
                own.wait()
                q = slice(0, 2) if second else slice(par, par + 1)
                rsqrt_guess(own, dve, mv[:, q, :, 1], rs[:, q, 0, :], rs[:, q, 1, :], rs[:, q, 2, :])
                dve.tensor_scalar(rs[:, q, 2, :].bitcast(I32), rs[:, q, 2, :].bitcast(I32), -1, RSQRT_MAGIC,
                                  ALU.mult, ALU.add).then_inc(stat, 1)

            def layer_norm(n, par, src, done):
                for t in range(2):
                    ins = dve.tensor_scalar(xn[:, par, t, :], src[:, t, :], mv[:, par, t, 0:1],
                                            rs[:, par, 2, t:t + 1], ALU.subtract, ALU.mult)
                ins.then_inc(done, 1)

            def layer_norm_1(n, par, at):
                dve.wait_ge(root_done, n + 1)
                if not (isinstance(n, int) and n < 2):
                    dve.wait_ge(e_xt, n - 1)
                layer_norm(n, par, x[:, at, :, :], ln1)

            def layer_norm_2(n, par):
                if ln2:
                    dve.wait_ge(root_done, n + 2)
                    layer_norm(n, par, xn[:, par, :, :], ln2_done)

            def v_bias(b):
                dve.wait_ge(e_v, b + 1)
                if not (isinstance(b, int) and b == 0):
                    dve.wait_ge(v_lo, b)
                if bias:
                    dve.tensor_tensor(vt[:, :], ps_m[0:S, 0:HD], vbias[:, :], ALU.add).then_inc(vt_raw, 1)
                else:
                    dve.tensor_copy(vt[:, :], ps_m[0:S, 0:HD]).then_inc(vt_raw, 1)

            def k_block(b, T):
                dve.wait_ge(kt_hi, b + 1)
                if T is not None:
                    dve.wait_ge(e_s, T)
                for c in range(C):
                    ins = dve.tensor_tensor(kblk[0][:, c, :, :], spread(kt_part[0][:, c, :].unsqueeze(1), 1, HC),
                                            spread(head_mask[:, :].unsqueeze(2), 2, S), ALU.mult)
                ins.then_inc(kb_hi, 1)

            sc = ps_s[:, :, 0:4 * S].rearrange("p g (h s) -> p g h s", h=4)

            def shift(T, t):
                dve.wait_ge(e_s, T + 1)
                own.step(dve.tensor_reduce(negmax[:, :].rearrange("p (g h) -> p g h", h=4), sc, AX.X, ALU.max,
                                           negate=True))
                if not (isinstance(T, int) and T < 2):
                    dve.wait_ge(e_t, G * (T - 1))
                dve.tensor_tensor(prob[:, t, :, 0:S].rearrange("p (g h) s -> p g h s", h=4), sc,
                                  spread(negmax[:, :].rearrange("p (g h) -> p g h", h=4).unsqueeze(3), 3, S),
                                  ALU.add).then_inc(d_sub, 1)

            def prob_lo(T, par, t, half):
                for g in range(G // 2 * half, G // 2 * (half + 1)):
                    dve.wait_ge(t_hi, G * T + g + 1)
                    cols = slice(t * TOK, (t + 1) * TOK)
                    dve.tensor_tensor(pt[1][0:S, par, 4 * g:4 * g + 4, cols],
                                      ps_t[0:S, g % 2, :].rearrange("s (h q) -> s h q", h=4),
                                      pt[0][0:S, par, 4 * g:4 * g + 4, cols], ALU.subtract).then_inc(t_lo, 1)

            def recip_sum(T, par, t):
                if MANY:
                    dve.wait_ge(p_sum, T + 1)
                else:
                    dve.wait_ge(a_exp, T + 1)
                own.step(dve.tensor_reduce(rsum[:, par, t, :], half_sum[:, t, :, :] if MANY else prob[:, t, :, 0:S],
                                           AX.X, ALU.add))
                dve.reciprocal(rsum[:, par, t, :], rsum[:, par, t, :]).then_inc(d_r, 1)

            def normalize(n):
                dve.wait_ge(e_pv, n + 1)
                dve.wait_ge(rt_copied, n + 1)
                if not (isinstance(n, int) and n == 0):
                    dve.wait_ge(o_lo, n)
                dve.tensor_tensor(ot[:, :, :], ps_o[:, :, :], rt[:, :, :], ALU.mult).then_inc(o_raw, 1)

            def residual(n, at, times):
                dve.wait_ge(e_o, n + 1)
                if bias:
                    dve.wait_ge(r_biased, n + 1)
                else:
                    dve.wait_ge(r_in[at], 16 * times)
                src = ps_m[:, 0:2 * D].rearrange("p (t d) -> p t d", t=2)
                dve.scalar_tensor_tensor(out=res[:, at, :, :], in0=src, scalar=gate, in1=res[:, at, :, :],
                                         op0=ALU.mult, op1=ALU.add).then_inc(d_fin, 1)

            own.link(dve.memset(rs[:, :, :, :], 1.0))
            own.link(dve.memset(vpad[0][:, :].bitcast(F32), 0.0))
            own.link(dve.memset(vpad[1][:, :].bitcast(F32), 0.0))
            own.wait()
            dve.sem_inc(s_zeros, 1)
            ln_stats(0, 0, 0, 1, second=False)
            own.link(dve.memset(prob[:, :, :, S:S2], 0.0))
            layer_norm_1(0, 0, 0)
            dve.wait_ge(s_const, 1)
            k_block(0, None)
            if bias:
                dve.wait_ge(s_small, 16 * 4)
            v_bias(0)
            ln_stats(1, 1, 1, 1)
            layer_norm_2(0, 0)
            for i, (part, raw) in enumerate(((wq, wq_raw), (wo, wo_raw))):
                dve.wait_ge(w_hi, i + 1)
                dve.tensor_tensor(part[1][:, :, :], raw[:, :, :], part[0][:, :, :], ALU.subtract).then_inc(w_lo, 1)
            layer_norm_1(1, 1, 1)
            if ln2:
                ln_stats(2, 0, 2, 1)
            dve.memset(pt[0][S // 32 * 32:P, :, :, :].bitcast(F32), 0.0).then_inc(s_pt_zeros[0], 1)
            if Q_ON_DVE:
                q_low(dve, 0, 0)
            if ln2:
                layer_norm_1(2, 0, 2)
                layer_norm_2(1, 1)
            dve.wait_ge(s_pt_zeros[1], 1)

            def body(b, first):
                for p in range(PB):
                    n = PB * b + p
                    T = 2 * n
                    m = p + AHEAD
                    one_before, two_before = not first or p >= 1, not first or p >= 2
                    if two_before:
                        normalize(n - 2)
                    if one_before:
                        if not first or p >= 3:
                            dve.wait_ge(e_pv, n - 2)
                        prob_lo(T - 1, (p - 1) % 2, 1, 0)
                    shift(T, 0)
                    if one_before and MANY:
                        recip_sum(T - 1, (p - 1) % 2, 1)
                    if one_before:
                        prob_lo(T - 1, (p - 1) % 2, 1, 1)
                    ln_stats(n + AHEAD, m % 2, m % RING, b + 1 + m // RING)
                    if not MANY:
                        recip_sum(T, p % 2, 0)
                    if two_before:
                        residual(n - 2, (p - 2) % RING, b + p // 2)
                        dve.wait_ge(e_pv, n - 1)
                    prob_lo(T, p % 2, 0, 0)
                    shift(T + 1, 1)
                    if MANY:
                        recip_sum(T, p % 2, 0)
                    if p == PB - 1:
                        k_block(b + 1, 2 * n + 2)
                    if not MANY:
                        layer_norm_1(n + AHEAD, m % 2, m % RING)
                        layer_norm_2(n + 2, p % 2)
                        recip_sum(T + 1, p % 2, 1)
                        q_low(dve, n + 1, (p + 1) % 2)
                    prob_lo(T, p % 2, 0, 1)
                    if MANY:
                        layer_norm_1(n + AHEAD, m % 2, m % RING)
                    if p == 0 and not first:
                        v_bias(b)

            own.clear()
            batches(dve, body, own)
            n = NP
            normalize(n - 2)
            if MANY:
                recip_sum(2 * n - 1, (n - 1) % 2, 1)
            prob_lo(2 * n - 1, (n - 1) % 2, 1, 0)
            prob_lo(2 * n - 1, (n - 1) % 2, 1, 1)
            residual(n - 2, RING - 2, B)
            normalize(n - 1)
            residual(n - 1, RING - 1, B)


WCH = 1024


class FfnWeights:

    def __init__(self, w1T, w2T, h1T, h2T, w3T):
        self.K = {"w1": w1T.shape[0] // P, "w2": w2T.shape[0] // P, "h1": h1T.shape[0] // P,
                  "h2": h2T.shape[0] // P, "w3": w3T.shape[0] // P}
        self.src = []
        self.at = {}
        col = 0
        for name, w in (("w1", w1T), ("w2", w2T), ("h1", h1T), ("h2", h2T), ("w3", w3T)):
            self.at[name] = (col, w.shape[1])
            per = WCH // w.shape[1]
            for k in range(0, self.K[name], per):
                self.src.append(w[k * P:(k + per) * P, :].rearrange("(k p) n -> p k n", p=P))
            col += self.K[name] * w.shape[1]
        self.cols = col
        assert col == WCH * len(self.src)

    def chunk(self, w, name, k, a, b):
        at, width = self.at[name]
        return w[:, at + k * width + a:at + k * width + b]


def feed_forward(nc, ident, gate, x_src, x_dst, fw, w, scales, s3, exact, tag):
    BT = 4
    BLK = BT * TOK
    NB = x_src.shape[0] // BLK
    HC = fw.K["h1"]
    XR = 2
    xs = x_src.rearrange("(n t p) d -> n p t d", t=BT, p=P)
    xd = x_dst.rearrange("(n t p) d -> n p t d", t=BT, p=P)
    ADT = F32R if exact else F32
    PARTS = 2 if exact else 1
    U = 2 * HC

    with semaphores(nc, tag) as sem, ExitStack() as ctx:
        def sb(name, shape, dt=F32):
            return ctx.enter_context(nc.sbuf_tensor(f"{tag}_{name}", shape, dt))

        x = sb("x", [P, XR, BT, D])
        stats = sb("stats", [P, BT, 6])
        mv = sb("mv", [P, BT, 2])
        rs = sb("rs", [P, 4, BT])
        xn = sb("xn", [P, BT, D])
        xt = sb("xt", [P, DC, BLK]) if exact else None
        xt_part = [sb(f"xt_part{i}", [P, DC, BLK], ADT) for i in range(PARTS)]
        silu = sb("silu", [P, 2, BLK])
        raw = sb("raw", [P, 2, BLK]) if exact else None
        ha = [sb(f"ha{i}", [P, HC, BLK], ADT) for i in range(PARTS)]
        hb = [sb(f"hb{i}", [P, HC, BLK], ADT) for i in range(PARTS)]
        y = sb("y", [P, 2, 2, D])
        ps = ctx.enter_context(nc.psum_tensor(f"{tag}_ps", [P, 4, 512], F32))
        ps_x = ctx.enter_context(nc.psum_tensor(f"{tag}_ps_x", [P, DC, BLK], F32))
        ps_y = ctx.enter_context(nc.psum_tensor(f"{tag}_ps_y", [P, BT, D], F32))

        x_in = [sem(f"x_in{i}") for i in range(XR)]
        x_out = [sem(f"x_out{i}") for i in range(XR)]
        stat, ln, e_xt, xt_raw, xt_hi, xt_lo = (sem(n) for n in ("stat", "ln", "pe_xt", "xt_raw", "s_xt_hi", "s_xt_lo"))
        e_a, a_silu, a_raw, a_hi, a_lo = (sem(n) for n in ("pe_a", "a_silu", "a_raw", "a_hi", "a_lo"))
        e_u, u_raw, u_hi, u_lo = (sem(n) for n in ("pe_u", "u_raw", "u_hi", "u_lo"))
        e_y, d_y, rooted = sem("pe_y"), sem("y_done"), sem("root")
        own_v, own_a, own_p = sem("own_v"), sem("own_a"), sem("own_p")
        if not exact:
            xt_lo, a_lo, u_lo = xt_raw, a_raw, u_raw

        def blocks(eng, body, own=None, end=NB // XR):
            def pair(i, first):
                for u in range(XR):
                    body(XR * i + u, u, i, first and u == 0)
                if own:
                    own.clear()

            pair(0, True)
            with eng.Fori(1, end) as i:
                pair(i, False)

        block = ctx.enter_context(nc.Block())

        @block.sync
        def _(sp):
            def load(b, at):
                sp.dma_start(x[:, at, :, :], xs[b]).then_inc(x_in[at], 16)

            def body(b, u, i, first, ahead=None):
                if not first:
                    sp.wait_ge(x_out[1 - u], 16 * (i + u))
                load(b + 1 if ahead is None else ahead, 1 - u)
                sp.wait_ge(d_y, 2 * b + 2)
                sp.dma_start(xd[b], x[:, u, :, :]).then_inc(x_out[u], 16)

            load(0, 0)
            blocks(sp, body, end=NB // XR - 1)
            i = NB // XR - 1
            body(NB - 2, 0, i, False)
            body(NB - 1, 1, i, False, ahead=0)
            for u in range(XR):
                sp.wait_ge(x_out[u], 16 * (NB // XR))

        @block.tensor
        def _(pe):
            def x_transpose(b):
                pe.wait_ge(ln, b + 1)
                for c in range(DC):
                    for t in range(BT):
                        mm = pe.transpose(ps_x[:, c, t * TOK:(t + 1) * TOK], xn[:, t, c * P:(c + 1) * P], ident[:, :])
                mm.then_inc(e_xt, 1)

            def product(out, name, j, parts, ready=None):
                K = fw.K[name]
                for k in range(K):
                    if ready is not None:
                        for s, v in ready(k):
                            pe.wait_ge(s, v)
                    for i, a in enumerate(parts):
                        mm = pe.matmul(out, fw.chunk(w, name, k, j * P, (j + 1) * P), a[:, k, :],
                                       start=k == 0 and i == 0, stop=k == K - 1 and i == len(parts) - 1)
                return mm

            pe.wait_ge(ln, 1)
            x_transpose(0)

            def body(b, u_, i_, first):
                for j in range(HC):
                    if j == 0:
                        pe.wait_ge(xt_hi if exact else xt_raw, b + 1)
                        pe.wait_ge(xt_lo, b + 1)
                    if j >= 2:
                        pe.wait_ge(a_raw, HC * b + j - 1)
                    elif not first:
                        pe.wait_ge(u_raw, U * b)
                    product(ps[:, 2 * (j % 2), :], "w1", j, xt_part)
                    product(ps[:, 2 * (j % 2) + 1, :], "w2", j, xt_part).then_inc(e_a, 1)
                for u in range(U):
                    if u < 4:
                        pe.wait_ge(a_raw, HC * b + HC - 1 + u // 2)
                    else:
                        pe.wait_ge(u_raw, U * b + u - 3)
                    if u < HC:
                        ready = (lambda k: ((a_hi if exact else a_raw, HC * b + k + 1), (a_lo, HC * b + k + 1)))
                        product(ps[:, u % 4, :], "h1", u, ha, ready if u == 0 else None).then_inc(e_u, 1)
                    else:
                        ready = (lambda k: ((u_hi if exact else u_raw, U * b + k + 1), (u_lo, U * b + k + 1)))
                        product(ps[:, u % 4, :], "h2", u - HC, hb, ready if u == HC else None).then_inc(e_u, 1)
                pe.wait_ge(xt_raw, b + 1)
                x_transpose(b + 1)
                for half in range(2):
                    if half == 0 and not first:
                        pe.wait_ge(d_y, 2 * b)
                    for t in range(2 * half, 2 * half + 2):
                        for k in range(HC):
                            if t == 0:
                                pe.wait_ge(u_hi if exact else u_raw, U * b + HC + k + 1)
                                pe.wait_ge(u_lo, U * b + HC + k + 1)
                            for i, a in enumerate(ha):
                                mm = pe.matmul(ps_y[:, t, :], a[:, k, t * TOK:(t + 1) * TOK],
                                               fw.chunk(w, "w3", k, 0, D), start=k == 0 and i == 0,
                                               stop=k == HC - 1 and i == PARTS - 1)
                    mm.then_inc(e_y, 1)

            blocks(pe, body)

        @block.scalar
        def _(act):
            own = Own(act, own_a)

            def x_out_of_psum(b):
                act.wait_ge(e_xt, b + 1)
                if exact:
                    if not (isinstance(b, int) and b == 0):
                        act.wait_ge(xt_lo, b)
                    act.activation(xt[:, :, :], ps_x[:, :, :], ACT.Copy).then_inc(xt_raw, 1)
                    act.wait_ge(xt_raw, b + 1)
                    act.activation(xt_part[0][:, :, :], xt[:, :, :], ACT.Copy).then_inc(xt_hi, 1)
                else:
                    act.activation(xt_part[0][:, :, :], ps_x[:, :, :], ACT.Copy).then_inc(xt_raw, 1)

            def a_high(b, j):
                if exact:
                    act.wait_ge(a_raw, HC * b + j + 1)
                    act.activation(ha[0][:, j, :], raw[:, j % 2, :], ACT.Copy).then_inc(a_hi, 1)

            x_out_of_psum(0)

            def body(b, u_, i_, first):
                for j in range(HC):
                    act.wait_ge(e_a, HC * b + j + 1)
                    if not (first and j < 2):
                        act.wait_ge(a_raw, HC * b + j - 1)
                    act.activation(silu[:, j % 2, :], ps[:, 2 * (j % 2), :], ACT.Silu,
                                   scale=scales[:, 0, j:j + 1]).then_inc(a_silu, 1)
                    if j:
                        a_high(b, j - 1)
                a_high(b, HC - 1)
                for u in range(U):
                    act.wait_ge(e_u, U * b + u + 1)
                    dst = (hb if u < HC else ha)[0][:, u % HC, :]
                    scale = scales[:, 2 + u // HC, u % HC:u % HC + 1]
                    if not exact:
                        act.activation(dst, ps[:, u % 4, :], ACT.Gelu, scale=scale).then_inc(u_raw, 1)
                        continue
                    if u < 2:
                        act.wait_ge(a_lo, HC * b + HC - 1 + u)
                    else:
                        act.wait_ge(u_lo, U * b + u - 1)
                    act.activation(raw[:, u % 2, :], ps[:, u % 4, :], ACT.Gelu, scale=scale).then_inc(u_raw, 1)
                    act.wait_ge(u_raw, U * b + u + 1)
                    act.activation(dst, raw[:, u % 2, :], ACT.Copy).then_inc(u_hi, 1)
                x_out_of_psum(b + 1)

            blocks(act, body, own)

        @block.gpsimd
        def _(pool):
            own = Own(pool, own_p)

            def root(b):
                pool.wait_ge(stat, b + 1)
                newton(own, pool, rs[:, 1, :], rs[:, 2, :], rs[:, 3, :])
                pool.sem_inc(rooted, 1)

            def x_low(b):
                if exact:
                    pool.wait_ge(xt_hi, b + 1)
                    pool.tensor_tensor(xt_part[1][:, :, :], xt[:, :, :], xt_part[0][:, :, :],
                                       ALU.subtract).then_inc(xt_lo, 1)

            root(0)
            x_low(0)

            def body(b, u, i, first):
                root(b + 1)
                x_low(b + 1)

            own.clear()
            blocks(pool, body, own)

        @block.vector
        def _(dve):
            own = Own(dve, own_v)

            def ln_stats(b, at, times):
                dve.wait_ge(x_in[at], 16 * times)
                if not (isinstance(b, int) and b == 0):
                    dve.wait_ge(ln, b)
                for t in range(BT):
                    own.link(dve.bn_stats(stats[:, t, :], x[:, at, t, :]))
                own.wait()
                for t in range(BT):
                    own.link(dve.bn_aggr(mv[:, t, :], stats[:, t, :]))
                own.wait()
                rsqrt_guess(own, dve, mv[:, :, 1], rs[:, 0, :], rs[:, 1, :], rs[:, 2, :])
                dve.tensor_scalar(rs[:, 2, :].bitcast(I32), rs[:, 2, :].bitcast(I32), -1, RSQRT_MAGIC,
                                  ALU.mult, ALU.add).then_inc(stat, 1)

            def layer_norm(b, at):
                dve.wait_ge(rooted, b + 1)
                if not (isinstance(b, int) and b == 0):
                    dve.wait_ge(e_xt, b)
                for t in range(BT):
                    ins = dve.tensor_scalar(xn[:, t, :], x[:, at, t, :], mv[:, t, 0:1], rs[:, 2, t:t + 1],
                                            ALU.subtract, ALU.mult)
                ins.then_inc(ln, 1)

            def a_low(b, j):
                if exact:
                    dve.wait_ge(a_hi, HC * b + j + 1)
                    dve.tensor_tensor(ha[1][:, j, :], raw[:, j % 2, :], ha[0][:, j, :],
                                      ALU.subtract).then_inc(a_lo, 1)

            ln_stats(0, 0, 1)
            layer_norm(0, 0)

            def body(b, u_, i, first):
                for j in range(HC):
                    if j >= 2 or not first:
                        if exact and j >= 2:
                            dve.wait_ge(a_lo, HC * b + j - 1)
                    dve.wait_ge(a_silu, HC * b + j + 1)
                    dst = raw[:, j % 2, :] if exact else ha[0][:, j, :]
                    dve.scalar_tensor_tensor(out=dst, in0=ps[:, 2 * (j % 2) + 1, :], scalar=scales[:, 1, j:j + 1],
                                             in1=silu[:, j % 2, :], op0=ALU.mult, op1=ALU.mult).then_inc(a_raw, 1)
                    if j:
                        a_low(b, j - 1)
                a_low(b, HC - 1)
                for u in range(U):
                    if exact:
                        dve.wait_ge(u_hi, U * b + u + 1)
                        dst = (hb if u < HC else ha)[1][:, u % HC, :]
                        hi = (hb if u < HC else ha)[0][:, u % HC, :]
                        dve.tensor_tensor(dst, raw[:, u % 2, :], hi, ALU.subtract).then_inc(u_lo, 1)
                    if u == HC // 2:
                        ln_stats(b + 1, 1 - u_, i + 1 if u_ == 0 else i + 2)
                    if u == HC:
                        layer_norm(b + 1, 1 - u_)
                for half in range(2):
                    t = slice(2 * half, 2 * half + 2)
                    dve.wait_ge(e_y, 2 * b + half + 1)
                    if not first:
                        dve.wait_ge(d_y, 2 * b + half - 1)
                    own.step(dve.tensor_tensor(y[:, half, :, :], ps_y[:, t, :], spread(s3[:, :].unsqueeze(1), 1, 2), ALU.mult))
                    dve.scalar_tensor_tensor(out=x[:, u_, t, :], in0=y[:, half, :, :], scalar=gate, in1=x[:, u_, t, :],
                                             op0=ALU.mult, op1=ALU.add).then_inc(d_y, 1)

            own.clear()
            blocks(dve, body, own)


def self_attention(nc, ident, gate, x_src, x_dst, wq_src, wk_src, wv_src, ws_src, wo_src, bo_src, B, H, topk):
    N = x_src.shape[0] // B
    NT = N // TOK
    KC = N // P
    HD = wq_src.shape[1]
    dh = HD // H
    CP = H // 2
    PT_ = NT // 2
    SLOTS = H * NT
    UNITS = SLOTS // 2
    PS = 2 * NT
    SCALE = float(dh) ** -0.5
    assert dh == 64 and N == 1024 and DC == 2

    xb_src = x_src.rearrange("(b t p) d -> b p t d", b=B, p=P)
    xb_dst = x_dst.rearrange("(b t p) d -> b p t d", b=B, p=P)
    xp_src = x_src.rearrange("(b q t p) d -> b q p t d", b=B, t=2, p=P)

    items = []
    for c in range(CP):
        s = PS * c
        if c:
            items += [(s + 2, "r", (c - 1, 0)), (s + 3, "r", (c - 1, 1))]
        items += [(s + 5, "k", (c, 0)), (s + 7, "k", (c, 1))]
        items += [(s + 9, "q", (c, 0)), (s + 10, "q", (c, 1))]
        items += [(s + 11, "v", (c, 0)), (s + 12, "v", (c, 1))]
    items += [(PS, "h", 0), (PS + 1, "h", 1), (13, "x", 0), (14, "g", 0), (15, "x", 1), (PS + 4, "g", 1),
              (PS + 13, "x", 2), (PS + 14, "g", 2), (PS + 15, "x", 3), (2 * PS + 4, "g", 3)]
    items.sort(key=lambda i: i[0])
    items += [(SLOTS + i, "r", (CP - 1, i)) for i in range(2)] + [(SLOTS + 2 + i, "o", i) for i in range(PT_)]
    AT = {}
    for m, (slot, _, _) in enumerate(items):
        assert slot not in AT
        AT[slot] = m
    M = len(items)
    READS_ACT = ("k", "q", "v", "x", "g", "h")
    READS_DVE = ("k", "q", "v", "r", "o")
    ln_at = {5: 0, 9: 1, PS + 5: 2, PS + 9: 3}

    SPLIT_AT = 2

    def count(kinds, m):
        return sum(kind in kinds for _, kind, _ in items[:m])

    ACT_M, DVE_M = count(READS_ACT, M), count(READS_DVE, M)
    R_M = 2 * CP

    with semaphores(nc, "E") as sem, ExitStack() as ctx:
        def sb(name, shape, dt=F32):
            return ctx.enter_context(nc.sbuf_tensor(f"E_{name}", shape, dt))

        xp = sb("xp", [P, 2, 2, D])
        stats = sb("stats", [P, 2, 6])
        mv = sb("mv", [P, 2, 2, 2])
        rs = sb("rs", [P, 2, 4, 2])
        xn = sb("xn", [P, 2, 2, D])
        xt = sb("xt", [P, DC, N])
        xb = xt[:, :, :].rearrange("p k n -> p (k n)").rearrange("p (t d) -> p t d", d=D)
        xt_part = [sb("xt_hi", [P, DC, N], F32R), sb("xt_lo", [P, DC, N], F32R)]
        w_raw = sb("w_raw", [P, 3, DC, P])
        wq = [sb("wq_hi", [P, DC, P], F32R), sb("wq_lo", [P, DC, P], F32R)]
        wk = [sb("wk_hi", [P, DC, P], F32R), sb("wk_lo", [P, DC, P], F32R)]
        wv = [sb("wv_hi", [P, DC, P], F32R), sb("wv_lo", [P, DC, P], F32R)]
        wo = [sb("wo_hi", [P, CP, D], F32R), sb("wo_lo", [P, CP, D], F32R)]
        ws = sb("ws", [P, DC, H])
        bo = sb("bo", [H, D])
        kk = sb("kk", [P, 2, 2, N], F32R)
        qq = [sb("q_hi", [P, 2, 2, N], F32R), sb("q_lo", [P, 2, 2, N], F32R)]
        vv = sb("vv", [P, 2, KC, 2, P], F32R)
        prob = sb("prob", [P, 2, N])
        pt = [sb("pt_hi", [P, 2, KC, PAIR], F32R), sb("pt_lo", [P, 2, KC, PAIR], F32R)]
        negmax = sb("negmax", [P, 4])
        den = sb("den", [P, H, NT])
        wgt = sb("wgt", [P, 2, NT])
        wwide = sb("wwide", [P, 2, NT // 2, P])
        ot_other = sb("ot_other", [P, PAIR])
        ot_raw = sb("ot_raw", [P, N])
        wo_raw = ot_raw[:, :].rearrange("p (c d) -> p c d", d=D)
        ot = sb("ot", [P, 2, 512])
        o_part = [sb("o_hi", [P, CP, N], F32R), sb("o_lo", [P, CP, N], F32R)]
        logit = sb("logit", [P, NT, H])
        score = sb("score", [P, NT, H])
        before, equal = (wwide[:, :, :, :].rearrange("p n t w -> p (n t w)")[:, i * NT * H * H:(i + 1) * NT * H * H]
                         .rearrange("p (t i j) -> p t i j", i=H, j=H) for i in range(2))
        rank = sb("rank", [P, NT, H])
        one = sb("one", [P, 1])
        lower = sb("lower", [P, H, H])
        chosen = sb("chosen", [P, NT, H])
        chosenT = sb("chosenT", [H, NT, TOK])

        ps_s = ctx.enter_context(nc.psum_tensor("E_ps_s", [P, 2, N], F32))
        ps_t = ctx.enter_context(nc.psum_tensor("E_ps_t", [P, 2, 4, TOK], F32))
        ps_o = ctx.enter_context(nc.psum_tensor("E_ps_o", [P, 2, PAIR], F32))
        ps_m = ctx.enter_context(nc.psum_tensor("E_ps_m", [P, 512], F32))

        w_in, xb_in, xb_out, small = sem("w_in"), sem("xb_in"), sem("xb_out"), sem("small")
        wo_in, xb_free = sem("wo_in"), sem("xb_free")
        xp_in = [sem("xp_in0"), sem("xp_in1")]
        w_hi, w_lo, wo_hi, wo_lo = sem("s_w_hi"), sem("s_w_lo"), sem("s_wo_hi"), sem("s_wo_lo")
        stat, rooted, ln = sem("stat"), sem("root"), sem("ln")
        c_hi, c_lo = sem("convert_hi"), sem("convert_lo")
        e_s, e_t, e_pv, e_m = sem("pe_s"), sem("pe_t"), sem("pe_pv"), sem("pe_item")
        m_act, m_dve = sem("item_act"), sem("item_dve")
        d_max, a_exp, t_hi, t_lo = sem("max"), sem("exp"), sem("t_hi"), sem("t_lo")
        o_other, o_sum, d_wgt, p_wide = sem("o_other"), sem("o_sum"), sem("wgt"), sem("wide")
        o_hi, o_lo = sem("s_o_hi"), sem("s_o_lo")
        a_gate, d_chosen, s_lower = (sem(n) for n in (
            "a_gate", "chosen_done", "lower_made"))
        q_both = sem("q_both")
        batch_done, o_read = sem("batch_done"), sem("o_read")
        pre_pe, pre_act, pre_hi, pre_dve = sem("pre_pe"), sem("pre_act"), sem("pre_hi"), sem("pre_dve")
        own_v, own_a, own_p = sem("own_v"), sem("own_a"), sem("own_p")

        def batches(eng, body, own=None, waits=True):
            if own:
                own.clear()
            with eng.Fori(0, B) as b:
                if waits:
                    eng.wait_ge(batch_done, b + 1)
                body(b)
                if own:
                    own.clear()

        def head(v):
            return v // NT

        banks = (ps_m[:, :], ps_t[:, 0, :, :].rearrange("p t q -> p (t q)"),
                 ps_t[:, 1, :, :].rearrange("p t q -> p (t q)"), ps_o[:, :, :].rearrange("p t q -> p (t q)"))

        def bank(kind, arg):
            if kind == "o":
                return banks[arg]
            return banks[1] if (kind, arg) == ("r", (CP - 1, 1)) else banks[0]

        def r_item(c, n):
            return AT[(PS * (c + 1) + 2 if c < CP - 1 else SLOTS) + n]

        def at_x(q):
            return [m for m, (_, kind, arg) in enumerate(items) if kind == "x" and arg == q][0]

        first_items = [(kind, (n,)) for n in range(2) for kind in "kqv"]

        block = ctx.enter_context(nc.Block())

        @block.sync
        def _(sp):
            def load_w(c):
                for i, w in enumerate((wq_src, wk_src, wv_src)):
                    sp.dma_start(w_raw[:, i, :, :], w[:, c * P:(c + 1) * P].rearrange("(k p) n -> p k n", p=P)
                                 ).then_inc(w_in, 16)

            def load_xp(b, q):
                sp.dma_start(xp[:, q % 2, :, :], xp_src[b, q]).then_inc(xp_in[q % 2], 16)

            for q in range(2):
                load_xp(0, q)
            load_w(0)
            sp.dma_start(ws[:, :, :], ws_src.rearrange("(k p) n -> p k n", p=P)).then_inc(small, 16)
            sp.dma_start(bo[:, :], bo_src).then_inc(small, 16)
            for q in range(2, PT_):
                sp.wait_ge(ln, q - 1)
                load_xp(0, q)
            sp.dma_start(wo_raw, wo_src.rearrange("(c p) n -> p c n", p=P)).then_inc(wo_in, 16)
            sp.wait_ge(w_lo, 1)
            load_w(1)

            def body(b, ahead):
                sp.wait_ge(batch_done, b + 1)
                for c in range(CP):
                    if c < 2:
                        for q in (2 * c, 2 * c + 1):
                            sp.wait_ge(ln, PT_ * b + PT_ + q - 1)
                            load_xp(ahead, q)
                    sp.wait_ge(w_lo, CP * b + c + 2)
                    if not (isinstance(b, int) and c == CP - 1):
                        load_w((c + 2) % CP)
                sp.wait_ge(c_lo, PT_ * b + 2 * PT_)
                sp.dma_start(xb, xb_src[b]).then_inc(xb_in, 16)
                for q in range(PT_):
                    sp.wait_ge(m_dve, DVE_M * b + DVE_M - PT_ + q + 1)
                    sp.dma_start(xb_dst[b][:, 2 * q:2 * q + 2, :], xb[:, 2 * q:2 * q + 2, :]).then_inc(xb_out, 16)
                sp.wait_ge(xb_out, 16 * PT_ * b + 16 * PT_)
                sp.sem_inc(xb_free, 1)

            sp.sem_inc(xb_free, 1)
            with sp.Fori(0, B - 1) as b:
                body(b, b + 1)
            body(B - 1, 0)

        @block.tensor
        def _(pe):
            def item(m, b):
                slot, kind, arg = items[m]
                if slot > SLOTS:
                    if kind == "o" and arg < 2:
                        pe.wait_ge(m_dve, DVE_M * b + count(READS_DVE, AT[SLOTS] + 1 + arg))
                elif m:
                    prev = items[m - 1][1]
                    if prev in READS_DVE:
                        pe.wait_ge(m_dve, DVE_M * b + count(READS_DVE, m))
                    else:
                        pe.wait_ge(m_act, ACT_M * b + count(READS_ACT, m))
                run(kind, arg, b).then_inc(e_m, 1)

            def run(kind, arg, b):
                if kind in "kqv":
                    c = arg[0]
                    if arg[1:] in ((0,), (0, 0)) and kind == "k":
                        pe.wait_ge(w_hi, CP * b + c + 2)
                        pe.wait_ge(w_lo, CP * b + c + 2)
                        if c == CP - 1:
                            pe.wait_ge(c_hi, PT_ * b + 2 * PT_)
                            pe.wait_ge(c_lo, PT_ * b + 2 * PT_)
                    return {"k": k_proj, "q": q_proj, "v": v_proj}[kind](*arg[1:])
                if kind == "x":
                    return x_transpose(arg, PT_ * b + PT_ + arg + 1)
                if kind == "g":
                    return logits(arg)
                if kind == "h":
                    pe.wait_ge(d_chosen, b + 1)
                    for t in range(4):
                        mm = pe.transpose(ps_m[0:H, t * TOK:(t + 1) * TOK], chosen[:, 4 * arg + t, :], ident[:, :])
                    return mm
                if kind == "r":
                    c, n = arg
                    pe.wait_ge(p_wide, R_M * b + 2 * c + n + 1)
                    for t in range(4):
                        mm = pe.transpose(bank(kind, arg)[:, t * TOK:(t + 1) * TOK], wwide[:, n, t, :], ident[:, :])
                    return mm
                if arg % 2 == 0:
                    pe.wait_ge(o_hi, R_M * b + R_M - 1 + arg // 2)
                    pe.wait_ge(o_lo, R_M * b + R_M - 1 + arg // 2)
                for t in range(2):
                    tile = 2 * arg + t
                    cols = slice(tile * TOK, (tile + 1) * TOK)
                    out = bank(kind, arg)[:, t * D:(t + 1) * D]
                    pe.matmul(out, chosenT[:, tile, :], bo[:, :], start=True, stop=False)
                    i = 0
                    for c in range(CP):
                        for a, w in split_passes(o_part, wo):
                            i += 1
                            mm = pe.matmul(out, a[:, c, cols], w[:, c, :], start=False, stop=i == 3 * CP)
                return mm

            def x_transpose(q, done, out=ps_m):
                pe.wait_ge(ln, done)
                for k in range(DC):
                    for t in range(2):
                        at = k * PAIR + t * TOK
                        mm = pe.transpose(out[:, at:at + TOK], xn[:, q % 2, t, k * P:(k + 1) * P], ident[:, :])
                return mm

            def logits(q, at=0):
                for t in range(2):
                    for k in range(DC):
                        cols = slice((2 * q + t) * TOK, (2 * q + t + 1) * TOK)
                        mm = pe.matmul(ps_m[:, (at + t) * H:(at + t + 1) * H], xt[:, k, cols], ws[:, k, :],
                                       start=k == 0, stop=k == DC - 1)
                return mm

            def k_proj(n, out=ps_m):
                for i, (k, (w, a)) in enumerate((k, x) for k in range(DC) for x in split_passes(wk, xt_part)):
                    mm = pe.matmul(out[:, :], w[:, k, :], a[:, k, n * 512:(n + 1) * 512], start=i == 0,
                                   stop=i == 3 * DC - 1)
                return mm

            def q_proj(n, out=ps_m):
                for i, (k, (w, a)) in enumerate((k, x) for k in range(DC) for x in split_passes(wq, xt_part)):
                    mm = pe.matmul(out[:, :], w[:, k, :], a[:, k, n * 512:(n + 1) * 512], start=i == 0,
                                   stop=i == 3 * DC - 1)
                return mm

            def v_proj(n, out=ps_m):
                for t in range(4):
                    cols = slice((4 * n + t) * TOK, (4 * n + t + 1) * TOK)
                    for i, (k, (a, w)) in enumerate((k, x) for k in range(DC) for x in split_passes(xt_part, wv)):
                        mm = pe.matmul(out[:, t * P:(t + 1) * P], a[:, k, cols], w[:, k, :], start=i == 0,
                                       stop=i == 3 * DC - 1)
                return mm

            def scores(v):
                j, cp, cols = head(v) % 2, (head(v) // 2) % 2, slice((v % NT) * TOK, (v % NT + 1) * TOK)
                for n in range(2):
                    for i in range(2):
                        mm = pe.matmul(ps_s[:, v % 2, n * 512:(n + 1) * 512], qq[i][:, cp, j, cols],
                                       kk[:, cp, j, n * 512:(n + 1) * 512], start=i == 0, stop=i == 1)
                mm.then_inc(e_s, 1)

            def p_transpose(v, b):
                for g in range(2):
                    if v:
                        pe.wait_ge(t_lo, 2 * SLOTS * b + 2 * (v - 1) + g + 1)
                    for i in range(4):
                        at = (4 * g + i) * P
                        mm = pe.transpose(ps_t[:, g, i, :], prob[:, v % 2, at:at + P], ident[:, :])
                    mm.then_inc(e_t, 1)

            def pv(u, half, b):
                h = u // PT_
                pe.wait_ge(t_lo, 2 * SLOTS * b + 4 * u + 3 + half)
                if u and half == 0:
                    pe.wait_ge(o_sum, UNITS * b + u)
                for i in range(KC // 2 * half, KC // 2 * (half + 1)):
                    for n, a in enumerate(pt):
                        mm = pe.matmul(ps_o[:, u % 2, :], vv[:, (h // 2) % 2, i, h % 2, :], a[:, u % 2, i, :],
                                       start=i == 0 and n == 0, stop=i == KC - 1 and n == 1)
                if half:
                    mm.then_inc(e_pv, 1)

            for q in range(PT_):
                x_transpose(q, q + 1, banks[q]).then_inc(pre_pe, 1)
            pe.wait_ge(w_hi, 1)
            pe.wait_ge(w_lo, 1)
            for i, (f, arg) in enumerate(first_items):
                if f == "k":
                    pe.wait_ge(c_hi, PT_ // 2 * (arg[0] + 1))
                    pe.wait_ge(c_lo, PT_ // 2 * (arg[0] + 1))
                if i < 4:
                    pe.wait_ge(pre_act, i + 1)
                else:
                    pe.wait_ge(pre_dve, i - 3)
                {"k": k_proj, "q": q_proj, "v": v_proj}[f](*arg, out=banks[i % 4]).then_inc(pre_pe, 1)
            pe.wait_ge(small, 32)
            pe.wait_ge(pre_dve, (len(first_items) - 1) // 4 * 4 + 1)
            for q in range(PT_):
                mm = logits(q, 2 * q)
            mm.then_inc(pre_pe, 1)

            def ready(v, b):
                if v % PS == 0 and v:
                    m = AT[v - PS + 10] + 1
                    pe.wait_ge(m_dve, DVE_M * b + count(READS_DVE, m))
                    pe.wait_ge(q_both, 2 * CP * b + 2 * (v // PS) + 2)

            def body(b):
                for v in range(SLOTS):
                    pe.wait_ge(a_exp, SLOTS * b + v + 1)
                    if v + 2 < SLOTS:
                        ready(v + 2, b)
                        scores(v + 2)
                    if v == 0:
                        pe.wait_ge(o_read, b + 1)
                    p_transpose(v, b)
                    if v >= 2:
                        u = v // 2 - 1
                        if u % (2 * PT_) == 0 and u and v % 2 == 0:
                            m = AT[2 * u - PS + 12] + 1
                            pe.wait_ge(m_dve, DVE_M * b + count(READS_DVE, m))
                        pv(u, v % 2, b)
                    if v in AT:
                        item(AT[v], b)
                for half in range(2):
                    pv(UNITS - 1, half, b)
                for m in (AT[SLOTS], AT[SLOTS] + 1):
                    item(m, b)
                pe.wait_ge(q_both, 2 * CP * b + 2 * CP + 2)
                scores(0)
                scores(1)
                for m in range(AT[SLOTS] + 2, M):
                    item(m, b)

            pe.wait_ge(pre_dve, len(first_items))
            pe.wait_ge(q_both, 2)
            scores(0)
            scores(1)
            pe.wait_ge(pre_act, PT_ + 1)
            pe.wait_ge(wo_hi, 1)
            pe.wait_ge(wo_lo, 1)
            batches(pe, body)

        def act_item(act, kind, arg, ready, done, par, src=ps_m):
            ready()
            if kind == "k":
                cols = slice(arg[-1] * 512, arg[-1] * 512 + 512)
                act.activation(kk[0:64, par, 0, cols], src[0:64, :], ACT.Copy)
                ins = act.activation(kk[64:P, par, 1, cols], src[64:P, :], ACT.Copy)
            elif kind == "q":
                cols = slice(arg[-1] * 512, arg[-1] * 512 + 512)
                act.activation(qq[0][0:64, par, 0, cols], src[0:64, :], ACT.Copy, scale=SCALE)
                ins = act.activation(qq[0][64:P, par, 1, cols], src[64:P, :], ACT.Copy, scale=SCALE)
            elif kind == "v":
                n = arg[-1]
                ins = act.activation(vv[:, par, 4 * n:4 * n + 4, :, 0:dh],
                                     src[:, :].rearrange("p (t j w) -> p t j w", t=4, j=2), ACT.Copy)
            elif kind == "x":
                ins = act.activation(xt[:, :, arg * PAIR:(arg + 1) * PAIR],
                                     src[:, :].rearrange("p (k q) -> p k q", k=DC), ACT.Copy)
            elif kind == "h":
                ins = act.activation(chosenT[:, 4 * arg:4 * arg + 4, :],
                                     src[0:H, :].rearrange("h (t q) -> h t q", t=4), ACT.Copy)
            else:
                ins = act.activation(logit[:, 2 * arg:2 * arg + 2, :],
                                     src[:, 0:2 * H].rearrange("p (t h) -> p t h", t=2), ACT.Copy)
            ins.then_inc(done, 1)

        def dve_item(dve, kind, arg, done, par, src=ps_m):
            if kind == "k":
                cols = slice(arg[-1] * 512, arg[-1] * 512 + 512)
                dve.tensor_tensor(kk[64:P, par, 0, cols], src[0:64, :], kk[0:64, par, 0, cols], ALU.subtract)
                ins = dve.tensor_tensor(kk[0:64, par, 1, cols], src[64:P, :], kk[64:P, par, 1, cols], ALU.subtract)
            elif kind == "q":
                cols = slice(arg[-1] * 512, arg[-1] * 512 + 512)
                for j, rows in enumerate((slice(0, 64), slice(64, P))):
                    ins = dve.scalar_tensor_tensor(out=qq[1][rows, par, j, cols], in0=src[rows, :], scalar=SCALE,
                                                   in1=qq[0][rows, par, j, cols], op0=ALU.mult, op1=ALU.subtract)
            else:
                n = arg[-1]
                ins = dve.tensor_tensor(vv[:, par, 4 * n:4 * n + 4, :, dh:P],
                                        src[:, :].rearrange("p (t j w) -> p t j w", t=4, j=2),
                                        vv[:, par, 4 * n:4 * n + 4, :, 0:dh], ALU.subtract)
            ins.then_inc(done, 1)

        @block.scalar
        def _(act):
            own = Own(act, own_a)

            def split_weights(n):
                act.wait_ge(w_in, 48 * n)
                act.activation(wq[0][:, :, :], w_raw[:, 0, :, :], ACT.Copy)
                act.activation(wk[0][:, :, :], w_raw[:, 1, :, :], ACT.Copy)
                act.activation(wv[0][:, :, :], w_raw[:, 2, :, :], ACT.Copy).then_inc(w_hi, 1)

            def convert(q):
                cols = slice(q * PAIR, (q + 1) * PAIR)
                act.activation(xt_part[0][:, :, cols], xt[:, :, cols], ACT.Copy).then_inc(c_hi, 1)

            def exp(v, b):
                act.wait_ge(d_max, SLOTS * b + v + 1)
                if v >= 2:
                    act.wait_ge(e_t, 2 * SLOTS * b + 2 * (v - 1))
                act.activation(prob[:, v % 2, :], ps_s[:, v % 2, :], ACT.Exp, bias=negmax[:, v % 4:v % 4 + 1],
                               scale=1.0, accum_out=den[:, head(v), v % NT:v % NT + 1]).then_inc(a_exp, 1)

            def prob_hi(v, b):
                u = v // 2
                if u >= 2 and v % 2 == 0:
                    act.wait_ge(e_pv, UNITS * b + u - 1)
                for g in range(2):
                    act.wait_ge(e_t, 2 * SLOTS * b + 2 * v + g + 1)
                    act.activation(pt[0][:, u % 2, 4 * g:4 * g + 4, (v % 2) * TOK:(v % 2 + 1) * TOK],
                                   ps_t[:, g, :, :], ACT.Copy).then_inc(t_hi, 1)

            def other_half(u, b):
                act.wait_ge(e_pv, UNITS * b + u + 1)
                if u:
                    act.wait_ge(o_sum, UNITS * b + u)
                if (u // PT_) % 2 == 0:
                    ins = act.activation(ot_other[0:64, :], ps_o[64:P, u % 2, :], ACT.Copy)
                else:
                    ins = act.activation(ot_other[64:P, :], ps_o[0:64, u % 2, :], ACT.Copy)
                ins.then_inc(o_other, 1)

            def out_hi(c, n, b):
                act.wait_ge(m_dve, DVE_M * b + count(READS_DVE, r_item(c, n) + 1))
                act.activation(o_part[0][:, c, n * 512:(n + 1) * 512], ot[:, n, :], ACT.Copy).then_inc(o_hi, 1)


            def item(m, b):
                slot, kind, arg = items[m]
                if kind in READS_ACT:
                    c = arg[0] if kind in "kqv" else 0
                    if kind == "x" and arg == 0:
                        act.wait_ge(xb_free, b + 1)
                    act_item(act, kind, arg, lambda: act.wait_ge(e_m, M * b + m + 1), m_act, (c + 1) % 2)
                elif kind == "r":
                    out_hi(*arg, b)

            split_weights(1)
            for q in range(PT_):
                act_item(act, "x", q, lambda: act.wait_ge(pre_pe, q + 1), pre_act, 0, banks[q])
                act.wait_ge(pre_act, q + 1)
                convert(q)
            for i, (kind, arg) in enumerate(first_items):
                act_item(act, kind, arg, lambda: act.wait_ge(pre_pe, PT_ + i + 1), pre_hi, 0, banks[i % 4])
            act.wait_ge(pre_pe, PT_ + len(first_items) + 1)
            act.activation(logit[:, :, :], ps_m[:, 0:NT * H].rearrange("p (t h) -> p t h", h=H),
                           ACT.Copy).then_inc(pre_act, 1)
            act.wait_ge(wo_in, 16)
            act.activation(wo[0][:, :, :], wo_raw, ACT.Copy).then_inc(wo_hi, 1)

            def body(b):
                act.activation(score[:, :, :], logit[:, :, :], ACT.Exp, scale=-1.0).then_inc(a_gate, 1)
                for v in range(SLOTS):
                    if v - 1 in AT:
                        item(AT[v - 1], b)
                    if v % PS == SPLIT_AT:
                        split_weights(CP * b + v // PS + 2)
                    if v == (CP - 1) * PS:
                        act.wait_ge(m_act, ACT_M * b + count(READS_ACT, AT[PS + 15] + 1))
                        for q in range(PT_):
                            convert(q)
                    prob_hi(v, b)
                    if v + 2 < SLOTS:
                        exp(v + 2, b)
                    if v % 2 and v >= 3:
                        other_half((v - 3) // 2, b)
                other_half(UNITS - 1, b)
                for m in range(AT[SLOTS], M):
                    item(m, b)
                exp(0, b + 1)
                exp(1, b + 1)

            exp(0, 0)
            exp(1, 0)
            act.wait_ge(pre_act, PT_ + 1)
            batches(act, body, own)

        @block.gpsimd
        def _(pool):
            own = Own(pool, own_p)

            def split_weights(n):
                pool.wait_ge(w_hi, n)
                pool.tensor_tensor(wq[1][:, :, :], w_raw[:, 0, :, :], wq[0][:, :, :], ALU.subtract)
                pool.tensor_tensor(wk[1][:, :, :], w_raw[:, 1, :, :], wk[0][:, :, :], ALU.subtract)
                pool.tensor_tensor(wv[1][:, :, :], w_raw[:, 2, :, :], wv[0][:, :, :], ALU.subtract).then_inc(w_lo, 1)

            def root(q, n):
                pool.wait_ge(stat, n + 1)
                newton(own, pool, rs[:, q % 2, 1, :], rs[:, q % 2, 2, :], rs[:, q % 2, 3, :])
                pool.sem_inc(rooted, 1)

            def convert(q, n):
                pool.wait_ge(c_hi, n + 1)
                cols = slice(q * PAIR, (q + 1) * PAIR)
                pool.tensor_tensor(xt_part[1][:, :, cols], xt[:, :, cols], xt_part[0][:, :, cols],
                                   ALU.subtract).then_inc(c_lo, 1)

            def q_over(par, n):
                cols = slice(n * 512, (n + 1) * 512)
                for part in qq:
                    for j, (rows, other) in enumerate(((slice(0, 64), slice(64, P)), (slice(64, P), slice(0, 64)))):
                        own.step(pool.tensor_tensor(part[other, par, j, cols], part[rows, par, j, cols],
                                                    one[rows, :].broadcast_to([64, 512]), ALU.mult))
                pool.sem_inc(q_both, 1)

            def widen(c, n, b):
                pool.wait_ge(d_wgt, CP * b + c + 1)
                if c:
                    pool.wait_ge(e_m, M * b + r_item(c - 1, n) + 1)
                pool.tensor_tensor(wwide[:, n, :, :].rearrange("p t (j w) -> p t j w", j=2),
                                   spread(wgt[:, :, 4 * n:4 * n + 4].rearrange("p j t -> p t j").unsqueeze(3), 3, dh),
                                   one[:, :].unsqueeze(2).unsqueeze(3).broadcast_to([P, 4, 2, dh]),
                                   ALU.mult).then_inc(p_wide, 1)

            def out_lo(c, n, b):
                pool.wait_ge(o_hi, R_M * b + 2 * c + n + 1)
                cols = slice(n * 512, (n + 1) * 512)
                pool.tensor_tensor(o_part[1][:, c, cols], ot[:, n, :], o_part[0][:, c, cols],
                                   ALU.subtract).then_inc(o_lo, 1)

            own.link(pool.memset(one[:, :], 1.0))
            own.step(pool.memset(lower[:, :, :], 1.0))
            pool.affine_select(out=lower[:, :, :], in_=lower[:, :, :], compare_op=ALU.is_gt, fill=0.0,
                               base=0, pattern=[[1, H], [-1, H]], channel_multiplier=0).then_inc(s_lower, 1)
            root(0, 0)
            root(1, 1)
            split_weights(1)
            for q in range(PT_):
                convert(q, q)
                if q + 2 < PT_:
                    root(q + 2, q + 2)
            pool.wait_ge(c_lo, PT_)
            for n in range(2):
                pool.wait_ge(pre_dve, first_items.index(("q", (n,))) + 1)
                q_over(0, n)
            pool.wait_ge(wo_hi, 1)
            pool.tensor_tensor(wo[1][:, :, :], wo_raw, wo[0][:, :, :], ALU.subtract).then_inc(wo_lo, 1)

            def body(b):
                for v in range(SLOTS):
                    c, s = v // PS, v % PS
                    if s == SPLIT_AT:
                        split_weights(CP * b + c + 2)
                    if v in ln_at:
                        q = ln_at[v]
                        root(q, PT_ * b + PT_ + q)
                    if c and s in (4, 5):
                        out_lo(c - 1, s - 4, b)
                    if v == (CP - 1) * PS + 4:
                        for q in range(PT_):
                            convert(q, PT_ * b + PT_ + q)
                    if s == 10 and c:
                        pool.wait_ge(o_lo, R_M * b + 2 * c)
                    if s in (10, 11):
                        pool.wait_ge(m_dve, DVE_M * b + count(READS_DVE, AT[v - 1] + 1))
                        q_over((c + 1) % 2, 0 if s == 10 else 1)
                    if s == PS - 1:
                        widen(c, 0, b)
                        widen(c, 1, b)

            batches(pool, body, own)

        @block.vector
        def _(dve):
            own = Own(dve, own_v)

            def ln_stats(q, n, times):
                dve.wait_ge(xp_in[q % 2], 16 * times)
                if not (isinstance(n, int) and n < 2):
                    dve.wait_ge(ln, n - 1)
                for t in range(2):
                    own.link(dve.bn_stats(stats[:, t, :], xp[:, q % 2, t, :]))
                own.wait()
                for t in range(2):
                    own.link(dve.bn_aggr(mv[:, q % 2, t, :], stats[:, t, :]))
                own.wait()
                rsqrt_guess(own, dve, mv[:, q % 2, :, 1], rs[:, q % 2, 0, :], rs[:, q % 2, 1, :], rs[:, q % 2, 2, :])
                dve.tensor_scalar(rs[:, q % 2, 2, :].bitcast(I32), rs[:, q % 2, 2, :].bitcast(I32), -1, RSQRT_MAGIC,
                                  ALU.mult, ALU.add).then_inc(stat, 1)

            def layer_norm(q, n, wait_xn):
                dve.wait_ge(rooted, n + 1)
                wait_xn()
                for t in range(2):
                    ins = dve.tensor_scalar(xn[:, q % 2, t, :], xp[:, q % 2, t, :], mv[:, q % 2, t, 0:1],
                                            rs[:, q % 2, 2, t:t + 1], ALU.subtract, ALU.mult)
                ins.then_inc(ln, 1)

            def row_max(v, b):
                dve.wait_ge(e_s, SLOTS * b + v + 1)
                dve.tensor_reduce(negmax[:, v % 4:v % 4 + 1], ps_s[:, v % 2, :], AX.X, ALU.max,
                                  negate=True).then_inc(d_max, 1)

            CHOOSE_STEPS = 8

            def choose(step, b):
                other = spread(score[:, :, :].unsqueeze(2), 2, H)
                mine = spread(score[:, :, :].unsqueeze(3), 3, H)
                if step == 0:
                    dve.wait_ge(a_gate, b + 1)
                else:
                    own.wait()
                if step == 0:
                    ins = dve.tensor_scalar(score[:, :, :], score[:, :, :], 1.0, None, ALU.add)
                elif step == 1:
                    ins = dve.reciprocal(score[:, :, :], score[:, :, :])
                elif step == 2:
                    ins = dve.tensor_tensor(before, other, mine, ALU.is_gt)
                elif step == 3:
                    ins = dve.tensor_tensor(equal, other, mine, ALU.is_equal)
                elif step == 4:
                    ins = dve.tensor_tensor(equal, equal, spread(lower[:, :, :].unsqueeze(1), 1, NT), ALU.mult)
                elif step == 5:
                    ins = dve.tensor_tensor(before, before, equal, ALU.add)
                elif step == 6:
                    ins = dve.tensor_reduce(rank[:, :, :], before, AX.X, ALU.add)
                else:
                    ins = dve.scalar_tensor_tensor(out=chosen[:, :, :], in0=rank[:, :, :], scalar=float(topk),
                                                   in1=score[:, :, :], op0=ALU.is_lt, op1=ALU.mult)
                if step < CHOOSE_STEPS - 1:
                    own.link(ins)
                else:
                    ins.then_inc(d_chosen, 1)

            def prob_lo(v, b):
                u = v // 2
                for g in range(2):
                    dve.wait_ge(t_hi, 2 * SLOTS * b + 2 * v + g + 1)
                    at = (slice(None), u % 2, slice(4 * g, 4 * g + 4), slice((v % 2) * TOK, (v % 2 + 1) * TOK))
                    dve.tensor_tensor(pt[1][at], ps_t[:, g, :, :], pt[0][at], ALU.subtract).then_inc(t_lo, 1)

            def out_sum(u, b):
                dve.wait_ge(o_other, UNITS * b + u + 1)
                rows = slice(0, 64) if (u // PT_) % 2 == 0 else slice(64, P)
                cols = slice((u % PT_) * PAIR, (u % PT_ + 1) * PAIR)
                dve.tensor_tensor(ot_raw[rows, cols], ps_o[rows, u % 2, :], ot_other[rows, :],
                                  ALU.add).then_inc(o_sum, 1)

            def weights_of(c, b):
                dve.wait_ge(a_exp, SLOTS * b + PS * (c + 1))
                if c:
                    dve.wait_ge(p_wide, R_M * b + 2 * c)
                else:
                    dve.wait_ge(d_chosen, b + 1)
                own.step(dve.reciprocal(wgt[:, :, :], den[:, 2 * c:2 * c + 2, :]))
                dve.tensor_tensor(wgt[:, :, :], wgt[:, :, :], chosen[:, :, 2 * c:2 * c + 2].rearrange("p t j -> p j t"),
                                  ALU.mult).then_inc(d_wgt, 1)

            def item(m, b):
                slot, kind, arg = items[m]
                if kind in "kqv":
                    dve.wait_ge(m_act, ACT_M * b + count(READS_ACT, m + 1))
                    dve_item(dve, kind, arg, m_dve, (arg[0] + 1) % 2)
                elif kind == "r":
                    c, n = arg
                    dve.wait_ge(e_m, M * b + m + 1)
                    dve.wait_ge(o_sum, UNITS * b + 2 * PT_ * (c + 1))
                    if c:
                        dve.wait_ge(o_lo, R_M * b + 2 * (c - 1) + n + 1)
                    dve.tensor_tensor(ot[:, n, :], ot_raw[:, n * 512:(n + 1) * 512], bank(kind, arg),
                                      ALU.mult).then_inc(m_dve, 1)
                elif kind == "o":
                    dve.wait_ge(e_m, M * b + m + 1)
                    if arg == 0:
                        dve.wait_ge(xb_in, 16 * b + 16)
                    rows = xb[:, 2 * arg:2 * arg + 2, :]
                    dve.scalar_tensor_tensor(out=rows, in0=bank(kind, arg).rearrange("p (t d) -> p t d", t=2),
                                             scalar=gate, in1=rows, op0=ALU.mult, op1=ALU.add).then_inc(m_dve, 1)

            for q in range(2):
                ln_stats(q, q, 1)
            for q in range(PT_):
                layer_norm(q, q, lambda: dve.wait_ge(pre_pe, q - 1) if q >= 2 else None)
                if q + 2 < PT_:
                    ln_stats(q + 2, q + 2, 2)
            for i, (kind, arg) in enumerate(first_items):
                dve.wait_ge(pre_hi, i + 1)
                dve_item(dve, kind, arg, pre_dve, 0, banks[i % 4])
            row_max(0, 0)
            row_max(1, 0)
            dve.wait_ge(s_lower, 1)
            dve.sem_inc(batch_done, 1)
            dve.sem_inc(o_read, 1)

            def body(b):
                for v in range(SLOTS):
                    if v - 1 in AT:
                        item(AT[v - 1], b)
                    if v + 2 < SLOTS:
                        row_max(v + 2, b)
                    prob_lo(v, b)
                    if 2 <= v < 2 + CHOOSE_STEPS:
                        choose(v - 2, b)
                    if v in ln_at:
                        q = ln_at[v]
                        ln_stats(q, PT_ * b + PT_ + q, (b + 1) * (PT_ // 2) + q // 2 + 1)
                    if v - 3 in ln_at:
                        q = ln_at[v - 3]
                        layer_norm(q, PT_ * b + PT_ + q,
                                   lambda: dve.wait_ge(e_m, M * b + at_x(q - 2) + 1) if q >= 2 else None)
                    if v % PS == PS - 1:
                        weights_of(v // PS, b)
                    if v % 2 and v >= 3:
                        out_sum((v - 3) // 2, b)
                out_sum(UNITS - 1, b)
                for n in range(2):
                    item(AT[SLOTS] + n, b)
                for n in range(2):
                    cols = slice(n * 512, (n + 1) * 512)
                    dve.wait_ge(o_hi, R_M * b + 2 * CP - 1 + n)
                    dve.tensor_tensor(o_part[1][:, CP - 1, cols], ot[:, n, :], o_part[0][:, CP - 1, cols],
                                      ALU.subtract).then_inc(o_lo, 1)
                row_max(0, b + 1)
                row_max(1, b + 1)
                dve.wait_ge(o_lo, R_M * b + R_M)
                dve.sem_inc(batch_done, 1)
                for m in range(AT[SLOTS] + 2, M):
                    item(m, b)
                dve.wait_ge(m_dve, DVE_M * b + DVE_M)
                dve.sem_inc(o_read, 1)

            batches(dve, body, own)


def ffn_weights(nc, fw, w, scales, s3, scale_src, s3_src, inexact, ident, tag):
    N = len(fw.src)
    RING = 4
    STAGE = 8

    def on_act(i):
        return i % 4 == 3

    def maxima(i):
        return sum(not on_act(k) for k in range(i + 1))

    with semaphores(nc, tag) as sem, ExitStack() as ctx:
        stage = ctx.enter_context(nc.sbuf_tensor(f"{tag}_stage", [P, STAGE, WCH], F32))
        rest = ctx.enter_context(nc.sbuf_tensor(f"{tag}_rest", [P, RING, WCH], F32))
        worst = ctx.enter_context(nc.sbuf_tensor(f"{tag}_worst", [P, N + 1], F32))
        ps = ctx.enter_context(nc.psum_tensor(f"{tag}_ps", [P, 512], F32))
        loaded = [sem(f"loaded{i}") for i in range(STAGE)]
        diffed = [sem("diffed_dve"), sem("diffed_pool")]
        small, rounded, max_of, sum_of, worst_all, transposed = (sem(n) for n in (
            "small", "rounded", "max_of", "sum_of", "worst_all", "transposed"))
        block = ctx.enter_context(nc.Block())

        def subtract(eng, i):
            eng.wait_ge(rounded, i + 1)
            if i >= RING and on_act(i):
                eng.wait_ge(sum_of, i // 4)
            elif i >= RING:
                eng.wait_ge(max_of, maxima(i - RING))
            eng.tensor_tensor(rest[:, i % RING, :], stage[:, i % STAGE, :], w[:, i * WCH:(i + 1) * WCH],
                              ALU.subtract).then_inc(diffed[i % 2], 1)

        @block.sync
        def _(sp):
            for i, src in enumerate(fw.src):
                if i >= STAGE:
                    sp.wait_ge(diffed[i % 2], (i - STAGE) // 2 + 1)
                sp.dma_start(stage[:, i % STAGE, :].rearrange("p (k n) -> p k n", n=src.shape[2]),
                             src).then_inc(loaded[i % STAGE], 16)
            for i, v in enumerate(scale_src):
                sp.dma_start(scales[:, i, :], v).then_inc(small, 16)
            sp.dma_start(s3[:, :], spread(s3_src.rearrange("(a n) -> a n", a=1), 0, P)).then_inc(small, 16)
            sp.wait_ge(small, 16 * (len(scale_src) + 1))

        @block.scalar
        def _(act):
            def row_sum(i):
                act.wait_ge(diffed[1], i // 2 + 1)
                act.activation(rest[:, i % RING, :], rest[:, i % RING, :], ACT.Abs,
                               accum_out=worst[:, i:i + 1]).then_inc(sum_of, 1)

            for i in range(N):
                act.wait_ge(loaded[i % STAGE], 16 * (i // STAGE + 1))
                act.activation(w[:, i * WCH:(i + 1) * WCH], stage[:, i % STAGE, :], ACT.Copy).then_inc(rounded, 1)
                if i >= 2 and on_act(i - 2):
                    row_sum(i - 2)
            for i in range(N - 2, N):
                if on_act(i):
                    row_sum(i)

        @block.gpsimd
        def _(pool):
            for i in range(1, N, 2):
                subtract(pool, i)

        @block.vector
        def _(dve):
            def row_max(i):
                if not on_act(i):
                    dve.wait_ge(diffed[i % 2], i // 2 + 1)
                    dve.tensor_reduce(worst[:, i:i + 1], rest[:, i % RING, :], AX.X, ALU.max,
                                      apply_absolute_value=True).then_inc(max_of, 1)

            for i in range(N):
                if i % 2 == 0:
                    subtract(dve, i)
                if i:
                    row_max(i - 1)
            row_max(N - 1)
            dve.wait_ge(max_of, maxima(N - 1))
            dve.wait_ge(sum_of, N // 4)
            dve.tensor_reduce(worst[:, N:N + 1], worst[:, 0:N], AX.X, ALU.max).then_inc(worst_all, 1)
            dve.wait_ge(transposed, 1)
            dve.tensor_reduce(inexact[0:1, 0:1], ps[0:1, 0:P], AX.X, ALU.max).then_inc(worst_all, 1)
            dve.wait_ge(worst_all, 2)

        @block.tensor
        def _(pe):
            pe.wait_ge(worst_all, 1)
            pe.transpose(ps[0:1, 0:P], worst[:, N:N + 1], ident[:, :]).then_inc(transposed, 1)


def load_full(nc, fw, w):
    with semaphores(nc, "G") as sem, nc.Block() as block:
        loaded = sem("full_loaded")

        @block.sync
        def _(sp):
            for i, src in enumerate(fw.src):
                sp.dma_start(w[:, i * WCH:(i + 1) * WCH].rearrange("p (k n) -> p k n", n=src.shape[2]),
                             src).then_inc(loaded, 16)
            sp.wait_ge(loaded, 16 * len(fw.src))


def ffn_either_way(nc, ident, gate, x_src, x_dst, t):
    fw = FfnWeights(*(t[f"L0_ffn_{n}T"] for n in ("w1_w", "w2_w", "h1_w", "h2_w", "w3_w")))
    scale_src = [t[f"L0_ffn_{n}_s"] for n in ("w1", "w2", "h1", "h2")]
    with ExitStack() as ctx:
        scales = ctx.enter_context(nc.sbuf_tensor("ffn_scales", [P, 4, fw.K["h1"]], F32))
        s3 = ctx.enter_context(nc.sbuf_tensor("ffn_s3", [P, D], F32))
        inexact = ctx.enter_context(nc.sbuf_tensor("ffn_inexact", [1, 1], F32))
        with nc.sbuf_tensor("ffn_w_rounded", [P, fw.cols], F32R) as w:
            ffn_weights(nc, fw, w, scales, s3, scale_src, t["L0_ffn_w3_s"], inexact, ident, "W")
            flag = nc.values_load(inexact[0:1, 0:1].bitcast(I32))
            with nc.If_eq(flag.val, 0):
                feed_forward(nc, ident, gate, x_src, x_dst, fw, w, scales, s3, True, "F")
        with nc.Else():
            with nc.sbuf_tensor("ffn_w_full", [P, fw.cols], F32) as w:
                load_full(nc, fw, w)
                feed_forward(nc, ident, gate, x_src, x_dst, fw, w, scales, s3, False, "G")


def constants(nc, ident, gates, g_xattn, g_ffn):
    with semaphores(nc, "S") as sem, nc.Block() as block:
        gates_in, tanh_done, ident_zero, ident_made = (sem(n) for n in (
            "gates_in", "tanh_done", "ident_zero", "ident_made"))

        @block.sync
        def _(sp):
            for i, g in enumerate((g_xattn, g_ffn)):
                sp.dma_start(gates[:, i, :], spread(g.rearrange("(a n) -> a n", a=1), 0, P)).then_inc(gates_in, 16)

        @block.scalar
        def _(act):
            act.wait_ge(gates_in, 32)
            act.activation(gates[:, :, :], gates[:, :, :], ACT.Tanh).then_inc(tanh_done, 1)
            act.wait_ge(tanh_done, 1)

        @block.gpsimd
        def _(pool):
            pool.memset(ident[:, :], 0.0).then_inc(ident_zero, 1)
            pool.wait_ge(ident_zero, 1)
            pool.affine_select(out=ident[:, :], in_=ident[:, :], compare_op=ALU.not_equal, fill=1.0,
                               base=0, pattern=[[-1, P]], channel_multiplier=1).then_inc(ident_made, 1)
            pool.wait_ge(ident_made, 1)


def gated_layers(nc, t, only=None):
    T = t["x"].shape[0]
    x1, x2, x3 = (nc.dram_tensor(f"x{i}", [T, D], F32, kind="Internal").ap() for i in range(1, 4))
    with ExitStack() as ctx:
        ident = ctx.enter_context(nc.sbuf_tensor("ident", [P, P], F32))
        gates = ctx.enter_context(nc.sbuf_tensor("gates", [P, 2, 2], F32))
        constants(nc, ident, gates, t["g_xattn"], t["g_ffn"])
        layers = [
            lambda src, dst: cross_attention(
                nc, ident, gates[:, 0, 0:1], src, dst, t["ctxT"],
                *(t[f"L0_xattn_{n}T"] for n in ("wq", "wk", "wv", "wo")),
                tuple(t[f"L0_xattn_{n}"] for n in ("bq", "bk", "bv", "bo")), None, 16, "A"),
            lambda src, dst: ffn_either_way(nc, ident, gates[:, 1, 0:1], src, dst, t),
            lambda src, dst: cross_attention(
                nc, ident, gates[:, 0, 1:2], src, dst, t["ctxT"],
                *(t[f"L1_xattn_{n}"] for n in ("Wq", "Wk", "Wv", "Wo")),
                None, (t["L1_xattn_ln_scale"], t["L1_xattn_ln_bias"]), 8, "C"),
            lambda src, dst: self_attention(
                nc, ident, gates[:, 1, 1:2], src, dst, *(t[f"L1_ffn_{n}"] for n in ("Wq", "Wk", "Wv", "Ws")),
                t["L1_ffn_Wo"].rearrange("h e d -> (h e) d"), t["L1_ffn_bo"], t["ctxT"].shape[0],
                t["L1_ffn_Ws"].shape[1], 3),
        ]
        if only is not None:
            layers[only](t["x"], t["out"])
            return
        for layer, src, dst in zip(layers, (t["x"], x1, x2, x3), (x1, x2, x3, t["out"])):
            layer(src, dst)


def laid_out(inputs):
    import numpy as np

    def cols(v):
        return v.reshape(-1, P).T

    a = {}
    for name, v in inputs.items():
        v = np.asarray(v)
        if name == "x":
            a[name] = v.reshape(-1, v.shape[-1])
        elif name == "ctx_1024":
            a["ctxT"] = v.transpose(0, 2, 1)
        elif name.startswith("L0_xattn_w") or (name.startswith("L0_ffn_") and name.endswith("_w")):
            a[name + "T"] = v.T
        elif name.endswith("Wkv"):
            half = v.shape[1] // 2
            a[name[:-3] + "Wk"], a[name[:-3] + "Wv"] = v[:, :half], v[:, half:]
        elif name in ("L0_xattn_bq", "L0_xattn_bk", "L1_xattn_ln_scale", "L1_xattn_ln_bias", "L0_ffn_w1_s",
                      "L0_ffn_w2_s", "L0_ffn_h1_s", "L0_ffn_h2_s"):
            a[name] = cols(v)
        else:
            a[name] = v
    return {name: np.ascontiguousarray(v) for name, v in a.items()}


def kernel(**inputs):
    import concourse.bacc as bacc
    from concourse.bass_utils import run_bass_kernel_spmd

    arrays = laid_out(inputs)
    nc = bacc.Bacc("TRN2", target_bir_lowering=False, num_devices=1)
    tensors = {n: nc.dram_tensor(f"in_{n}", list(v.shape), mybir.dt.from_np(v.dtype), kind="ExternalInput").ap()
               for n, v in arrays.items()}
    tensors["out"] = nc.dram_tensor("out_x", list(arrays["x"].shape), F32, kind="ExternalOutput").ap()
    gated_layers(nc, tensors)
    r = run_bass_kernel_spmd(nc, [{f"in_{n}": v for n, v in arrays.items()}], core_ids=[0])
    return r.results[0]["out_x"].reshape(inputs["x"].shape)
```
